# Optimizing a Trainium2 kernel written in Bass

```python
import numpy as np
import jax
import jax.numpy as jnp

def _softmax(x, axis=-1):
    return jax.nn.softmax(x, axis=axis)

def _gelu(x):
    return jax.nn.gelu(x, approximate=True)

def _silu(x):
    return jax.nn.silu(x)

def _sigmoid(x):
    return jax.nn.sigmoid(x)

def _layernorm(x, axis=-1, eps=1e-05):
    m = jnp.mean(x, axis=axis, keepdims=True)
    v = jnp.var(x, axis=axis, keepdims=True)
    return (x - m) / jnp.sqrt(v + eps)

def _scatter_add(tgt, idx, src, axis=0):
    return tgt.at[idx].add(src)

def _segment_sum(src, seg, n):
    return jax.ops.segment_sum(src, seg, n)
kernel_name = 'mk_prb_d2_jaxref_r8_92b0a2'

def setup_inputs(seed: int=0):
    np.random.seed(seed)
    _w = jnp.asarray

    def _L0_attn_setup():
        import jax, jax.numpy as jnp
        import numpy as np
        EPS_RMS = 1e-06
        EPS_LN = 1e-05
        ETA_MIN = 1e-06
        B, T, D, F = (8, 64, 128, 64)

        def _rmsnorm(x, w):
            return x * jax.lax.rsqrt(jnp.mean(x * x, axis=-1, keepdims=True) + EPS_RMS) * w

        def _phi(x):
            return jax.nn.elu(x) + 1.0

        def _ln2(M):
            mu = jnp.mean(M, axis=(-2, -1), keepdims=True)
            var = jnp.mean((M - mu) ** 2, axis=(-2, -1), keepdims=True)
            return (M - mu) * jax.lax.rsqrt(var + EPS_LN)

        def _reference_tuple_inner(x, norm_weight, Wk, Wv, Wq, eta, Wout):
            b, t, d = x.shape
            f = Wk.shape[0]
            x_norm = _rmsnorm(x, norm_weight)
            k = _phi(jnp.einsum('btd,fd->btf', x_norm, Wk))
            v = jnp.einsum('btd,ed->bte', x_norm, Wv)
            eta_c = jnp.maximum(jnp.abs(eta), ETA_MIN)

            def step(M, kv):
                k_t, v_t = kv
                v_pred = jnp.einsum('bf,bfd->bd', k_t, M)
                surprise = jnp.linalg.norm(v_t - v_pred, axis=-1, keepdims=True)
                delta = k_t[:, :, None] * v_t[:, None, :]
                M = M + eta_c[None, :, None] * surprise[:, :, None] * delta
                return (_ln2(M), None)
            M0 = jnp.zeros((b, f, d), dtype=x.dtype)
            kT = jnp.transpose(k, (1, 0, 2))
            vT = jnp.transpose(v, (1, 0, 2))
            M, _ = jax.lax.scan(step, M0, (kT, vT))
            q = _phi(jnp.einsum('btd,fd->btf', x_norm, Wq))
            mem_out = jnp.einsum('btf,bfd->btd', q, M)
            out = jnp.einsum('btd,ed->bte', mem_out, Wout)
            output = x + out
            return (output, M)
        key = jax.random.key(seed)
        ks = jax.random.split(key, 5)
        x = jax.random.normal(ks[0], (B, T, D), dtype=jnp.float32)
        norm_weight = jnp.ones((D,), dtype=jnp.float32)
        Wk = jax.random.normal(ks[1], (F, D), dtype=jnp.float32) * 0.02
        Wv = jax.random.normal(ks[2], (D, D), dtype=jnp.float32) * 0.02
        Wq = jax.random.normal(ks[3], (F, D), dtype=jnp.float32) * 0.02
        Wout = jax.random.normal(ks[4], (D, D), dtype=jnp.float32) * 0.02
        eta = jnp.ones((F,), dtype=jnp.float32) * 0.01
        return {'x': x, 'norm_weight': norm_weight, 'Wk': Wk, 'Wv': Wv, 'Wq': Wq, 'eta': eta, 'Wout': Wout}
    _L0_attn_in = _L0_attn_setup()

    def _L0_ffn_setup():
        import jax, jax.numpy as jnp
        import numpy as np
        B, S, D, O, H, E, K = (4, 128, 128, 128, 256, 16, 4)
        key = jax.random.key(seed)
        ks = jax.random.split(key, 8)
        x = jax.random.normal(ks[0], (B, S, D), dtype=jnp.float32)
        w_gate = jax.random.normal(ks[1], (D, E), dtype=jnp.float32) * 0.01
        w_noise = jnp.zeros((D, E), dtype=jnp.float32)
        W1 = jax.random.normal(ks[2], (E, D, H), dtype=jnp.float32) * (1.0 / np.sqrt(D))
        b1 = jnp.zeros((E, H), dtype=jnp.float32)
        W2 = jax.random.normal(ks[3], (E, H, O), dtype=jnp.float32) * (1.0 / np.sqrt(H))
        b2 = jnp.zeros((E, O), dtype=jnp.float32)
        return {'x': x, 'w_gate': w_gate, 'w_noise': w_noise, 'W1': W1, 'b1': b1, 'W2': W2, 'b2': b2}
    _L0_ffn_in = _L0_ffn_setup()

    def _L1_attn_setup():
        import jax, jax.numpy as jnp
        import numpy as np
        B, T, DM = (2, 256, 128)
        DH = 128
        NH = DM // DH
        ROTARY_BASE = 10000.0

        def fractional_rope(x, base):
            dh = x.shape[-1]
            rot, skip = jnp.split(x, 2, axis=-1)
            width = rot.shape[-1]
            half = width // 2
            t = rot.shape[-2]
            positions = jnp.arange(t)[:, None]
            dims = jnp.arange(half)
            ang_freqs = jnp.power(base, -dims / half)[None, :]
            radians = positions * ang_freqs
            cos = jnp.cos(radians).astype(x.dtype)
            sin = jnp.sin(radians).astype(x.dtype)
            even, odd = jnp.split(rot, 2, axis=-1)
            r_even = even * cos - odd * sin
            r_odd = even * sin + odd * cos
            return jnp.concatenate([r_even, r_odd, skip], axis=-1)
        key = jax.random.key(seed)
        ks = jax.random.split(key, 5)
        scale = (1.0 / DM) ** 0.5
        x = jax.random.normal(ks[0], (B, T, DM), dtype=jnp.float32)
        wq = jax.random.normal(ks[1], (NH, DM, DH), dtype=jnp.float32) * scale
        wk = jax.random.normal(ks[2], (NH, DM, DH), dtype=jnp.float32) * scale
        wv = jax.random.normal(ks[3], (NH, DM, DH), dtype=jnp.float32) * scale
        wo = jax.random.normal(ks[4], (NH * DH, DM), dtype=jnp.float32) * (1.0 / (NH * DH)) ** 0.5
        return {'x': x, 'wq': wq, 'wk': wk, 'wv': wv, 'wo': wo}
    _L1_attn_in = _L1_attn_setup()

    def _L1_ffn_setup():
        import jax, jax.numpy as jnp
        import numpy as np
        D_IN, D_HID = (128, 512)

        def _ternary(key, shape):
            return jax.random.randint(key, shape, -1, 2).astype(jnp.float32)

        def _tlin(x, w, s):
            return jnp.einsum('bsi,oi->bso', x, w) * s
        key = jax.random.key(seed)
        ks = jax.random.split(key, 12)
        inv = lambda fan: 1.0 / np.sqrt(fan).astype(np.float32)
        return {'x': jax.random.normal(ks[0], (4, 256, D_IN), dtype=jnp.float32), 'w1_w': _ternary(ks[1], (D_HID, D_IN)), 'w1_s': jax.random.uniform(ks[2], (D_HID,), dtype=jnp.float32) * inv(D_IN), 'w2_w': _ternary(ks[3], (D_HID, D_IN)), 'w2_s': jax.random.uniform(ks[4], (D_HID,), dtype=jnp.float32) * inv(D_IN), 'h1_w': _ternary(ks[5], (D_HID, D_HID)), 'h1_s': jax.random.uniform(ks[6], (D_HID,), dtype=jnp.float32) * inv(D_HID), 'h2_w': _ternary(ks[7], (D_HID, D_HID)), 'h2_s': jax.random.uniform(ks[8], (D_HID,), dtype=jnp.float32) * inv(D_HID), 'w3_w': _ternary(ks[9], (D_IN, D_HID)), 'w3_s': jax.random.uniform(ks[10], (D_IN,), dtype=jnp.float32) * inv(D_HID)}
    _L1_ffn_in = _L1_ffn_setup()
    _d = {'L0_attn_x': _L0_attn_in['x'], 'L0_attn_norm_weight': _L0_attn_in['norm_weight'], 'L0_attn_Wk': _L0_attn_in['Wk'], 'L0_attn_Wv': _L0_attn_in['Wv'], 'L0_attn_Wq': _L0_attn_in['Wq'], 'L0_attn_eta': _L0_attn_in['eta'], 'L0_attn_Wout': _L0_attn_in['Wout'], 'L0_ffn_w_gate': _L0_ffn_in['w_gate'], 'L0_ffn_w_noise': _L0_ffn_in['w_noise'], 'L0_ffn_W1': _L0_ffn_in['W1'], 'L0_ffn_b1': _L0_ffn_in['b1'], 'L0_ffn_W2': _L0_ffn_in['W2'], 'L0_ffn_b2': _L0_ffn_in['b2'], 'L1_attn_wq': _L1_attn_in['wq'], 'L1_attn_wk': _L1_attn_in['wk'], 'L1_attn_wv': _L1_attn_in['wv'], 'L1_attn_wo': _L1_attn_in['wo'], 'L1_ffn_w1_w': _L1_ffn_in['w1_w'], 'L1_ffn_w1_s': _L1_ffn_in['w1_s'], 'L1_ffn_w2_w': _L1_ffn_in['w2_w'], 'L1_ffn_w2_s': _L1_ffn_in['w2_s'], 'L1_ffn_h1_w': _L1_ffn_in['h1_w'], 'L1_ffn_h1_s': _L1_ffn_in['h1_s'], 'L1_ffn_h2_w': _L1_ffn_in['h2_w'], 'L1_ffn_h2_s': _L1_ffn_in['h2_s'], 'L1_ffn_w3_w': _L1_ffn_in['w3_w'], 'L1_ffn_w3_s': _L1_ffn_in['w3_s']}
    _x0 = _d['L0_attn_x']
    _d['L0_attn_x'] = jax.random.normal(jax.random.fold_in(jax.random.key(seed), 1), (1, 2048, 128), dtype=_x0.dtype)
    del _x0
    return _d

def reference(L0_attn_x, L0_attn_norm_weight, L0_attn_Wk, L0_attn_Wv, L0_attn_Wq, L0_attn_eta, L0_attn_Wout, L0_ffn_w_gate, L0_ffn_w_noise, L0_ffn_W1, L0_ffn_b1, L0_ffn_W2, L0_ffn_b2, L1_attn_wq, L1_attn_wk, L1_attn_wv, L1_attn_wo, L1_ffn_w1_w, L1_ffn_w1_s, L1_ffn_w2_w, L1_ffn_w2_s, L1_ffn_h1_w, L1_ffn_h1_s, L1_ffn_h2_w, L1_ffn_h2_s, L1_ffn_w3_w, L1_ffn_w3_s):

    def _L0_attn_ref(x, norm_weight, Wk, Wv, Wq, eta, Wout):
        import jax, jax.numpy as jnp
        import numpy as np
        EPS_RMS = 1e-06
        EPS_LN = 1e-05
        ETA_MIN = 1e-06
        B, T, D, F = (8, 64, 128, 64)

        def _rmsnorm(x, w):
            return x * jax.lax.rsqrt(jnp.mean(x * x, axis=-1, keepdims=True) + EPS_RMS) * w

        def _phi(x):
            return jax.nn.elu(x) + 1.0

        def _ln2(M):
            mu = jnp.mean(M, axis=(-2, -1), keepdims=True)
            var = jnp.mean((M - mu) ** 2, axis=(-2, -1), keepdims=True)
            return (M - mu) * jax.lax.rsqrt(var + EPS_LN)

        def _reference_tuple_inner(x, norm_weight, Wk, Wv, Wq, eta, Wout):
            b, t, d = x.shape
            f = Wk.shape[0]
            x_norm = _rmsnorm(x, norm_weight)
            k = _phi(jnp.einsum('btd,fd->btf', x_norm, Wk))
            v = jnp.einsum('btd,ed->bte', x_norm, Wv)
            eta_c = jnp.maximum(jnp.abs(eta), ETA_MIN)

            def step(M, kv):
                k_t, v_t = kv
                v_pred = jnp.einsum('bf,bfd->bd', k_t, M)
                surprise = jnp.linalg.norm(v_t - v_pred, axis=-1, keepdims=True)
                delta = k_t[:, :, None] * v_t[:, None, :]
                M = M + eta_c[None, :, None] * surprise[:, :, None] * delta
                return (_ln2(M), None)
            M0 = jnp.zeros((b, f, d), dtype=x.dtype)
            kT = jnp.transpose(k, (1, 0, 2))
            vT = jnp.transpose(v, (1, 0, 2))
            M, _ = jax.lax.scan(step, M0, (kT, vT))
            q = _phi(jnp.einsum('btd,fd->btf', x_norm, Wq))
            mem_out = jnp.einsum('btf,bfd->btd', q, M)
            out = jnp.einsum('btd,ed->bte', mem_out, Wout)
            output = x + out
            return (output, M)
        return _reference_tuple_inner(x, norm_weight, Wk, Wv, Wq, eta, Wout)[0]

    def _L0_ffn_ref(x, w_gate, w_noise, W1, b1, W2, b2):
        import jax, jax.numpy as jnp
        import numpy as np
        B, S, D, O, H, E, K = (4, 128, 128, 128, 256, 16, 4)
        logits = jnp.zeros((x.shape[0], x.shape[1], E), dtype=x.dtype).at[..., 1].set(100.0)
        top_vals, top_idx = jax.lax.top_k(logits, K)
        gates_k = jax.nn.softmax(top_vals, axis=-1)
        gates = jnp.einsum('bske,bsk->bse', jax.nn.one_hot(top_idx, E, dtype=x.dtype), gates_k)
        h = jax.nn.relu(jnp.einsum('bsd,edh->ebsh', x, W1) + b1[:, None, None, :])
        y = jnp.einsum('ebsh,eho->ebso', h, W2) + b2[:, None, None, :]
        out = jnp.einsum('ebso,bse->bso', y, gates)
        return out

    def _L1_attn_ref(x, wq, wk, wv, wo):
        import jax, jax.numpy as jnp
        import numpy as np
        B, T, DM = (2, 256, 128)
        DH = 128
        NH = DM // DH
        ROTARY_BASE = 10000.0

        def fractional_rope(x, base):
            dh = x.shape[-1]
            rot, skip = jnp.split(x, 2, axis=-1)
            width = rot.shape[-1]
            half = width // 2
            t = rot.shape[-2]
            positions = jnp.arange(t)[:, None]
            dims = jnp.arange(half)
            ang_freqs = jnp.power(base, -dims / half)[None, :]
            radians = positions * ang_freqs
            cos = jnp.cos(radians).astype(x.dtype)
            sin = jnp.sin(radians).astype(x.dtype)
            even, odd = jnp.split(rot, 2, axis=-1)
            r_even = even * cos - odd * sin
            r_odd = even * sin + odd * cos
            return jnp.concatenate([r_even, r_odd, skip], axis=-1)
        b, t, dm = x.shape
        q = jnp.einsum('btd,hdk->bhtk', x, wq)
        k = jnp.einsum('btd,hdk->bhtk', x, wk)
        v = jnp.einsum('btd,hdk->bhtk', x, wv)
        q = fractional_rope(q, ROTARY_BASE)
        k = fractional_rope(k, ROTARY_BASE)
        inv_sqrt_dh = DH ** (-0.5)
        q = q * inv_sqrt_dh
        k = k * inv_sqrt_dh
        s = jnp.einsum('bhik,bhjk->bhij', q, k)
        i = jnp.arange(t)[:, None]
        j = jnp.arange(t)[None, :]
        mask = jnp.less(i, j).astype(s.dtype)
        s = s - 1e+30 * mask
        p = jax.nn.softmax(s, axis=-1)
        o = jnp.einsum('bhij,bhjv->bihv', p, v)
        o = jnp.reshape(o, (b, t, NH * DH))
        return jnp.einsum('bto,od->btd', o, wo)

    def _L1_ffn_ref(x, w1_w, w1_s, w2_w, w2_s, h1_w, h1_s, h2_w, h2_s, w3_w, w3_s):
        import jax, jax.numpy as jnp
        import numpy as np
        D_IN, D_HID = (128, 512)

        def _ternary(key, shape):
            return jax.random.randint(key, shape, -1, 2).astype(jnp.float32)

        def _tlin(x, w, s):
            return jnp.einsum('bsi,oi->bso', x, w) * s
        h = jax.nn.silu(_tlin(x, w1_w, w1_s)) * _tlin(x, w2_w, w2_s)
        h = jax.nn.gelu(_tlin(h, h1_w, h1_s), approximate=False)
        h = jax.nn.gelu(_tlin(h, h2_w, h2_s), approximate=False)
        return _tlin(h, w3_w, w3_s)
    x = L0_attn_x
    xn = _layernorm(x, axis=-1)
    x = x + _L0_attn_ref(xn, L0_attn_norm_weight, L0_attn_Wk, L0_attn_Wv, L0_attn_Wq, L0_attn_eta, L0_attn_Wout) + _L0_ffn_ref(xn, L0_ffn_w_gate, L0_ffn_w_noise, L0_ffn_W1, L0_ffn_b1, L0_ffn_W2, L0_ffn_b2)
    xn = _layernorm(x, axis=-1)
    x = x + _L1_attn_ref(xn, L1_attn_wq, L1_attn_wk, L1_attn_wv, L1_attn_wo) + _L1_ffn_ref(xn, L1_ffn_w1_w, L1_ffn_w1_s, L1_ffn_w2_w, L1_ffn_w2_s, L1_ffn_h1_w, L1_ffn_h1_s, L1_ffn_h2_w, L1_ffn_h2_s, L1_ffn_w3_w, L1_ffn_w3_s)
    return x

_drawn_inputs = setup_inputs


def setup_inputs(seed=0):
    import zlib

    import numpy as np

    out = dict(_drawn_inputs(seed))
    spreads = {'L0_attn_norm_weight': (1.0, 0.2),
     'L0_attn_eta': (0.009999999776482582, 0.2),
     'L0_ffn_w_noise': (0.0, 0.1),
     'L0_ffn_b1': (0.0, 0.1),
     'L0_ffn_b2': (0.0, 0.1)}
    factors = {}
    for name, (base, spread) in spreads.items():
        noise = np.random.default_rng([zlib.crc32(name.encode()), seed]).standard_normal(out[name].shape)
        drawn = base * np.exp(spread * noise) if base else spread * noise
        out[name] = jnp.asarray(drawn.astype(out[name].dtype))
    for name, factor in factors.items():
        out[name] = (out[name] * factor).astype(out[name].dtype)
    return out
```

```python
from contextlib import ExitStack

import numpy as np
import concourse.bass as bass
from concourse import mybir

ALU = mybir.AluOpType
ACT = mybir.ActivationFunctionType
AX = mybir.AxisListType
F32 = mybir.dt.float32
I32 = mybir.dt.int32

P = 128
T, D = 2048, 128
NT = T // P
F = 64
HALF = 16
S = T // HALF
L = 2 * HALF
W = S - 1
SH = S // 2 + 1
N = float(F * D)
BANK = 512
EPS_LN, EPS_RMS, ETA_MIN = 1e-5, 1e-6, 1e-6
EXPERT = 1
EH = 256
HID = 512
TOLERANCE = 2.0 ** -8
HT4 = HID // P
ROT = 64
ZC = 256

C_ID, C_CAUSAL, C_ONES, C_END = 0, 128, 256, 384

RW = L + 2
R_N, R_0, R_CD, R_D, R_G, R_T, R_Q, R_B, R_R, R_E, R_X = range(L, L + 11)
R_Z = R_R + (R_R - R_D)
R_END = R_Z + 1
SCAN = R_X - R_N + 1


def shape_constants():
    c = np.zeros((P, C_END), np.float32)
    i = np.arange(P)
    c[:, C_ID:C_ID + P] = np.eye(P)
    c[:, C_CAUSAL:C_CAUSAL + P] = np.where(i[None, :] > i[:, None], -1e30, 0.0)
    c[:, C_ONES:C_ONES + P] = 1.0
    return c


class Order:

    def __init__(self, engine, semaphore):
        self.engine, self.semaphore, self.n, self.offset = engine, semaphore, 0, 0

    def did(self, instruction):
        instruction.then_inc(self.semaphore, 1)
        self.n += 1
        return self.n

    def need(self, n):
        self.engine.wait_ge(self.semaphore, n + self.offset)


def program(nc, a, out):
    with ExitStack() as ctx:
        def sb(name, shape, dt=F32):
            return ctx.enter_context(nc.sbuf_tensor(name, shape, dt))

        def sem(name):
            return ctx.enter_context(nc.semaphore(name))

        x = sb("x", [P, NT, D])
        xn = sb("xn", [P, NT, D])
        xT = sb("xT", [P, T])
        con = sb("con", [P, C_END])
        ident = con[:, C_ID:C_ID + P]
        ones = con[:, C_ONES:C_ONES + P]
        wkT = sb("wkT", [P, F])
        wvT = sb("wvT", [P, D])
        wqT = sb("wqT", [P, F])
        woutT = sb("woutT", [P, D])
        normw = sb("normw", [P, 1])
        etac = sb("etac", [P, 1])
        w1e = sb("w1e", [P, EH])
        w2e = sb("w2e", [P, 2, D])
        b1e = sb("b1e", [P, 2])
        b2e = sb("b2e", [P, D])
        st = sb("st", [P, NT, 6])
        mv = sb("mv", [P, NT, 2])
        lnt = sb("lnt", [P, 6, NT])

        arena = sb("arena", [P, 45000])
        at = [0]

        def take(n):
            at[0] += n
            return arena[:, at[0] - n:at[0]]

        wq, wk, wvT2, wo, WVO, s3 = (take(P) for _ in range(6))
        w1T, w2T, w3T = (take(HID) for _ in range(3))
        w3T = w3T.rearrange("p (m e) -> p m e", m=HT4)
        s1, s2, sh1, sh2, s1h, s12 = (take(HT4) for _ in range(6))
        a_tab = at[0]
        HT = take(2 * T).rearrange("p (h t) -> p h t", h=2)
        cosT, sinT = arena[ROT:P, a_tab:a_tab + T], arena[ROT:P, a_tab + T:a_tab + 2 * T]
        a_blocks = at[0]

        KU = take(SH * 2 * L).rearrange("p (c t i) -> p c t i", c=SH, t=2)
        UX = take(SH * (HALF + 1)).rearrange("p (c j) -> p c j", c=SH)
        VT = take(T + HALF)
        VX = take(S * (HALF + 1)).rearrange("p (s j) -> p s j", s=S)
        xrT = take(T)
        a_tk = at[0]
        TK = [take(SH * HALF) for _ in range(2)]
        QE, MOE = arena[0:F, a_tk:a_tk + T], xrT
        XR = arena[:, at[0]:at[0] + T].rearrange("p (n d) -> p n d", n=NT)
        Gf = take((HALF + 1) * S)
        G = Gf.rearrange("p (j s) -> p j s", j=HALF + 1)
        CC = take(6 * (L + 1) * L)[0:W].rearrange("p (q j t) -> p q j t", q=6, j=L + 1)
        GG = take(L * L)[0:W].rearrange("p (j t) -> p j t", j=L)
        VC = take(L * L)[0:W].rearrange("p (j l) -> p j l", j=L)
        tmpA, tmpB = (Gf[0:W, L * L * i:L * L * (i + 1)].rearrange("p (j t) -> p j t", j=L) for i in range(2))
        STf = take(R_END * RW)[0:W]
        ST = STf.rearrange("p (r t) -> p r t", t=RW)
        lane = take(12 * L)[0:W].rearrange("p (r t) -> p r t", t=L)
        VB, MM, KD, FD, M2, MR, MZ, DVS, VJJ, SB, T0, T1 = range(12)
        SG = take(L * SCAN)[0:W].rearrange("p (j k) -> p j k", k=SCAN)
        WS = take(L * SCAN)[0:W].rearrange("p (j k) -> p j k", k=SCAN)
        HG = take((L + 1) * 3)[0:W].rearrange("p (j k) -> p j k", k=3)
        S3 = take(L * 3)[0:W].rearrange("p (j k) -> p j k", k=3)
        SQ = take(L)[0:W]
        U, P2 = take(L)[0:W], take(2 * L)[0:W].rearrange("p (r t) -> p r t", r=2)
        sc = take(16)
        EC, rh, bound, agree = sc[0:W, 0:2], sc[0:W, 2:4], sc[0:W, 4:5], sc[0:W, 5:6]
        wcol, negm = sc[0:L, 6:7], sc[0:L, 7:8]
        wts, c0, c1 = take(L)[0:W], take(HALF)[0:W], take(L)[0:W]
        U32, UW, WM = (take(F)[0:L] for _ in range(3))
        VW, WSUM = (take(D)[0:L] for _ in range(2))
        MW = take(D)[0:F]
        qT = xT[0:F, :]
        a_oj = at[0]
        OJf = take(sum(n * n for n in range(L - 1)))
        OJ, o_ = [], 0
        for j in range(L - 2):
            n_ = L - 2 - j
            OJ.append(OJf[0:W, o_:o_ + n_ * n_].rearrange("p (l t) -> p l t", l=n_))
            o_ += n_ * n_
        KF = OJf[0:F, 0:T]
        MS, MQ, DIAG = OJf[0:F, 2 * T:2 * T + D], OJf[0:F, 2 * T + D:2 * T + 2 * D], OJf[:, 2 * T + 2 * D:2 * T + 3 * D]
        MT = OJf[:, 2 * T + 3 * D:2 * T + 3 * D + F]
        g_ = OJf[:, 2 * T + 4 * D:2 * T + 4 * D + 16]
        vt, dv_, d2, sp_ = (g_[:, i:i + 1] for i in range(4))
        kt, su, rs, r2, mean, var, sd, rinv_ = (g_[0:F, i:i + 1] for i in range(4, 12))

        b_at = [a_blocks]

        def second(n):
            b_at[0] += n
            return arena[:, b_at[0] - n:b_at[0]]

        h1T, h2T = (second(HT4 * HID).rearrange("p (k o) -> p k o", k=HT4) for i in range(2))
        qT1, kT1 = second(T), second(T)
        V1 = second(T).rearrange("p (n e) -> p n e", n=NT)
        hA, hB = (second(HT4 * T).rearrange("p (m t) -> p m t", m=HT4) for _ in range(2))
        Pr = [second(T) for _ in range(2)]
        PT = [second(T), xn[:, :, :].rearrange("p n d -> p (n d)")]
        assert b_at[0] <= at[0] <= 45000, (b_at, at)
        TH = [hB[:, 3, 0:ZC], hB[:, 3, ZC:2 * ZC]]
        ZU = [hB[:, 3, 2 * ZC:3 * ZC], hB[:, 3, 3 * ZC:4 * ZC]]
        mxs, nbs, rsum, rinv = (lnt[:, i, :] for i in range(2, 6))

        PS = ctx.enter_context(nc.psum_tensor("PS", [P, 8, BANK], F32))
        flag = sb("flag", [1, 1], I32)

        x_in = [sem(f"x_in{c}") for c in range(4)]
        early_in, moe_in, late_in = sem("early_in"), sem("moe_in"), sem("late_in")
        dve_order, dve_order2, act_order, pool_order, loop_order = (
            sem(n) for n in ("dve_order", "dve_order2", "act_order", "pool_order", "loop_order"))
        var_ready, sd_ready, ms_ready, rms_ready = sem("var_ready"), sem("sd_ready"), sem("ms_ready"), sem("rms_ready")
        xr_ready, xn_ready, set_once = sem("xr_ready"), sem("xn_ready"), sem("set_once")
        xrt_done, xrt_act, xrt_dve = sem("xrt_done"), sem("xrt_act"), sem("xrt_dve")
        k_done, v_done, kphi_act, vt_ready, vx_ready = sem("k_done"), sem("v_done"), sem("kphi_act"), sem("vt_ready"), sem("vx_ready")
        k_ready, ku_ready, ku_act = sem("k_ready"), sem("ku_ready"), sem("ku_act")
        gram_done, gram_act, lanes_done, lanes_act = sem("gram_done"), sem("gram_act"), sem("lanes_done"), sem("lanes_act")
        xnt_done, xnt_act, eh_done, eh_act, eo_done, eo_act = (sem(n) for n in ("xnt_done", "xnt_act", "eh_done", "eh_act", "eo_done", "eo_act"))
        q_done, qphi_act, q_ready, xres_ready = sem("q_done"), sem("qphi_act"), sem("q_ready"), sem("xres_ready")
        last_done, last_act, mrow_ready, neg_done, neg_act = (sem(n) for n in ("last_done", "last_act", "mrow_ready", "neg_done", "neg_act"))
        vc_ready, oj_ready, b_ready, sb_ready = sem("vc_ready"), sem("oj_ready"), sem("b_ready"), sem("sb_ready")
        ssq_ready, sigma_ready, w_ready, h_ready = sem("ssq_ready"), sem("sigma_ready"), sem("w_ready"), sem("h_ready")
        wts_ready, wcol_done, uw_ready, mw_done, mw_act = (sem(n) for n in ("wts_ready", "wcol_done", "uw_ready", "mw_done", "mw_act"))
        c0_ready, shift_done, agree_ready, count_done, flag_set = (sem(n) for n in ("c0_ready", "shift_done", "agree_ready", "count_done", "flag_set"))
        ao_done, x1_ready = sem("ao_done"), sem("x1_ready")
        token_ready, state_ready, pred_done, d2_ready, ss_done, s_ready = (
            sem(n) for n in ("token_ready", "state_ready", "pred_done", "d2_ready", "ss_done", "s_ready"))
        rows_ready, sum_done, sq_rows_ready, sq_done, var_s_ready, sd_s_ready = (
            sem(n) for n in ("rows_ready", "sum_done", "sq_rows_ready", "sq_done", "var_s_ready", "sd_s_ready"))
        gmt_done, gmt_act, gmw_done, gmw_act = (sem(n) for n in ("gmt_done", "gmt_act", "gmw_done", "gmw_act"))
        tab_in, small_in, h_in = sem("tab_in"), sem("small_in"), sem("h_in")
        var2_ready, sd2_ready, xn2_ready, xt2_done, xt2_act = (sem(n) for n in ("var2_ready", "sd2_ready", "xn2_ready", "xt2_done", "xt2_act"))
        wvo_done, wvo_act, qk_done, qk_act, qk_dve, rope_add = (sem(n) for n in ("wvo_done", "wvo_act", "qk_done", "qk_act", "qk_dve", "rope_add"))
        v1_done, v1_act = sem("v1_done"), sem("v1_act")
        s_done, bias_ready, p_ready, pt_done, pt_act, pt_dve, pv_done, pv_read = (
            sem(n) for n in ("s_done", "bias_ready", "p_ready", "pt_done", "pt_act", "pt_dve", "pv_done", "pv_read"))
        z_done, tanh_ready, hA_ready = sem("z_done"), sem("tanh_ready"), sem("hA_ready")
        g1_done, g1_act, g2_done, g2_act, y_done, out_ready = (
            sem(n) for n in ("g1_done", "g1_act", "g2_done", "g2_act", "y_done", "out_ready"))
        scales_ready = sem("scales_ready")
        out_sem = sem("out_sem")

        def bank(b, rows=P, cols=BANK):
            return PS[0:rows, b, 0:cols]

        def groups_of(t):
            before = sum((u + 4) // 4 for u in range(t))
            return [(before + k, c, min(4, t + 1 - c)) for k, c in enumerate(range(0, t + 1, 4))]

        PACK = 22
        GRAM_RUNS = [(b, s0, min(PACK, hi - s0)) for b, s0, hi in zip(
            (7, 0, 1, 2, 3, 4), [*range(0, S // 2, PACK), *range(S // 2, S, PACK)], [S // 2] * 3 + [S] * 3)]
        LANE_RUNS = [(0, 5, 0), (5, 5, 0), (10, 5, 0), (15, 2, 0), (17, 5, 1), (22, 5, 1), (27, 5, 1), (32, 1, 1)]

        block = ctx.enter_context(nc.Block())

        x_dram = a["L0_attn_x"].rearrange("b (n p) d -> p (b n) d", p=P)
        out_dram = out.rearrange("b (n p) d -> p (b n) d", p=P)

        @block.sync
        def _(sp):
            for c in range(4):
                sp.dma_start(x[:, 4 * c:4 * c + 4, :], x_dram[:, 4 * c:4 * c + 4, :]).then_inc(x_in[c], 16)
            sp.dma_start(w1e[:], a["L0_ffn_W1"][EXPERT]).then_inc(moe_in, 16)
            sp.dma_start(w2e[:], a["L0_ffn_W2"][EXPERT].rearrange("(k p) o -> p k o", p=P)).then_inc(moe_in, 16)
            sp.dma_start(b1e[:], a["b1_by_partition"][EXPERT]).then_inc(moe_in, 16)
            sp.dma_start(b2e[:], a["L0_ffn_b2"][EXPERT:EXPERT + 1, :].broadcast_to([P, D])).then_inc(moe_in, 16)
            sp.dma_start(wqT[:], a["WqT"]).then_inc(late_in, 16)
            sp.dma_start(woutT[:], a["WoutT"]).then_inc(late_in, 16)
            for dst, n in ((wq, "wq_turned"), (wk, "wk_turned"), (wvT2, "wv_T"), (wo, "L1_attn_wo"), (w1T, "w1_T"), (w2T, "w2_T"),
                           (w3T, "w3_T"), (s1, "s1"), (s2, "s2"), (sh1, "sh1"), (sh2, "sh2")):
                sp.dma_start(dst, a[n]).then_inc(small_in, 16)
            sp.dma_start(s3, a["L1_ffn_w3_s"].rearrange("(o d) -> o d", o=1).broadcast_to([P, D])).then_inc(small_in, 16)
            sp.wait_ge(eo_done, 4)
            for i, n in enumerate(("cos", "sin")):
                sp.dma_start((cosT, sinT)[i], a[n]).then_inc(tab_in, 16)
            sp.wait_ge(x1_ready, 1)
            for dst, n in ((h1T, "h1_T"), (h2T, "h2_T")):
                sp.dma_start(dst, a[n]).then_inc(h_in, 16)
            for c in range(4):
                sp.wait_ge(out_ready, c + 1)
                sp.dma_start(out_dram[:, 4 * c:4 * c + 4, :], x[:, 4 * c:4 * c + 4, :]).then_inc(out_sem, 16)
            sp.wait_ge(out_sem, 64)

        def general_path(engine, run):
            engine.wait_ge(flag_set, 1)
            agreed = engine.value_load(flag[0:1, 0:1], min_val=0, max_val=1)
            with engine.If(agreed == 0):
                run()

        @block.tensor
        def _(pe):
            mm, tr = nc.tensor.matmul, nc.tensor.transpose

            pe.wait_ge(early_in, 16 * 6)
            for n in range(NT):
                pe.wait_ge(xr_ready, n + 1)
                i = tr(PS[:, n // 4, (n % 4) * P:(n % 4 + 1) * P], XR[:, n, :], ident)
                if n % 4 == 3:
                    i.then_inc(xrt_done, 1)
            pe.wait_ge(xrt_act, 2)
            pe.wait_ge(xrt_dve, 2)
            for hf in range(2):
                t0 = hf * (T - SH * HALF)
                for b, c in enumerate(range(0, SH * HALF, BANK)):
                    n = min(BANK, SH * HALF - c)
                    i = mm(PS[64 * hf:64 * hf + F, 4 + b, 0:n], wkT[:, :], xrT[:, t0 + c:t0 + c + n], start=True, stop=True)
            i.then_inc(k_done, 1)
            for ch in range(4):
                mm(bank(ch), wvT[:, :], xrT[:, ch * BANK:(ch + 1) * BANK], start=True, stop=True).then_inc(v_done, 1)
            pe.wait_ge(set_once, 6)
            pe.wait_ge(vt_ready, 4)
            pe.wait_ge(vx_ready, 4)
            for b, s0, cnt in GRAM_RUNS:
                if b == 4:
                    pe.wait_ge(kphi_act, 2)
                for s in range(s0, s0 + cnt):
                    mm(PS[2 * L:3 * L, b, (s - s0) * (HALF + 1):(s - s0 + 1) * (HALF + 1)], VT[:, HALF * s:HALF * s + L], VX[:, s, :], start=True, stop=True)
            pe.wait_ge(ku_ready, 3)
            pe.wait_ge(ku_act, 2)
            for b, s0, cnt in GRAM_RUNS:
                h0 = 0 if s0 < S // 2 else F
                for s in range(s0, s0 + cnt):
                    c = s - (S - SH) * (h0 // F)
                    i = mm(PS[0:2 * L, b, (s - s0) * (HALF + 1):(s - s0 + 1) * (HALF + 1)],
                           KU[h0:h0 + F, c, :, :].rearrange("p t i -> p (t i)"), UX[h0:h0 + F, c, :], start=True, stop=True)
                i.then_inc(gram_done, 1)
            pe.wait_ge(gram_act, 6)
            for b, (r0, cnt, behind) in enumerate(LANE_RUNS):
                for r in range(r0, r0 + cnt):
                    j = (HALF if r == 0 else r - 1) if not behind else r - 1 - HALF
                    i = tr(PS[0:W, b, (r - r0) * 3 * L:(r - r0 + 1) * 3 * L], G[0:3 * L, j, behind:behind + W], ident[0:3 * L, 0:3 * L])
                i.then_inc(lanes_done, 1)
            pe.wait_ge(xn_ready, NT)
            for n in range(NT):
                if n % 4 == 0:
                    pe.wait_ge(lanes_act, n // 4 + 1)
                i = tr(PS[:, n // 4, (n % 4) * P:(n % 4 + 1) * P], xn[:, n, :], ident)
                if n % 4 == 3:
                    i.then_inc(xnt_done, 1)
            pe.wait_ge(lanes_act, 8)
            pe.wait_ge(late_in, 32)
            tr(PS[0:L, 7, 0:F], KU[F:P, SH - 2, 1, :], con[F:P, C_ID + F:C_ID + P])
            mm(PS[0:L, 7, F:F + D], VT[:, T - L:T], woutT[:, :], start=True, stop=True)
            mm(PS[0:L, 7, F + D:F + 2 * D], ones[:, 0:L], woutT[:, :], start=True, stop=True).then_inc(last_done, 1)
            pe.wait_ge(moe_in, 64)
            pe.wait_ge(xnt_act, 4)
            pe.wait_ge(last_act, 3)
            for h in range(2):
                for ch in range(4):
                    mm(bank((4, 0)[h] + ch), w1e[:, h * P:(h + 1) * P], xT[:, ch * BANK:(ch + 1) * BANK], start=True, stop=True).then_inc(eh_done, 1)
            pe.wait_ge(eh_act, 4)
            for ch in range(4):
                i = mm(PS[0:F, 4 + ch, :], wqT[:, :], xrT[:, ch * BANK:(ch + 1) * BANK], start=True, stop=True)
            i.then_inc(q_done, 1)
            pe.wait_ge(eh_act, 8)
            for n in range(NT):
                for h in range(2):
                    i = mm(PS[:, n // 4, (n % 4) * P:(n % 4 + 1) * P], HT[:, h, n * P:(n + 1) * P], w2e[:, h, :], start=(h == 0), stop=(h == 1))
                if n % 4 == 3:
                    i.then_inc(eo_done, 1)
            pe.wait_ge(qphi_act, 2)
            pe.wait_ge(mrow_ready, 1)
            mm(PS[0:L, 4, 0:1], lane[:, MM, :], con[0:W, C_ID + W - 1:C_ID + W], start=True, stop=True).then_inc(neg_done, 1)
            pe.wait_ge(wts_ready, 1)
            mm(PS[0:L, 5, 0:1], wts, con[0:W, C_ID + W - 1:C_ID + W], start=True, stop=True).then_inc(wcol_done, 1)
            pe.wait_ge(c0_ready, 1)
            mm(PS[0:W - 1, 6, 0:HALF], con[0:W, C_ID + 1:C_ID + W], c0, start=True, stop=True).then_inc(shift_done, 1)
            pe.wait_ge(uw_ready, 2)
            mm(PS[0:F, 7, 0:D], UW, VW, start=True, stop=False)
            mm(PS[0:F, 7, 0:D], WM, WSUM, start=False, stop=True).then_inc(mw_done, 1)
            pe.wait_ge(agree_ready, 1)
            mm(PS[0:1, 4, 1:2], agree[0:W - 1, :], con[0:W - 1, C_ONES:C_ONES + 1], start=True, stop=True).then_inc(count_done, 1)

            def general():
                with pe.Fori(0, T) as t:
                    pe.wait_ge(state_ready, t + 1)
                    pe.wait_ge(token_ready, t + 1)
                    mm(PS[:, 0, 0:1], MS, kt, start=True, stop=True)
                    mm(PS[:, 1, 0:D], ones, DIAG, start=True, stop=True).then_inc(pred_done, 1)
                    pe.wait_ge(d2_ready, t + 1)
                    mm(PS[:, 2, 0:1], ones, d2, start=True, stop=True).then_inc(ss_done, 1)
                    pe.wait_ge(rows_ready, t + 1)
                    mm(PS[:, 3, 0:1], ones[0:F, :], rs, start=True, stop=True).then_inc(sum_done, 1)
                    pe.wait_ge(sq_rows_ready, t + 1)
                    mm(PS[:, 3, 1:2], ones[0:F, :], r2, start=True, stop=True).then_inc(sq_done, 1)
                pe.wait_ge(state_ready, T + 1)
                tr(PS[:, 0, 0:F], MS, con[0:F, C_ID:C_ID + F]).then_inc(gmt_done, 1)
                pe.wait_ge(gmt_act, 1)
                mm(PS[0:F, 7, 0:D], MT, woutT[:, :], start=True, stop=True).then_inc(gmw_done, 1)
                pe.wait_ge(gmw_act, 1)

            pe.wait_ge(mw_act, 1)
            general_path(pe, general)
            pe.wait_ge(q_ready, 1)
            pe.wait_ge(eo_act, 4)
            for n in range(NT):
                i = mm(PS[:, 4 + n // 4, (n % 4) * P:(n % 4 + 1) * P], qT[:, n * P:(n + 1) * P], MW, start=True, stop=True)
                if n % 4 == 3:
                    i.then_inc(ao_done, 1)

            pe.wait_ge(small_in, 16 * 12)
            mm(PS[:, 3, 0:D], wvT2, wo, start=True, stop=True).then_inc(wvo_done, 1)
            pe.wait_ge(x1_ready, 4)
            for n in range(NT):
                pe.wait_ge(xn2_ready, n + 1)
                if n == 12:
                    pe.wait_ge(wvo_act, 1)
                i = tr(PS[:, n // 4, (n % 4) * P:(n % 4 + 1) * P], xn[:, n, :], ident)
                if n % 4 == 3:
                    i.then_inc(xt2_done, 1)
            for ch in range(4):
                pe.wait_ge(xt2_act, ch + 1)
                mm(bank(4 + ch), wq, xT[:, ch * BANK:(ch + 1) * BANK], start=True, stop=True).then_inc(qk_done, 1)
            for ch in range(4):
                mm(bank(ch), wk, xT[:, ch * BANK:(ch + 1) * BANK], start=True, stop=True).then_inc(qk_done, 1)
            for n in range(NT):
                if n % 4 == 0:
                    pe.wait_ge(qk_act, n // 4 + 1)
                    pe.wait_ge(qk_dve, n // 4 + 1)
                i = mm(PS[:, 4 + n // 4, (n % 4) * P:(n % 4 + 1) * P], xT[:, n * P:(n + 1) * P], WVO, start=True, stop=True)
                if n % 4 == 3:
                    i.then_inc(v1_done, 1)
            pe.wait_ge(qk_act, 8)
            pe.wait_ge(qk_dve, 8)
            pe.wait_ge(rope_add, 8)
            pe.wait_ge(v1_act, 4)

            def gated(u):
                m, c = u % HT4, u // HT4
                if u:
                    pe.wait_ge(hA_ready, u)
                for k, w in enumerate((w1T, w2T)):
                    i = mm(PS[:, 6, k * ZC:(k + 1) * ZC], w[:, m * P:(m + 1) * P], xT[:, c * ZC:(c + 1) * ZC], start=True, stop=True)
                i.then_inc(z_done, 1)

            def scores(t):
                if t:
                    pe.wait_ge(p_ready, t)
                for c in range(0, t + 1, 4):
                    w = min(4, t + 1 - c) * P
                    last = c + 4 > t
                    i = mm(PS[:, c // 4, 0:w], qT1[:, t * P:(t + 1) * P], kT1[:, c * P:c * P + w], start=True, stop=not last)
                    if last:
                        i = mm(PS[:, c // 4, w - P:w], ident, con[:, C_CAUSAL:C_CAUSAL + P], start=False, stop=True)
                i.then_inc(s_done, 1)

            def weighted(t):
                pe.wait_ge(p_ready, t + 1)
                groups = groups_of(t)

                def product(g):
                    gi, c, cnt = g
                    if gi % 2 == 0:
                        pe.wait_ge(pt_act, gi // 2 + 1)
                    else:
                        pe.wait_ge(pt_dve, gi // 2 + 1)
                    if c == 0 and t:
                        pe.wait_ge(pv_read, t)
                    for b in range(c, c + cnt):
                        i = mm(PS[:, 7, (t % 4) * D:(t % 4 + 1) * D], PT[t % 2][:, b * P:(b + 1) * P], V1[:, b, :], start=(b == 0), stop=(b == t))
                    return i

                for k, (gi, c, cnt) in enumerate(groups):
                    if gi >= 2:
                        (pe.wait_ge(pt_act, gi // 2) if gi % 2 == 0 else pe.wait_ge(pt_dve, gi // 2))
                    for b in range(c, c + cnt):
                        i = tr(PS[:, 4 + gi % 2, (b - c) * P:(b - c + 1) * P], Pr[t % 2][:, b * P:(b + 1) * P], ident)
                    i.then_inc(pt_done, 1)
                    if k:
                        product(groups[k - 1])
                product(groups[-1]).then_inc(pv_done, 1)

            for t in range(NT + 1):
                if t < NT:
                    scores(t)
                    gated(2 * t)
                if t:
                    weighted(t - 1)
                if t < NT:
                    gated(2 * t + 1)
            pe.wait_ge(h_in, 32)
            pe.wait_ge(hA_ready, 32)
            pe.wait_ge(pv_read, NT)
            for layer, (w, src, done, read) in enumerate(((h1T, hA, g1_done, g1_act), (h2T, hB, g2_done, g2_act))):
                for ch in range(4):
                    if layer:
                        pe.wait_ge(g1_act, 4 * ch + 4)
                    for m in range(HT4):
                        u = 4 * ch + m
                        if u >= 8:
                            pe.wait_ge(read, u - 7)
                        elif layer:
                            pe.wait_ge(g1_act, 8 + u + 1)
                        for k in range(HT4):
                            i = mm(bank(u % 8), w[:, k, m * P:(m + 1) * P], src[:, k, ch * BANK:(ch + 1) * BANK], start=(k == 0), stop=(k == HT4 - 1))
                        i.then_inc(done, 1)
            for n in range(NT):
                if n % 4 == 0:
                    pe.wait_ge(g2_act, n + 4)
                    if n == 0:
                        pe.wait_ge(g2_act, 12)
                for k in range(HT4):
                    i = mm(PS[:, n // 4, (n % 4) * P:(n % 4 + 1) * P], hA[:, k, n * P:(n + 1) * P], w3T[:, k, :], start=(k == 0), stop=(k == HT4 - 1))
                if n % 4 == 3:
                    i.then_inc(y_done, 1)

        @block.scalar
        def _(act):
            f = nc.scalar.activation
            o = Order(act, act_order)
            act.dma_start(con[:], a["shape_constants"]).then_inc(early_in, 16)
            act.dma_start(wkT[:], a["WkT"]).then_inc(early_in, 16)
            act.dma_start(wvT[:], a["WvT"]).then_inc(early_in, 16)
            act.dma_start(normw[:], a["L0_attn_norm_weight"].rearrange("(d o) -> d o", o=1)).then_inc(early_in, 16)
            act.dma_start(etac[0:F, :], a["L0_attn_eta"].rearrange("(d o) -> d o", o=1)).then_inc(early_in, 16)
            act.dma_start(etac[F:P, :], a["L0_attn_eta"].rearrange("(d o) -> d o", o=1)).then_inc(early_in, 16)
            act.wait_ge(var_ready, 1)
            f(lnt[:, 1, :], lnt[:, 0, :], ACT.Sqrt).then_inc(sd_ready, 1)
            act.wait_ge(ms_ready, 1)
            f(lnt[:, 4, :], lnt[:, 3, :], ACT.Sqrt).then_inc(rms_ready, 1)
            act.wait_ge(early_in, 16 * 6)
            for b in range(2):
                act.wait_ge(xrt_done, b + 1)
                f(xrT[:, b * BANK:(b + 1) * BANK], bank(b), ACT.Copy, scale=normw[:, 0:1]).then_inc(xrt_act, 1)

            def phi(positive, exponent, z, done):
                f(positive, z, ACT.Relu).then_inc(done, 1)
                n = o.did(f(exponent, z, ACT.Relu, scale=-1.0))
                o.need(n)
                f(exponent, exponent, ACT.Exp, scale=-1.0).then_inc(done, 1)

            act.wait_ge(k_done, 1)
            phi(TK[0], TK[1], PS[:, 4:7, :].rearrange("p b c -> p (b c)")[:, 0:SH * HALF], kphi_act)
            act.wait_ge(set_once, 6)
            for ch in range(4):
                act.wait_ge(vt_ready, ch + 1)
                f(VX[:, 32 * ch:32 * ch + 32, 0:HALF], VT[:, ch * BANK:(ch + 1) * BANK].rearrange("p (s i) -> p s i", i=HALF), ACT.Copy).then_inc(vx_ready, 1)
            tk = TK[0].rearrange("p (c i) -> p c i", i=HALF)
            act.wait_ge(k_ready, 1)
            f(KU[:, :, 1, 0:HALF], tk, ACT.Copy, scale=etac[:, 0:1]).then_inc(ku_act, 1)
            f(KU[:, 0:SH - 1, 1, HALF:L], tk[:, 1:, :], ACT.Copy, scale=etac[:, 0:1]).then_inc(ku_act, 1)
            act.wait_ge(xrt_done, 4)
            for k, (b, s0, cnt) in enumerate(GRAM_RUNS):
                act.wait_ge(gram_done, k + 1)
                f(G[0:3 * L, :, s0:s0 + cnt].rearrange("p j s -> p s j"), PS[0:3 * L, b, 0:cnt * (HALF + 1)].rearrange("p (s j) -> p s j", s=cnt),
                  ACT.Copy).then_inc(gram_act, 1)
            for b, (r0, cnt, behind) in enumerate(LANE_RUNS):
                act.wait_ge(lanes_done, b + 1)
                src = PS[0:W, b, 0:cnt * 3 * L].rearrange("p (j q t) -> p q j t", q=3, t=L)
                if behind:
                    i = f(CC[:, 0:3, r0:r0 + cnt, HALF:L], src[:, :, :, 0:HALF], ACT.Copy)
                else:
                    i = f(CC[:, 0:3, r0:r0 + cnt, :], src, ACT.Copy)
                i.then_inc(lanes_act, 1)
            for ch in range(4):
                act.wait_ge(xnt_done, ch + 1)
                f(xT[:, ch * BANK:(ch + 1) * BANK], bank(ch), ACT.Copy).then_inc(xnt_act, 1)
            act.wait_ge(last_done, 1)
            f(U32, PS[0:L, 7, 0:F], ACT.Copy).then_inc(last_act, 1)
            f(VW, PS[0:L, 7, F:F + D], ACT.Copy).then_inc(last_act, 1)
            f(WSUM, PS[0:L, 7, F + D:F + 2 * D], ACT.Copy).then_inc(last_act, 1)
            act.wait_ge(moe_in, 64)
            for h in range(2):
                for ch in range(4):
                    act.wait_ge(eh_done, 4 * h + ch + 1)
                    f(HT[:, h, ch * BANK:(ch + 1) * BANK], bank((4, 0)[h] + ch), ACT.Relu, bias=b1e[:, h:h + 1]).then_inc(eh_act, 1)
            act.wait_ge(q_done, 1)
            act.wait_ge(ku_ready, 3)
            phi(qT, QE, PS[0:F, 4:8, :].rearrange("p b c -> p (b c)"), qphi_act)
            for ch in range(4):
                act.wait_ge(eo_done, ch + 1)
                f(MOE[:, ch * BANK:(ch + 1) * BANK], bank(ch), ACT.Copy).then_inc(eo_act, 1)
            act.wait_ge(neg_done, 1)
            f(negm, PS[0:L, 4, 0:1], ACT.Copy, scale=-1.0).then_inc(neg_act, 1)
            act.wait_ge(b_ready, 1)
            f(lane[:, SB, :], lane[:, T0, :], ACT.Sqrt).then_inc(sb_ready, 1)
            act.wait_ge(set_once, 6)
            for j in range(L):
                act.wait_ge(ssq_ready, j + 1)
                f(SG[:, j, 2:11].rearrange("p (g k) -> p g k", k=3)[:, :, 0:2], SQ[:, j:j + 1].unsqueeze(2).broadcast_to([W, 3, 2]),
                  ACT.Sqrt).then_inc(sigma_ready, 1)
                act.wait_ge(w_ready, j + 1)
                f(HG[:, j + 1, 1:3], WS[:, j, SCAN - 1:SCAN].broadcast_to([W, 2]), ACT.Sqrt).then_inc(h_ready, 1)
            act.wait_ge(mw_done, 1)
            f(MW, PS[0:F, 7, 0:D], ACT.Copy).then_inc(mw_act, 1)

            def general():
                with act.Fori(0, T) as t:
                    act.wait_ge(ss_done, t + 1)
                    f(sp_, PS[:, 2, 0:1], ACT.Sqrt).then_inc(s_ready, 1)
                    act.wait_ge(var_s_ready, t + 1)
                    f(sd, var, ACT.Sqrt).then_inc(sd_s_ready, 1)
                act.wait_ge(gmt_done, 1)
                f(MT, PS[:, 0, 0:F], ACT.Copy).then_inc(gmt_act, 1)
                act.wait_ge(gmw_done, 1)
                f(MW, PS[0:F, 7, 0:D], ACT.Copy).then_inc(gmw_act, 1)

            general_path(act, general)

            act.wait_ge(wvo_done, 1)
            f(WVO, PS[:, 3, 0:D], ACT.Copy).then_inc(wvo_act, 1)
            act.wait_ge(var2_ready, 1)
            f(lnt[:, 1, :], lnt[:, 0, :], ACT.Sqrt).then_inc(sd2_ready, 1)
            for ch in range(4):
                act.wait_ge(xt2_done, ch + 1)
                f(xT[:, ch * BANK:(ch + 1) * BANK], bank(ch), ACT.Copy).then_inc(xt2_act, 1)
            for u in range(8):
                dst, ch, b = (qT1, u, 4 + u) if u < 4 else (kT1, u - 4, u - 4)
                act.wait_ge(qk_done, u + 1)
                f(dst[0:ROT, ch * BANK:(ch + 1) * BANK], PS[0:ROT, b, :], ACT.Copy).then_inc(qk_act, 1)
            for ch in range(4):
                act.wait_ge(v1_done, ch + 1)
                f(V1[:, 4 * ch:4 * ch + 4, :].rearrange("p n d -> p (n d)"), bank(4 + ch), ACT.Copy).then_inc(v1_act, 1)

            def tanh(u):
                act.wait_ge(z_done, u + 1)
                if u == 0:
                    act.wait_ge(scales_ready, 2)
                if u >= 2:
                    act.wait_ge(hA_ready, u - 1)
                f(TH[u % 2], PS[:, 6, 0:ZC], ACT.Tanh, scale=s1h[:, u % HT4:u % HT4 + 1]).then_inc(tanh_ready, 1)

            for t in range(NT + 1):
                if t < NT:
                    if t >= 2:
                        act.wait_ge(pv_done, t - 1)
                    act.wait_ge(bias_ready, t + 1)
                    f(Pr[t % 2][:, 0:(t + 1) * P], PS[:, 0:4, :].rearrange("p b c -> p (b c)")[:, 0:(t + 1) * P], ACT.Exp,
                      scale=1.0 / D, bias=nbs[:, t:t + 1], accum_out=rsum[:, t:t + 1]).then_inc(p_ready, 1)
                    tanh(2 * t)
                if t:
                    for gi, c, cnt in groups_of(t - 1):
                        if gi % 2 == 0:
                            act.wait_ge(pt_done, gi + 1)
                            f(PT[(t - 1) % 2][:, c * P:(c + cnt) * P], PS[:, 4, 0:cnt * P], ACT.Copy).then_inc(pt_act, 1)
                if t < NT:
                    tanh(2 * t + 1)
            for dst, s_, done, read in ((hB, sh1, g1_done, g1_act), (hA, sh2, g2_done, g2_act)):
                for ch in range(4):
                    for m in range(HT4):
                        u = 4 * ch + m
                        act.wait_ge(done, u + 1)
                        f(dst[:, m, ch * BANK:(ch + 1) * BANK], bank(u % 8), ACT.Gelu, scale=s_[:, m:m + 1]).then_inc(read, 1)

        @block.gpsimd
        def _(pool):
            tt = nc.gpsimd.tensor_tensor
            o = Order(pool, pool_order)
            nc.gpsimd.memset(VX[:, :, HALF:HALF + 1], 1.0).then_inc(set_once, 1)
            nc.gpsimd.memset(VT[:, T:T + HALF], 0.0).then_inc(set_once, 1)
            nc.gpsimd.memset(UX[:, :, HALF:HALF + 1], 1.0).then_inc(set_once, 1)
            nc.gpsimd.memset(KU[:, SH - 1, :, HALF:L], 0.0).then_inc(set_once, 1)
            nc.gpsimd.memset(SG, 0.0).then_inc(set_once, 1)
            nc.gpsimd.memset(HG, 0.0).then_inc(set_once, 1)
            nc.gpsimd.memset(CC[:, 0:3, HALF + 1:L + 1, 0:HALF], 0.0).then_inc(set_once, 1)
            nc.gpsimd.memset(CC[:, 3:6, :, :], 0.0).then_inc(set_once, 1)
            nc.gpsimd.memset(STf, 0.0).then_inc(set_once, 1)
            nc.gpsimd.memset(EC[:, 0:1], 1.0 + EPS_LN).then_inc(set_once, 1)
            nc.gpsimd.memset(EC[:, 1:2], -EPS_LN).then_inc(set_once, 1)
            pool.wait_ge(set_once, 11)
            nc.gpsimd.memset(SG[:, :, SCAN - 1:SCAN], 1.0).then_inc(set_once, 1)
            nc.gpsimd.memset(ST[:, R_E, 0:1], EPS_LN).then_inc(set_once, 1)
            nc.gpsimd.memset(ST[:, R_X, 1:2], -EPS_LN).then_inc(set_once, 1)
            pool.wait_ge(lanes_act, 8)
            pool.wait_ge(vc_ready, 1)
            for j in range(L - 2):
                n = L - 2 - j
                tt(OJ[j], CC[:, 0, j + 1, j + 2:L].unsqueeze(1).broadcast_to([W, n, n]), VC[:, j, j + 1:L - 1].unsqueeze(2).broadcast_to([W, n, n]),
                   ALU.mult).then_inc(oj_ready, 1)
            pool.wait_ge(qphi_act, 2)
            tt(qT, qT, QE, ALU.add).then_inc(q_ready, 1)
            xf, xnf = x[:, :, :].rearrange("p n d -> p (n d)"), xn[:, :, :].rearrange("p n d -> p (n d)")
            pool.wait_ge(xn_ready, NT)
            n = o.did(tt(xf, xf, xnf, ALU.add))
            pool.wait_ge(eo_act, 4)
            o.need(n)
            n = o.did(tt(xf, xf, MOE, ALU.add))
            o.need(n)
            tt(x[:, :, :], x[:, :, :], b2e[:, :].unsqueeze(1).broadcast_to([P, NT, D]), ALU.add).then_inc(xres_ready, 1)

            for u in range(8):
                dst, ch = (qT1, u) if u < 4 else (kT1, u - 4)
                cols = slice(ch * BANK, (ch + 1) * BANK)
                pool.wait_ge(qk_dve, u + 1)
                tt(dst[ROT:P, cols], dst[ROT:P, cols], hB[ROT:P, 0, cols], ALU.add).then_inc(rope_add, 1)

        @block.vector
        def _(dve):
            v = nc.vector
            o = Order(dve, dve_order)
            did, need = o.did, o.need
            R = [lane[:, i, :] for i in range(12)]

            def last():
                need(o.n)

            def outer(a_, b_):
                return a_.unsqueeze(2).broadcast_to([W, L, L]), b_.unsqueeze(1).broadcast_to([W, L, L])

            for n in range(NT):
                if n % 4 == 0:
                    dve.wait_ge(x_in[n // 4], 16)
                did(v.bn_stats(st[:, n, :], x[:, n, :]))
            last()
            for n in range(NT):
                did(v.bn_aggr(mv[:, n, :], st[:, n, :]))
            last()
            v.tensor_scalar(lnt[:, 0, :], mv[:, :, 1], EPS_LN, None, ALU.add).then_inc(var_ready, 1)
            dve.wait_ge(sd_ready, 1)
            did(v.reciprocal(lnt[:, 1, :], lnt[:, 1, :]))
            last()
            did(v.tensor_tensor(lnt[:, 2, :], lnt[:, 1, :], lnt[:, 1, :], ALU.mult))
            last()
            did(v.tensor_tensor(lnt[:, 2, :], lnt[:, 2, :], mv[:, :, 1], ALU.mult))
            last()
            v.tensor_scalar(lnt[:, 3, :], lnt[:, 2, :], EPS_RMS, None, ALU.add).then_inc(ms_ready, 1)
            for n in range(NT):
                v.tensor_scalar(xn[:, n, :], x[:, n, :], mv[:, n, 0:1], lnt[:, 1, n:n + 1], ALU.subtract, ALU.mult).then_inc(xn_ready, 1)
            dve.wait_ge(rms_ready, 1)
            did(v.reciprocal(lnt[:, 4, :], lnt[:, 4, :]))
            last()
            dve.wait_ge(xn_ready, NT)
            for n in range(NT):
                v.tensor_scalar(XR[:, n, :], xn[:, n, :], lnt[:, 4, n:n + 1], None, ALU.mult).then_inc(xr_ready, 1)
            dve.wait_ge(early_in, 16 * 6)
            did(v.scalar_tensor_tensor(out=etac[:, :], in0=etac[:, :], scalar=-1.0, in1=etac[:, :], op0=ALU.mult, op1=ALU.max))
            last()
            did(v.tensor_scalar(etac[:, :], etac[:, :], ETA_MIN, None, ALU.max))
            last()
            for b in range(2, 4):
                dve.wait_ge(xrt_done, b + 1)
                v.tensor_scalar(xrT[:, b * BANK:(b + 1) * BANK], bank(b), normw[:, 0:1], None, ALU.mult).then_inc(xrt_dve, 1)
            dve.wait_ge(set_once, 6)
            for ch in range(4):
                dve.wait_ge(v_done, ch + 1)
                v.tensor_copy(VT[:, ch * BANK:(ch + 1) * BANK], bank(ch)).then_inc(vt_ready, 1)
            dve.wait_ge(kphi_act, 2)
            v.tensor_tensor(TK[0], TK[0], TK[1], ALU.add).then_inc(k_ready, 1)
            dve.wait_ge(k_ready, 1)
            tk = TK[0].rearrange("p (c i) -> p c i", i=HALF)
            v.tensor_copy(KU[:, :, 0, 0:HALF], tk).then_inc(ku_ready, 1)
            v.tensor_copy(KU[:, 0:SH - 1, 0, HALF:L], tk[:, 1:, :]).then_inc(ku_ready, 1)
            v.tensor_scalar(UX[:, :, 0:HALF], tk, etac[:, 0:1], None, ALU.mult).then_inc(ku_ready, 1)

            aT, bT, V = (CC[:, q, 1:L + 1, :] for q in range(3))
            KAP, FUS, Dv = (CC[:, q, 0, :] for q in range(3))

            def diagonal(m, first=0, right=0):
                return m.rearrange("p j t -> p (j t)")[:, first * (L + 1) + right:L * L - right * L:L + 1]

            dve.wait_ge(set_once, 14)
            dve.wait_ge(lanes_act, 8)
            did(v.tensor_scalar(R[VB], Dv, 2.0 / D, None, ALU.mult))
            did(v.tensor_copy(ST[:, R_N, 0:L - 1], diagonal(V, 1)))
            did(v.tensor_tensor(R[KD], KAP, Dv, ALU.mult))
            did(v.tensor_tensor(R[FD], FUS, Dv, ALU.mult))
            did(v.tensor_scalar(R[DVS], Dv, float(np.sqrt(2.0 / D)), None, ALU.mult))
            last()
            did(v.tensor_tensor(tmpA, *outer(Dv, R[VB]), ALU.mult))
            last()
            v.scalar_tensor_tensor(out=VC, in0=V, scalar=2.0, in1=tmpA, op0=ALU.mult, op1=ALU.subtract).then_inc(vc_ready, 1)
            v.tensor_scalar(R[MM], R[FD], 1.0 / N, None, ALU.mult).then_inc(mrow_ready, 1)
            did(v.tensor_scalar(R[M2], R[FD], 2.0 / N, None, ALU.mult))
            did(v.tensor_scalar(R[MR], R[FD], -2.0 / N / N, None, ALU.mult))
            did(v.tensor_scalar(R[MZ], R[FD], float(np.sqrt(2.0 * D)) / N, None, ALU.mult))
            did(v.tensor_tensor(R[T0], diagonal(bT), diagonal(V), ALU.mult))
            did(v.tensor_tensor(R[T1], R[FD], R[FD], ALU.mult))
            last()
            did(v.scalar_tensor_tensor(out=R[T0], in0=R[T1], scalar=-1.0 / N, in1=R[T0], op0=ALU.mult, op1=ALU.add))
            last()
            did(v.tensor_scalar(ST[:, R_B, 0:L], R[T0], 1.0 / N, None, ALU.mult))
            last()
            v.tensor_scalar(R[T0], R[T0], 1.0 / N, 0.0, ALU.mult, ALU.max).then_inc(b_ready, 1)
            did(v.tensor_tensor(tmpA, aT, V, ALU.mult))
            did(v.tensor_tensor(tmpB, *outer(R[M2], R[KD]), ALU.mult))
            last()
            did(v.scalar_tensor_tensor(out=CC[:, 3, 1:L + 1, 0:L - 1], in0=tmpA[:, :, 1:L], scalar=-2.0, in1=tmpB[:, :, 1:L], op0=ALU.mult, op1=ALU.add))
            last()
            did(v.tensor_tensor(tmpA, bT, V, ALU.mult))
            did(v.tensor_tensor(tmpB, *outer(R[MR], R[FD]), ALU.mult))
            did(v.tensor_copy(ST[:, R_CD, 0:L - 1], diagonal(CC[:, 3, 1:L + 1, :])[:, 0:L - 1]))
            last()
            did(v.scalar_tensor_tensor(out=CC[:, 4, 1:L + 1, :], in0=tmpA, scalar=2.0 / N, in1=tmpB, op0=ALU.mult, op1=ALU.add))
            last()
            did(v.tensor_tensor(tmpA, aT, R[DVS].unsqueeze(2).broadcast_to([W, L, L]), ALU.mult))
            did(v.tensor_tensor(tmpB, *outer(R[MZ], KAP), ALU.mult))
            did(v.tensor_scalar(R[VJJ], diagonal(VC), 0.5, None, ALU.mult))
            last()
            did(v.tensor_tensor(CC[:, 5, 1:L + 1, :], tmpA, tmpB, ALU.subtract))
            last()
            did(v.tensor_tensor(tmpA, aT, R[VJJ].unsqueeze(2).broadcast_to([W, L, L]), ALU.mult))
            did(v.scalar_tensor_tensor(out=tmpB, in0=CC[:, 5, 1:L + 1, :], scalar=0.5, in1=CC[:, 5, 1:L + 1, :], op0=ALU.mult, op1=ALU.mult))
            last()
            did(v.tensor_tensor(tmpA, tmpA, aT, ALU.mult))
            last()
            did(v.tensor_tensor(GG, tmpA, tmpB, ALU.add))
            last()
            did(v.tensor_copy(ST[:, R_G, 0:L - 1], diagonal(GG, 0, 1)))
            v.tensor_copy(SQ[:, 0:1], V[:, 0, 0:1]).then_inc(ssq_ready, 1)
            last()

            added = formed = o.n
            for j in range(L):
                sg = SG[:, j, 2:3]
                n = L - 2 - j
                need(max(added, formed))
                dve.wait_ge(sigma_ready, j + 1)
                v.tensor_tensor_scan(WS[:, j, :], SG[:, j, :], ST[:, R_N:R_X + 1, j], 0.0, ALU.mult, ALU.add).then_inc(w_ready, 1)
                if j == L - 1:
                    break
                if n > 0:
                    dve.wait_ge(oj_ready, j + 1)
                    nxt = ST[:, j + 1:j + 2, j + 2:L]
                    did(v.scalar_tensor_tensor(out=nxt, in0=OJ[j][:, 0:1, :], scalar=sg, in1=nxt, op0=ALU.mult, op1=ALU.add))
                rows = ST[:, R_D:R_Z + 1:R_R - R_D, j + 1:L]
                added = did(v.scalar_tensor_tensor(out=rows, in0=CC[:, 3:6, j + 1, j + 1:L], scalar=sg, in1=rows, op0=ALU.mult, op1=ALU.add))
                if n > 0:
                    u = did(v.scalar_tensor_tensor(out=U[:, 0:n], in0=GG[:, j, j + 2:L], scalar=sg, in1=ST[:, R_T, j + 1:L - 1], op0=ALU.mult, op1=ALU.add))
                dve.wait_ge(w_ready, j + 1)
                e0 = R_E * RW + j + 1
                did(v.tensor_tensor(STf[:, e0:e0 + RW + 2:RW + 1], WS[:, j, SCAN - 1:SCAN].broadcast_to([W, 2]), EC, ALU.mult))
                if n > 0:
                    need(added)
                    t1 = did(v.tensor_tensor(P2[:, :, 0:n], ST[:, j + 1:R_Z + 1:R_Z - j - 1, j + 2:L], CC[:, 0:6:5, j + 2, j + 2:L], ALU.mult))
                dve.wait_ge(h_ready, j + 1)
                s3_ = did(v.tensor_tensor_scan(S3[:, j, :], HG[:, j + 1, :], WS[:, j, 0:7:3], 0.0, ALU.mult, ALU.add))
                if n > 0:
                    need(u)
                    formed = did(v.scalar_tensor_tensor(out=ST[:, R_Q, j + 1:L - 1], in0=U[:, 0:n], scalar=sg, in1=ST[:, R_Q, j + 1:L - 1],
                                                        op0=ALU.mult, op1=ALU.add))
                need(s3_)
                v.tensor_scalar(SQ[:, j + 1:j + 2], S3[:, j, 2:3], 0.0, None, ALU.max).then_inc(ssq_ready, 1)
                if n > 0:
                    need(t1)
                    formed = did(v.tensor_tensor(ST[:, R_T, j + 1:L - 1], P2[:, 0, 0:n], P2[:, 1, 0:n], ALU.add))
                if n > 1:
                    later = ST[:, j + 2:L - 1, j + 2:L]
                    added = did(v.scalar_tensor_tensor(out=later, in0=OJ[j][:, 1:, :], scalar=sg, in1=later, op0=ALU.mult, op1=ALU.add))

            dve.wait_ge(h_ready, L)
            did(v.reciprocal(rh, HG[:, HALF:L + 1:HALF, 1]))
            last()
            v.tensor_scalar(wts, SG[:, :, 2], rh[:, 1:2], None, ALU.mult).then_inc(wts_ready, 1)
            dve.wait_ge(sb_ready, 1)
            v.scalar_tensor_tensor(out=c0, in0=SG[:, 0:HALF, 2], scalar=rh[:, 0:1], in1=R[SB][:, 0:HALF], op0=ALU.mult, op1=ALU.mult).then_inc(c0_ready, 1)
            dve.wait_ge(wts_ready, 1)
            cc = did(v.tensor_tensor(c1, wts, R[SB], ALU.mult))
            dve.wait_ge(wcol_done, 1)
            dve.wait_ge(neg_act, 1)
            dve.wait_ge(last_act, 3)
            did(v.tensor_copy(wcol, PS[0:L, 5, 0:1]))
            last()
            v.tensor_scalar(UW, U32, wcol, None, ALU.mult).then_inc(uw_ready, 1)
            v.tensor_scalar(WM, con[0:L, C_ONES:C_ONES + F], wcol, negm, ALU.mult, ALU.mult).then_inc(uw_ready, 1)
            need(cc)
            dve.wait_ge(shift_done, 1)
            did(v.tensor_tensor(c1[0:W - 1, HALF:L], c1[0:W - 1, HALF:L], PS[0:W - 1, 6, 0:HALF], ALU.subtract))
            last()
            did(v.tensor_reduce(bound, c1, AX.X, ALU.add, apply_absolute_value=True))
            last()
            v.tensor_scalar(agree, bound, TOLERANCE, None, ALU.is_le).then_inc(agree_ready, 1)
            dve.wait_ge(count_done, 1)
            v.tensor_scalar(flag[:, :], PS[0:1, 4, 1:2], W - 1.5, None, ALU.is_ge).then_inc(flag_set, 1)

            def general():
                lo = Order(dve, loop_order)
                lo.did(v.tensor_copy(KF[:, 0:T // 2].rearrange("p (c i) -> p c i", i=HALF), KU[0:F, 0:S // 2, 0, 0:HALF]))
                lo.did(v.tensor_copy(KF[:, T // 2:T].rearrange("p (c i) -> p c i", i=HALF), KU[F:P, 1:SH, 0, 0:HALF]))
                v.memset(MS, 0.0).then_inc(state_ready, 1)
                lo.need(lo.n)
                n0 = lo.n
                per = 8
                with dve.Fori(0, T) as t:
                    lo.offset = t * per
                    dve.wait_ge(state_ready, t + 1)
                    lo.did(v.tensor_copy(vt, VT[:, bass.ds(t, 1)]))
                    n = lo.did(v.tensor_copy(kt, KF[:, bass.ds(t, 1)]))
                    lo.need(n)
                    v.tensor_scalar(DIAG, ident, vt, None, ALU.mult).then_inc(token_ready, 1)
                    dve.wait_ge(pred_done, t + 1)
                    n = lo.did(v.tensor_tensor(dv_, vt, PS[:, 0, 0:1], ALU.subtract))
                    lo.need(n)
                    v.tensor_tensor(d2, dv_, dv_, ALU.mult).then_inc(d2_ready, 1)
                    dve.wait_ge(s_ready, t + 1)
                    n = lo.did(v.scalar_tensor_tensor(out=su, in0=kt, scalar=sp_[0:F, :], in1=etac[0:F, :], op0=ALU.mult, op1=ALU.mult))
                    lo.need(n)
                    n = lo.did(v.scalar_tensor_tensor(out=MS, in0=PS[0:F, 1, 0:D], scalar=su, in1=MS, op0=ALU.mult, op1=ALU.add))
                    lo.need(n)
                    v.tensor_reduce(rs, MS, AX.X, ALU.add).then_inc(rows_ready, 1)
                    dve.wait_ge(sum_done, t + 1)
                    n = lo.did(v.tensor_scalar(mean, PS[0:F, 3, 0:1], 1.0 / N, None, ALU.mult))
                    lo.need(n)
                    n = lo.did(v.tensor_scalar(MS, MS, mean, None, ALU.subtract))
                    lo.need(n)
                    v.tensor_tensor_reduce(out=MQ, in0=MS, in1=MS, scale=1.0, scalar=0.0, op0=ALU.mult, op1=ALU.add, accum_out=r2).then_inc(sq_rows_ready, 1)
                    dve.wait_ge(sq_done, t + 1)
                    v.tensor_scalar(var, PS[0:F, 3, 1:2], 1.0 / N, EPS_LN, ALU.mult, ALU.add).then_inc(var_s_ready, 1)
                    dve.wait_ge(sd_s_ready, t + 1)
                    n = lo.did(v.reciprocal(rinv_, sd))
                    lo.need(n)
                    v.tensor_scalar(MS, MS, rinv_, None, ALU.mult).then_inc(state_ready, 1)
                    assert lo.n == n0 + per
                dve.wait_ge(state_ready, T + 1)

            general_path(dve, general)
            dve.wait_ge(xres_ready, 1)
            for b in range(4):
                xb = x[:, 4 * b:4 * b + 4, :].rearrange("p n d -> p (n d)")
                dve.wait_ge(ao_done, b + 1)
                v.tensor_tensor(xb, xb, bank(4 + b), ALU.add).then_inc(x1_ready, 1)
            o2 = Order(dve, dve_order2)

            dve.wait_ge(small_in, 16 * 12)
            v.tensor_scalar(s1h, s1, 0.5, None, ALU.mult).then_inc(scales_ready, 1)
            v.scalar_tensor_tensor(out=s12, in0=s1, scalar=0.5, in1=s2, op0=ALU.mult, op1=ALU.mult).then_inc(scales_ready, 1)
            did, need = o2.did, o2.need
            dve.wait_ge(x1_ready, 4)
            for n in range(NT):
                i = did(v.bn_stats(st[:, n, :], x[:, n, :]))
            need(i)
            for n in range(NT):
                i = did(v.bn_aggr(mv[:, n, :], st[:, n, :]))
            need(i)
            v.tensor_scalar(lnt[:, 0, :], mv[:, :, 1], EPS_LN, None, ALU.add).then_inc(var2_ready, 1)
            dve.wait_ge(sd2_ready, 1)
            need(did(v.reciprocal(lnt[:, 1, :], lnt[:, 1, :])))
            for n in range(NT):
                v.tensor_scalar(xn[:, n, :], x[:, n, :], mv[:, n, 0:1], lnt[:, 1, n:n + 1], ALU.subtract, ALU.mult).then_inc(xn2_ready, 1)
            dve.wait_ge(tab_in, 32)
            for u in range(8):
                dst, ch, b = (qT1, u, 4 + u) if u < 4 else (kT1, u - 4, u - 4)
                cols = slice(ch * BANK, (ch + 1) * BANK)
                ev, od = slice(ROT, ROT + 32), slice(ROT + 32, P)
                dve.wait_ge(qk_done, u + 1)
                if u >= 4:
                    dve.wait_ge(rope_add, u - 3)
                did(v.tensor_tensor(hB[ev, 0, cols], PS[od, b, :], arena[od, a_tab + T + ch * BANK:a_tab + T + (ch + 1) * BANK], ALU.mult))
                did(v.tensor_tensor(hB[od, 0, cols], PS[ev, b, :], arena[ev, a_tab + T + ch * BANK:a_tab + T + (ch + 1) * BANK], ALU.mult))
                v.tensor_tensor(dst[ROT:P, cols], PS[ROT:P, b, :], cosT[:, cols], ALU.mult).then_inc(qk_dve, 1)
            zu = [0]

            def gate(u):
                m, c = u % HT4, u // HT4
                dve.wait_ge(tanh_ready, u + 1)
                need(did(v.scalar_tensor_tensor(out=ZU[0], in0=TH[u % 2], scalar=1.0, in1=PS[:, 6, 0:ZC], op0=ALU.add, op1=ALU.mult)))
                v.scalar_tensor_tensor(out=hA[:, m, c * ZC:(c + 1) * ZC], in0=PS[:, 6, ZC:2 * ZC], scalar=s12[:, m:m + 1], in1=ZU[0],
                                       op0=ALU.mult, op1=ALU.mult).then_inc(hA_ready, 1)
                dve.wait_ge(hA_ready, u + 1)

            for t in range(NT + 1):
                if t < NT:
                    dve.wait_ge(s_done, t + 1)
                    need(did(v.tensor_reduce(mxs[:, t:t + 1], PS[:, 0:4, :].rearrange("p b c -> p (b c)")[:, 0:(t + 1) * P], AX.X, ALU.max)))
                    v.tensor_scalar(nbs[:, t:t + 1], mxs[:, t:t + 1], -1.0 / D, None, ALU.mult).then_inc(bias_ready, 1)
                    gate(2 * t)
                if t:
                    for gi, c, cnt in groups_of(t - 1):
                        if gi % 2 == 1:
                            dve.wait_ge(pt_done, gi + 1)
                            v.tensor_copy(PT[(t - 1) % 2][:, c * P:(c + cnt) * P], PS[:, 5, 0:cnt * P]).then_inc(pt_dve, 1)
                    dve.wait_ge(p_ready, t)
                    need(did(v.reciprocal(rinv[:, t - 1:t], rsum[:, t - 1:t])))
                    dve.wait_ge(pv_done, t)
                    v.scalar_tensor_tensor(out=x[:, t - 1, :], in0=PS[:, 7, ((t - 1) % 4) * D:((t - 1) % 4 + 1) * D], scalar=rinv[:, t - 1:t],
                                           in1=x[:, t - 1, :], op0=ALU.mult, op1=ALU.add).then_inc(pv_read, 1)
                if t < NT:
                    gate(2 * t + 1)
            for b in range(4):
                dve.wait_ge(y_done, b + 1)
                dve.wait_ge(pv_read, NT)
                w = hB[:, 0, b * BANK:(b + 1) * BANK]
                need(did(v.tensor_tensor(w.rearrange("p (n e) -> p n e", n=4), bank(b).rearrange("p (n e) -> p n e", n=4),
                                         s3.unsqueeze(1).broadcast_to([P, 4, D]), ALU.mult)))
                xb = x[:, 4 * b:4 * b + 4, :].rearrange("p n d -> p (n d)")
                v.tensor_tensor(xb, xb, w, ALU.add).then_inc(out_ready, 1)


INPUTS = ["L0_attn_x", "L0_attn_norm_weight", "L0_attn_eta", "L0_ffn_W1", "L0_ffn_W2", "L0_ffn_b2", "L1_attn_wo", "L1_ffn_w3_s"]
TRANSPOSED = {"WkT": "L0_attn_Wk", "WvT": "L0_attn_Wv", "WqT": "L0_attn_Wq", "WoutT": "L0_attn_Wout", "w1_T": "L1_ffn_w1_w", "w2_T": "L1_ffn_w2_w"}
BY_PARTITION = {"s1": "L1_ffn_w1_s", "s2": "L1_ffn_w2_s", "sh1": "L1_ffn_h1_s", "sh2": "L1_ffn_h2_s"}


def rotary_tables():
    freqs = np.power(np.float32(10000.0), -np.arange(ROT // 2, dtype=np.float32) / np.float32(ROT // 2))
    angle = (np.arange(T, dtype=np.float32)[None, :] * freqs[:, None]).astype(np.float32)
    cos, sin = np.cos(angle).astype(np.float32), np.sin(angle).astype(np.float32)
    return np.concatenate([cos, cos]), np.concatenate([sin, -sin])


def kernel(**inputs):
    import concourse.bacc as bacc
    from concourse.bass_utils import run_bass_kernel_spmd

    nc = bacc.Bacc("TRN2", target_bir_lowering=False, num_devices=1)
    given = {n: np.asarray(v) for n, v in inputs.items()}
    arrays = {n: given[n] for n in INPUTS}
    arrays.update({n: given[m].T for n, m in TRANSPOSED.items()})
    arrays.update({n: given[m].reshape(-1, P).T for n, m in BY_PARTITION.items()})
    arrays["b1_by_partition"] = given["L0_ffn_b1"].reshape(-1, 2, P).transpose(0, 2, 1)
    for n, m in (("h1_T", "L1_ffn_h1_w"), ("h2_T", "L1_ffn_h2_w"), ("w3_T", "L1_ffn_w3_w")):
        arrays[n] = given[m].T.reshape(HT4, P, -1).transpose(1, 0, 2)
    for n, m in (("wq_turned", "L1_attn_wq"), ("wk_turned", "L1_attn_wk")):
        arrays[n] = np.concatenate([given[m][0][:, ROT:], given[m][0][:, :ROT]], axis=1)
    arrays["wv_T"] = given["L1_attn_wv"][0].T
    arrays["shape_constants"] = shape_constants()
    arrays["cos"], arrays["sin"] = rotary_tables()
    arrays = {n: np.ascontiguousarray(v) for n, v in arrays.items()}
    aps = {n: nc.dram_tensor(n, v.shape, mybir.dt.from_np(v.dtype), kind="ExternalInput").ap() for n, v in arrays.items()}
    out = nc.dram_tensor("out", (1, T, D), F32, kind="ExternalOutput").ap()
    program(nc, aps, out)
    return run_bass_kernel_spmd(nc, [arrays], core_ids=[0]).results[0]["out"]
```

```python
from contextlib import ExitStack

import numpy as np
import concourse.bass as bass
from concourse import mybir

ALU = mybir.AluOpType
ACT = mybir.ActivationFunctionType
AX = mybir.AxisListType
F32 = mybir.dt.float32
I32 = mybir.dt.int32
F16 = mybir.dt.float16

P = 128
T, D = 2048, 128
NT = T // P
F = 64
HALF = 16
S = T // HALF
L = 2 * HALF
W = S - 1
SH = S // 2 + 1
N = float(F * D)
BANK = 512
EPS_LN, EPS_RMS, ETA_MIN = 1e-5, 1e-6, 1e-6
EXPERT = 1
EH = 256
HID = 512
TOLERANCE = 2.0 ** -12
HT4 = HID // P
ROT = 64
ZC = 256
LOW = 2.0 ** 11
LIMIT = 2.0 ** 15

C_ID, C_CAUSAL, C_ONES, C_END = 0, 128, 256, 384

RW = L + 2
R_N, R_0, R_CD, R_D, R_G, R_T, R_Q, R_B, R_R, R_E, R_X = range(L, L + 11)
R_Z = R_R + (R_R - R_D)
R_END = R_Z + 1
SCAN = R_X - R_N + 1


def shape_constants():
    c = np.zeros((P, C_END), np.float32)
    i = np.arange(P)
    c[:, C_ID:C_ID + P] = np.eye(P)
    c[:, C_CAUSAL:C_CAUSAL + P] = np.where(i[None, :] > i[:, None], -1e30, 0.0)
    c[:, C_ONES:C_ONES + P] = 1.0
    return c


class Order:

    def __init__(self, engine, semaphore):
        self.engine, self.semaphore, self.n, self.offset = engine, semaphore, 0, 0

    def did(self, instruction):
        instruction.then_inc(self.semaphore, 1)
        self.n += 1
        return self.n

    def need(self, n):
        self.engine.wait_ge(self.semaphore, n + self.offset)


def program(nc, a, out):
    with ExitStack() as ctx:
        def sb(name, shape, dt=F32):
            return ctx.enter_context(nc.sbuf_tensor(name, shape, dt))

        def sem(name):
            return ctx.enter_context(nc.semaphore(name))

        x = sb("x", [P, NT, D])
        xn = sb("xn", [P, NT, D])
        xT = sb("xT", [P, T])
        con = sb("con", [P, C_END])
        ident = con[:, C_ID:C_ID + P]
        ones = con[:, C_ONES:C_ONES + P]
        wkT = sb("wkT", [P, F])
        wvT = sb("wvT", [P, D])
        wqT = sb("wqT", [P, F])
        woutT = sb("woutT", [P, D])
        normw = sb("normw", [P, 1])
        etac = sb("etac", [P, 1])
        w1e = sb("w1e", [P, EH])
        w2e = sb("w2e", [P, 2, D])
        b1e = sb("b1e", [P, 2])
        b2e = sb("b2e", [P, D])
        st = sb("st", [P, NT, 6])
        mv = sb("mv", [P, NT, 2])
        lnt = sb("lnt", [P, 7, NT])
        mxb = sb("mxb", [P, 40])
        rsums = sb("rsums", [P, 40])
        small = sb("small", [P, 40])

        arena = sb("arena", [P, 45000])
        at = [0]

        def take(n):
            at[0] += n
            return arena[:, at[0] - n:at[0]]

        wturn, wswap, wskip, wvT2, wo, WVO, s3 = (take(P) for _ in range(7))
        w1T, w2T, w3T = (take(HID) for _ in range(3))
        w3T = w3T.rearrange("p (m e) -> p m e", m=HT4)
        s1, s2, sh1, sh2, s1h, s12 = (take(HT4) for _ in range(6))
        a_tab = at[0]
        HT = take(2 * T).rearrange("p (h t) -> p h t", h=2)
        cosT, sinT = arena[:, a_tab:a_tab + T], arena[:, a_tab + T:a_tab + 2 * T]
        a_blocks = at[0]

        KU = take(SH * 2 * L).rearrange("p (c t i) -> p c t i", c=SH, t=2)
        UXf = take(SH * 2 * (HALF + 1))
        UX = UXf.rearrange("p (c h j) -> p c h j", c=SH, h=2)
        VT = take(T + HALF)
        VX = take(S * (HALF + 1)).rearrange("p (s j) -> p s j", s=S)
        xrT = take(T)
        MOE = xrT
        KE = take(SH * HALF)
        QT, QE = take(T // 2), xT[:, 0:T // 2]
        XR = arena[:, at[0]:at[0] + T].rearrange("p (n d) -> p n d", n=NT)
        Gf = take((HALF + 1) * S)
        G = Gf.rearrange("p (j s) -> p j s", j=HALF + 1)
        CC = take(6 * (L + 1) * L)[0:W].rearrange("p (q j t) -> p q j t", q=6, j=L + 1)
        GG = take(L * L)[0:W].rearrange("p (j t) -> p j t", j=L)
        VC = take(L * L)[0:W].rearrange("p (j l) -> p j l", j=L)
        tmpA, tmpB = (Gf[0:W, L * L * i:L * L * (i + 1)].rearrange("p (j t) -> p j t", j=L) for i in range(2))
        tmpC, tmpD = (xrT[0:W, L * L * i:L * L * (i + 1)].rearrange("p (j t) -> p j t", j=L) for i in range(2))
        STf = take(R_END * RW)[0:W]
        ST = STf.rearrange("p (r t) -> p r t", t=RW)
        lane = take(12 * L)[0:W].rearrange("p (r t) -> p r t", t=L)
        VB, MM, KD, FD, M2, MR, MZ, DVS, VJJ, SB, T0, T1 = range(12)
        SG = take(L * SCAN)[0:W].rearrange("p (j k) -> p j k", k=SCAN)
        WS = take(L * SCAN)[0:W].rearrange("p (j k) -> p j k", k=SCAN)
        HG = take((L + 1) * 3)[0:W].rearrange("p (j k) -> p j k", k=3)
        S3 = take(L * 3)[0:W].rearrange("p (j k) -> p j k", k=3)
        SQ = take(L)[0:W]
        U, P2 = take(L)[0:W], take(2 * L)[0:W].rearrange("p (r t) -> p r t", r=2)
        sc = take(16)
        EC, rh, bound, agree = sc[0:W, 0:2], sc[0:W, 2:4], sc[0:W, 4:5], sc[0:W, 5:6]
        wcol, negm = sc[0:L, 6:7], sc[0:L, 7:8]
        wts, c0, c1 = take(L)[0:W], take(HALF)[0:W], take(L)[0:W]
        U32, UW, WM = (take(F)[0:L] for _ in range(3))
        VW, WSUM = (take(D)[0:L] for _ in range(2))
        MW = take(D)
        a_oj = at[0]
        OJf = take(sum(n * n for n in range(L - 1)))
        OJ, o_ = [], 0
        for j in range(L - 2):
            n_ = L - 2 - j
            OJ.append(OJf[0:W, o_:o_ + n_ * n_].rearrange("p (l t) -> p l t", l=n_))
            o_ += n_ * n_
        KF = OJf[0:F, 0:T]
        MS, MQ, DIAG = OJf[0:F, 2 * T:2 * T + D], OJf[0:F, 2 * T + D:2 * T + 2 * D], OJf[:, 2 * T + 2 * D:2 * T + 3 * D]
        MT = OJf[:, 2 * T + 3 * D:2 * T + 3 * D + F]
        g_ = OJf[:, 2 * T + 4 * D:2 * T + 4 * D + 16]
        vt, dv_, d2, sp_ = (g_[:, i:i + 1] for i in range(4))
        kt, su, rs, r2, mean, var, sd, rinv_ = (g_[0:F, i:i + 1] for i in range(4, 12))

        b_at = [a_blocks]

        def second(n):
            b_at[0] += n
            return arena[:, b_at[0] - n:b_at[0]]

        w1H, w1L, w2H, w2L = (second(HID // 2).bitcast(F16) for _ in range(4))
        w3H, w3L = (second(HID // 2).bitcast(F16).rearrange("p (m e) -> p m e", m=HT4) for _ in range(2))
        h1H, h1L, h2H, h2L = (second(HT4 * HID // 2).bitcast(F16).rearrange("p (k o) -> p k o", k=HT4) for _ in range(4))
        xH, xL = (second(T // 2).bitcast(F16) for _ in range(2))
        qT1, kT1 = second(T), second(T)
        V1 = second(T).rearrange("p (n e) -> p n e", n=NT)
        hAf, hBf = second(HT4 * T), second(HT4 * T)
        hAH, hAL, hBH, hBL = (h[:, i * HT4 * T // 2:(i + 1) * HT4 * T // 2].bitcast(F16).rearrange("p (m t) -> p m t", m=HT4)
                              for h in (hAf, hBf) for i in range(2))
        Pr = [second(T) for _ in range(2)]
        PT = [second(T), xn[:, :, :].rearrange("p n d -> p (n d)")]
        assert max(b_at[0], at[0]) <= 45000, (b_at, at)
        TURN = [hBf[:, T * c:T * c + 2 * BANK].rearrange("p (k t) -> p k t", k=2) for c in range(2)]
        xd = hBf[:, T + 2 * BANK:T + 3 * BANK]
        h1S, h2S = (hBf[:, c:c + HT4 * HID].rearrange("p (k o) -> p k o", k=HT4) for c in (2 * T, 0))
        WC = [hBf[:, T + HID * i:T + HID * (i + 1)] for i in range(2)]
        gate_ = [hBf[:, 3 * T + ZC * i:3 * T + ZC * (i + 1)] for i in range(8)]
        TH, ZA, ZG, zd = gate_[0:3], gate_[3:6], gate_[6], gate_[7]
        FP, RP = ([q[:, BANK * i:BANK * (i + 1)] for i in range(4)] for q in (qT1, kT1))
        fin, ysc = V1, Pr[0]
        h1G, h2G = (q.rearrange("p (k o) -> p k o", k=HT4) for q in (qT1, kT1))
        gA, gB, gC, gz = (hAf[:, T * i:T * (i + 1)].rearrange("p (m t) -> p m t", m=HT4) for i in range(4))
        gT = hBf[:, 0:T].rearrange("p (m t) -> p m t", m=HT4)
        s12a, tern, ends = small[:, 0:HT4], small[:, 4:15], small[:, 16:16 + 3 * HT4]
        sums, reach, tmax, top_, ends_ok, fits = small[:, 28:30], small[:, 30:32], small[:, 32:33], small[:, 33:34], small[:, 34:35], small[:, 35:36]
        low_scale = small[:, 36:37]
        mxs, nbs, rsum, rinv = (lnt[:, i, :] for i in range(2, 6))

        PS = ctx.enter_context(nc.psum_tensor("PS", [P, 8, BANK], F32))
        flag = sb("flag", [1, 1], I32)
        fits_flag = sb("fits_flag", [1, 1], I32)

        x_in = [sem(f"x_in{c}") for c in range(4)]
        early_in, eta_in, moe_in, late_in = sem("early_in"), sem("eta_in"), sem("moe_in"), sem("late_in")
        dve_order, dve_order2, act_order, pool_order, loop_order = (
            sem(n) for n in ("dve_order", "dve_order2", "act_order", "pool_order", "loop_order"))
        var_ready, sd_ready = sem("var_ready"), sem("sd_ready")
        xr_ready, xn_ready, set_once = sem("xr_ready"), sem("xn_ready"), sem("set_once")
        xrt_done, xrt_act, xrt_dve = sem("xrt_done"), sem("xrt_act"), sem("xrt_dve")
        k_done, v_done, kphi_act, vt_ready, vx_ready = sem("k_done"), sem("v_done"), sem("kphi_act"), sem("vt_ready"), sem("vx_ready")
        eta_set, k_ready, ku_ready, ku_act = sem("eta_set"), sem("k_ready"), sem("ku_ready"), sem("ku_act")
        vgram_done, vgram_act, gram_done, gram_act, gram_dve, lanes_done, lanes_act = (
            sem(n) for n in ("vgram_done", "vgram_act", "gram_done", "gram_act", "gram_dve", "lanes_done", "lanes_act"))
        xnt_done, xnt_act, eh_done, eh_act, eo_done, eo_act = (sem(n) for n in ("xnt_done", "xnt_act", "eh_done", "eh_act", "eo_done", "eo_act"))
        q_done, qphi_act, q_ready, xres_ready = sem("q_done"), sem("qphi_act"), sem("q_ready"), sem("xres_ready")
        last_done, last_act, mrow_ready, neg_done, neg_act = (sem(n) for n in ("last_done", "last_act", "mrow_ready", "neg_done", "neg_act"))
        vc_ready, oj_ready, b_ready, sb_ready, rows_set, outer_ready = (
            sem(n) for n in ("vc_ready", "oj_ready", "b_ready", "sb_ready", "rows_set", "outer_ready"))
        ssq_ready, sigma_ready, w_ready, h_ready = sem("ssq_ready"), sem("sigma_ready"), sem("w_ready"), sem("h_ready")
        wts_ready, wcol_done, uw_ready, mw_done, mw_act = (sem(n) for n in ("wts_ready", "wcol_done", "uw_ready", "mw_done", "mw_act"))
        c0_ready, shift_done, agree_ready, count_done, flag_set = (sem(n) for n in ("c0_ready", "shift_done", "agree_ready", "count_done", "flag_set"))
        ao_done, x1_ready = sem("ao_done"), sem("x1_ready")
        token_ready, state_ready, pred_done, d2_ready, ss_done, s_ready = (
            sem(n) for n in ("token_ready", "state_ready", "pred_done", "d2_ready", "ss_done", "s_ready"))
        rows_ready, sum_done, sq_rows_ready, sq_done, var_s_ready, sd_s_ready = (
            sem(n) for n in ("rows_ready", "sum_done", "sq_rows_ready", "sq_done", "var_s_ready", "sd_s_ready"))
        gmt_done, gmt_act, gmw_done, gmw_act = (sem(n) for n in ("gmt_done", "gmt_act", "gmw_done", "gmw_act"))
        tab_in, small_in, h_in = sem("tab_in"), sem("small_in"), [sem(f"h_in{i}") for i in range(2)]
        var2_ready, sd2_ready, shift_ready, xn2_act, xn2_dve, xt2_done, xt2_act = (
            sem(n) for n in ("var2_ready", "sd2_ready", "shift_ready", "xn2_act", "xn2_dve", "xt2_done", "xt2_act"))
        wvo_done, wvo_act, turn_done, skip_done, skip_act, rope_dve, turned_dve, turned_pool = (
            sem(n) for n in ("wvo_done", "wvo_act", "turn_done", "skip_done", "skip_act", "rope_dve", "turned_dve", "turned_pool"))
        v1_done, v1_act = sem("v1_done"), sem("v1_act")
        s_done, bias_ready, p_ready, pt_done, pt_act, pt_dve, pv_done, pv_read = (
            sem(n) for n in ("s_done", "bias_ready", "p_ready", "pt_done", "pt_act", "pt_dve", "pv_done", "pv_read"))
        z_done, tanh_ready, hA_ready = sem("z_done"), sem("tanh_ready"), sem("hA_ready")
        g1_done, g1_act, g2_done, g2_act, y_done, out_ready = (
            sem(n) for n in ("g1_done", "g1_act", "g2_done", "g2_act", "y_done", "out_ready"))
        scales_ready = sem("scales_ready")
        w16_ready, xh_act, xl_ready, gate_high, gate_low, wc_ready, tern_ready, rest_ready, low_ready, pool2_order = (
            sem(n) for n in ("w16_ready", "xh_act", "xl_ready", "gate_high", "gate_low", "wc_ready", "tern_ready", "rest_ready", "low_ready", "pool2_order"))
        sums_ready, sums_done, fits_ready, fits_done, fits_set = (sem(n) for n in ("sums_ready", "sums_done", "fits_ready", "fits_done", "fits_set"))
        gw_in, gz_done, gt_ready, ga_ready, gh_done, gb_ready, gy_done, gy_read, net_order = (
            sem(n) for n in ("gw_in", "gz_done", "gt_ready", "ga_ready", "gh_done", "gb_ready", "gy_done", "gy_read", "net_order"))
        out_sem = sem("out_sem")

        def bank(b, rows=P, cols=BANK):
            return PS[0:rows, b, 0:cols]

        def groups_of(t):
            before = sum((u + 4) // 4 for u in range(t))
            return [(before + k, c, min(4, t + 1 - c)) for k, c in enumerate(range(0, t + 1, 4))]

        NU = HT4 * T // ZC
        counts = [3] * 8 + [2] * 4 + [0] * 5
        GATE_TILE = [list(range(sum(counts[:t]), sum(counts[:t + 1]))) for t in range(NT + 1)]
        GATE_BANK = [(6, 3, 2)[k] for n in counts for k in range(n)]
        GATE_AFTER = [max([w for w in range(u) if GATE_BANK[w] == GATE_BANK[u]], default=None) for u in range(NU)]
        assert len(GATE_BANK) == NU

        V_RUNS = [(b, s0, min(26, S - s0)) for b, s0 in zip((7, 2, 3, 5, 6), range(0, S, 26))]
        KU_RUNS = [(b, c0, min(15, SH - c0)) for b, c0 in zip((4, 7, 0, 1, 2), range(0, SH, 15))]
        K2 = BANK // HALF
        BLOCKS = [(slice(0, HALF), slice(0, L)), (slice(HALF, L), slice(HALF, L))]
        LANE_RUNS = [(0, 5, 0), (5, 5, 0), (10, 5, 0), (15, 2, 0), (17, 5, 1), (22, 5, 1), (27, 5, 1), (32, 1, 1)]

        block = ctx.enter_context(nc.Block())

        x_dram = a["L0_attn_x"].rearrange("b (n p) d -> p (b n) d", p=P)
        out_dram = out.rearrange("b (n p) d -> p (b n) d", p=P)

        @block.sync
        def _(sp):
            for c in range(4):
                sp.dma_start(x[:, 4 * c:4 * c + 4, :], x_dram[:, 4 * c:4 * c + 4, :]).then_inc(x_in[c], 16)
            sp.dma_start(normw[:], a["L0_attn_norm_weight"].rearrange("(d o) -> d o", o=1)).then_inc(early_in, 16)
            sp.dma_start(etac[0:F, :], a["L0_attn_eta"].rearrange("(d o) -> d o", o=1)).then_inc(eta_in, 16)
            sp.dma_start(etac[F:P, :], a["L0_attn_eta"].rearrange("(d o) -> d o", o=1)).then_inc(eta_in, 16)
            sp.dma_start(w1e[:], a["L0_ffn_W1"][EXPERT]).then_inc(moe_in, 16)
            sp.dma_start(w2e[:], a["L0_ffn_W2"][EXPERT].rearrange("(k p) o -> p k o", p=P)).then_inc(moe_in, 16)
            sp.dma_start(b1e[:], a["b1_by_partition"][EXPERT]).then_inc(moe_in, 16)
            sp.dma_start(b2e[:], a["L0_ffn_b2"][EXPERT:EXPERT + 1, :].broadcast_to([P, D])).then_inc(moe_in, 16)
            sp.dma_start(wqT[:], a["WqT"]).then_inc(late_in, 16)
            sp.dma_start(woutT[:], a["WoutT"]).then_inc(late_in, 16)
            for dst, n in ((wturn, "w_turn"), (wswap, "w_swap"), (wskip, "w_skip"), (wvT2, "wv_T"), (wo, "L1_attn_wo"), (w1T, "w1_T"), (w2T, "w2_T"),
                           (w3T, "w3_T"), (s1, "s1"), (s2, "s2"), (sh1, "sh1"), (sh2, "sh2")):
                sp.dma_start(dst, a[n]).then_inc(small_in, 16)
            sp.dma_start(s3, a["L1_ffn_w3_s"].rearrange("(o d) -> o d", o=1).broadcast_to([P, D])).then_inc(small_in, 16)
            sp.wait_ge(eo_done, 4)
            for i, n in enumerate(("cos", "sin")):
                sp.dma_start((cosT, sinT)[i], a[n]).then_inc(tab_in, 16)
            sp.wait_ge(x1_ready, 4)
            sp.dma_start(h1S, a["h1_T"]).then_inc(h_in[0], 16)
            sp.wait_ge(turned_dve, 4)
            sp.wait_ge(turned_pool, 4)
            sp.dma_start(h2S, a["h2_T"]).then_inc(h_in[1], 16)
            for c in range(4):
                sp.wait_ge(out_ready, c + 1)
                sp.dma_start(out_dram[:, 4 * c:4 * c + 4, :], fin[:, 4 * c:4 * c + 4, :]).then_inc(out_sem, 16)
            sp.wait_ge(out_sem, 64)

        def general_path(engine, run):
            engine.wait_ge(flag_set, 1)
            agreed = engine.value_load(flag[0:1, 0:1], min_val=0, max_val=1)
            with engine.If(agreed == 0):
                run()

        def network_general_path(engine, run):
            engine.wait_ge(fits_set, 1)
            fit = engine.value_load(fits_flag[0:1, 0:1], min_val=0, max_val=1)
            with engine.If(fit == 0):
                run()

        @block.tensor
        def _(pe):
            mm, tr = nc.tensor.matmul, nc.tensor.transpose

            pe.wait_ge(early_in, 16 * 4)
            for n in range(NT):
                pe.wait_ge(xr_ready, n + 1)
                i = tr(PS[:, n // 4, (n % 4) * P:(n % 4 + 1) * P], XR[:, n, :], ident)
                if n % 4 == 3:
                    i.then_inc(xrt_done, 1)
            pe.wait_ge(xrt_act, 2)
            pe.wait_ge(xrt_dve, 1)
            for b, c in enumerate(range(0, SH * HALF, BANK)):
                n = min(BANK, SH * HALF - c)
                for hf in range(2):
                    t0 = hf * (T - SH * HALF)
                    if b == 1 and hf == 1:
                        pe.wait_ge(xrt_dve, 2)
                    i = mm(PS[64 * hf:64 * hf + F, 4 + b, 0:n], wkT[:, :], xrT[:, t0 + c:t0 + c + n], start=True, stop=True)
                if b != 1:
                    i.then_inc(k_done, 1)
            for ch in range(4):
                mm(bank(ch), wvT[:, :], xrT[:, ch * BANK:(ch + 1) * BANK], start=True, stop=True).then_inc(v_done, 1)
            pe.wait_ge(late_in, 32)
            pe.wait_ge(vt_ready, 2)
            for hf in range(2):
                for b in range(2):
                    ch = 2 * hf + b
                    i = mm(PS[64 * hf:64 * hf + F, b, :], wqT[:, :], xrT[:, ch * BANK:(ch + 1) * BANK], start=True, stop=True)
            i.then_inc(q_done, 1)
            pe.wait_ge(set_once, 17)

            def values_gram(r):
                b, s0, cnt = V_RUNS[r]
                pe.wait_ge(vt_ready, min((s0 + cnt) * HALF // BANK, 3) + 1)
                pe.wait_ge(vx_ready, (s0 + cnt - 1) * HALF // BANK + 1)
                if r >= 1:
                    pe.wait_ge(vt_ready, 4)
                if r >= 3:
                    pe.wait_ge(k_ready, 2)
                for s in range(s0, s0 + cnt):
                    i = mm(PS[0:L, b, (s - s0) * (HALF + 1):(s - s0 + 1) * (HALF + 1)], VT[:, HALF * s:HALF * s + L], VX[:, s, :], start=True, stop=True)
                i.then_inc(vgram_done, 1)

            def keys_gram(r):
                b, c0, cnt = KU_RUNS[r]
                pe.wait_ge(ku_ready, 3 if r < 2 else 6)
                pe.wait_ge(ku_act, 2 if r < 2 else 4)
                if r == 1:
                    pe.wait_ge(vgram_act, 1)
                if r in (2, 3):
                    pe.wait_ge(qphi_act, 2)
                if r == 4:
                    pe.wait_ge(vgram_act, 2)
                for c in range(c0, c0 + cnt):
                    i = mm(PS[0:2 * L, b, (c - c0) * 2 * (HALF + 1):(c - c0 + 1) * 2 * (HALF + 1)], KU[:, c, :, :].rearrange("p t i -> p (t i)"),
                           UX[:, c, :, :].rearrange("p h j -> p (h j)"), start=True, stop=True)
                i.then_inc(gram_done, 1)

            values_gram(0)
            values_gram(1)
            values_gram(2)
            keys_gram(0)
            values_gram(3)
            values_gram(4)
            for r in range(1, 5):
                keys_gram(r)
            pe.wait_ge(vgram_act, 5)
            pe.wait_ge(gram_act, 3)
            pe.wait_ge(gram_dve, 2)
            for b, (r0, cnt, behind) in enumerate(LANE_RUNS):
                for r in range(r0, r0 + cnt):
                    j = (HALF if r == 0 else r - 1) if not behind else r - 1 - HALF
                    i = tr(PS[0:W, b, (r - r0) * 3 * L:(r - r0 + 1) * 3 * L], G[0:3 * L, j, behind:behind + W], ident[0:3 * L, 0:3 * L])
                i.then_inc(lanes_done, 1)
            pe.wait_ge(xn_ready, NT)
            for n in range(NT):
                if n % 4 == 0:
                    pe.wait_ge(lanes_act, n // 4 + 1)
                i = tr(PS[:, n // 4, (n % 4) * P:(n % 4 + 1) * P], xn[:, n, :], ident)
                if n % 4 == 3:
                    i.then_inc(xnt_done, 1)
            pe.wait_ge(lanes_act, 8)
            tr(PS[0:L, 7, 0:F], KU[F:P, SH - 2, 1, :], con[F:P, C_ID + F:C_ID + P])
            mm(PS[0:L, 7, F:F + D], VT[:, T - L:T], woutT[:, :], start=True, stop=True)
            mm(PS[0:L, 7, F + D:F + 2 * D], ones[:, 0:L], woutT[:, :], start=True, stop=True).then_inc(last_done, 1)
            pe.wait_ge(mrow_ready, 1)
            mm(PS[0:L, 6, 0:1], lane[:, MM, :], con[0:W, C_ID + W - 1:C_ID + W], start=True, stop=True).then_inc(neg_done, 1)
            pe.wait_ge(moe_in, 64)
            pe.wait_ge(xnt_act, 4)
            pe.wait_ge(last_act, 3)
            pe.wait_ge(neg_act, 1)
            for h in range(2):
                for ch in range(4):
                    mm(bank((4, 0)[h] + ch), w1e[:, h * P:(h + 1) * P], xT[:, ch * BANK:(ch + 1) * BANK], start=True, stop=True).then_inc(eh_done, 1)
            pe.wait_ge(eh_act, 8)
            for n in range(NT):
                for h in range(2):
                    i = mm(PS[:, n // 4, (n % 4) * P:(n % 4 + 1) * P], HT[:, h, n * P:(n + 1) * P], w2e[:, h, :], start=(h == 0), stop=(h == 1))
                if n % 4 == 3:
                    i.then_inc(eo_done, 1)
            pe.wait_ge(small_in, 16 * 13)
            mm(PS[:, 7, 0:D], wvT2, wo, start=True, stop=True).then_inc(wvo_done, 1)
            pe.wait_ge(wts_ready, 1)
            mm(PS[0:L, 5, 0:1], wts, con[0:W, C_ID + W - 1:C_ID + W], start=True, stop=True).then_inc(wcol_done, 1)
            pe.wait_ge(c0_ready, 1)
            mm(PS[0:W - 1, 6, 0:HALF], con[0:W, C_ID + 1:C_ID + W], c0, start=True, stop=True).then_inc(shift_done, 1)
            pe.wait_ge(uw_ready, 2)
            pe.wait_ge(wvo_act, 1)
            mm(PS[0:F, 7, 0:D], UW, VW, start=True, stop=False)
            mm(PS[0:F, 7, 0:D], WM, WSUM, start=False, stop=True).then_inc(mw_done, 1)
            pe.wait_ge(agree_ready, 1)
            mm(PS[0:1, 4, 1:2], agree[0:W - 1, :], con[0:W - 1, C_ONES:C_ONES + 1], start=True, stop=True).then_inc(count_done, 1)

            def general():
                with pe.Fori(0, T) as t:
                    pe.wait_ge(state_ready, t + 1)
                    pe.wait_ge(token_ready, t + 1)
                    mm(PS[:, 0, 0:1], MS, kt, start=True, stop=True)
                    mm(PS[:, 1, 0:D], ones, DIAG, start=True, stop=True).then_inc(pred_done, 1)
                    pe.wait_ge(d2_ready, t + 1)
                    mm(PS[:, 2, 0:1], ones, d2, start=True, stop=True).then_inc(ss_done, 1)
                    pe.wait_ge(rows_ready, t + 1)
                    mm(PS[:, 3, 0:1], ones[0:F, :], rs, start=True, stop=True).then_inc(sum_done, 1)
                    pe.wait_ge(sq_rows_ready, t + 1)
                    mm(PS[:, 3, 1:2], ones[0:F, :], r2, start=True, stop=True).then_inc(sq_done, 1)
                pe.wait_ge(state_ready, T + 1)
                tr(PS[:, 0, 0:F], MS, con[0:F, C_ID:C_ID + F]).then_inc(gmt_done, 1)
                pe.wait_ge(gmt_act, 1)
                mm(PS[0:F, 7, 0:D], MT, woutT[:, :], start=True, stop=True).then_inc(gmw_done, 1)
                pe.wait_ge(gmw_act, 2)

            pe.wait_ge(mw_act, 2)
            general_path(pe, general)
            pe.wait_ge(q_ready, 1)
            pe.wait_ge(eo_act, 4)
            for n in range(NT):
                h0 = F * (n // (NT // 2))
                i = mm(PS[:, 4 + n // 4, (n % 4) * P:(n % 4 + 1) * P], QT[h0:h0 + F, n % (NT // 2) * P:(n % (NT // 2) + 1) * P], MW[h0:h0 + F, :], start=True, stop=True)
                if n % 4 == 3:
                    i.then_inc(ao_done, 1)

            def normed(c):
                b = 4 * (c % 2)
                pe.wait_ge(xn2_act, 2 * c + 2)
                pe.wait_ge(xn2_dve, 2 * c + 2)
                if c >= 2:
                    pe.wait_ge(xt2_act, c - 1)
                for n in range(4 * c, 4 * c + 4):
                    i = tr(PS[:, b, (n % 4) * P:(n % 4 + 1) * P], xn[:, n, :], ident)
                i.then_inc(xt2_done, 1)

            def projected(c):
                b = 4 * (c % 2)
                xc = xT[:, c * BANK:(c + 1) * BANK]
                pe.wait_ge(xt2_act, c + 1)
                if c >= 2:
                    pe.wait_ge(rope_dve, 2 * c - 2)
                    pe.wait_ge(skip_act, 2 * c - 2)
                mm(bank(b + 2), wturn, xc, start=True, stop=True).then_inc(turn_done, 1)
                mm(bank(b + 3), wswap, xc, start=True, stop=True).then_inc(turn_done, 1)
                mm(bank(b + 1), wskip, xc, start=True, stop=True).then_inc(skip_done, 1)

            def values(c):
                b = (0, 4, 1, 5)[c]
                pe.wait_ge(*((xt2_act, c + 3) if c < 2 else (skip_act, 2 * c + 2)))
                for n in range(4 * c, 4 * c + 4):
                    i = mm(PS[:, b, (n % 4) * P:(n % 4 + 1) * P], xT[:, n * P:(n + 1) * P], WVO, start=True, stop=True)
                i.then_inc(v1_done, 1)

            pe.wait_ge(x1_ready, 4)
            pe.wait_ge(wvo_act, 1)
            normed(0)
            normed(1)
            for c in range(4):
                projected(c)
                if c < 2:
                    normed(c + 2)
            for c in range(4):
                values(c)

            def gated(u):
                m, c = u % HT4, u // HT4
                if GATE_AFTER[u] is not None:
                    pe.wait_ge(hA_ready, GATE_AFTER[u] + 1)
                if u == 0:
                    pe.wait_ge(w16_ready, 4)
                if u % (2 * HT4) == 0:
                    pe.wait_ge(xl_ready, u // (2 * HT4) + 1)
                for k, (wH, wL) in enumerate(((w1H, w1L), (w2H, w2L))):
                    z = PS[:, GATE_BANK[u], k * ZC:(k + 1) * ZC]
                    mm(z, wH[:, m * P:(m + 1) * P], xH[:, c * ZC:(c + 1) * ZC], start=True, stop=False)
                    i = mm(z, wL[:, m * P:(m + 1) * P], xL[:, c * ZC:(c + 1) * ZC], start=False, stop=True)
                i.then_inc(z_done, 1)

            def scores(t):
                if t % 4 == 0:
                    pe.wait_ge(skip_act, t // 2 + 2)
                    pe.wait_ge(turned_dve, t // 4 + 1)
                    pe.wait_ge(turned_pool, t // 4 + 1)
                    pe.wait_ge(v1_act, t // 4 + 1)
                before = groups_of(t - 1) if t else []
                for k, (gi, c, cnt) in enumerate(groups_of(t)):
                    if k == len(before) and k:
                        pe.wait_ge(hA_ready, max([u for u in range(NU) if GATE_BANK[u] == k], default=-1) + 1)
                    if k < len(before):
                        pe.wait_ge(p_ready, before[k][0] + 1)
                    last = c + 4 > t
                    i = mm(PS[:, k, 0:cnt * P], qT1[:, t * P:(t + 1) * P], kT1[:, c * P:(c + cnt) * P], start=True, stop=not last)
                    if last:
                        i = mm(PS[:, k, (cnt - 1) * P:cnt * P], ident, con[:, C_CAUSAL:C_CAUSAL + P], start=False, stop=True)
                    i.then_inc(s_done, 1)

            def turn_round(t, gi, c, cnt):
                pe.wait_ge(p_ready, gi + 1)
                if gi >= 2:
                    (pe.wait_ge(pt_act, gi // 2) if gi % 2 == 0 else pe.wait_ge(pt_dve, gi // 2))
                for b in range(c, c + cnt):
                    i = tr(PS[:, 4 + gi % 2, (b - c) * P:(b - c + 1) * P], Pr[t % 2][:, b * P:(b + 1) * P], ident)
                i.then_inc(pt_done, 1)

            def weighted(t, gi, c, cnt):
                if gi % 2 == 0:
                    pe.wait_ge(pt_act, gi // 2 + 1)
                else:
                    pe.wait_ge(pt_dve, gi // 2 + 1)
                if c == 0 and t:
                    pe.wait_ge(pv_read, t)
                for b in range(c, c + cnt):
                    i = mm(PS[:, 7, (t % 4) * D:(t % 4 + 1) * D], PT[t % 2][:, b * P:(b + 1) * P], V1[:, b, :], start=(b == 0), stop=(b == t))
                if c + cnt > t:
                    i.then_inc(pv_done, 1)

            for t in range(NT + 1):
                if t < NT:
                    scores(t)
                groups = groups_of(t - 1) if t else []
                for g in groups[0:2]:
                    turn_round(t - 1, *g)
                if t < NT:
                    if t == 0:
                        pe.wait_ge(skip_act, 8)
                        pe.wait_ge(rope_dve, 8)
                        pe.wait_ge(v1_act, 4)
                for u in GATE_TILE[t][0:1]:
                    gated(u)
                for k, g in enumerate(groups):
                    weighted(t - 1, *g)
                    if k + 2 < len(groups):
                        turn_round(t - 1, *groups[k + 2])
                for u in GATE_TILE[t][1:]:
                    gated(u)
                if t == NT - 2:
                    pe.wait_ge(sums_ready, 2)
                    mm(PS[:, 6, 0:2], ones, sums, start=True, stop=True).then_inc(sums_done, 1)
            pe.wait_ge(fits_ready, 1)
            mm(PS[0:1, 6, 2:3], fits, con[:, C_ONES:C_ONES + 1], start=True, stop=True).then_inc(fits_done, 1)
            pe.wait_ge(w16_ready, 2 * 11)
            pe.wait_ge(gate_low, NU)
            pe.wait_ge(pv_read, NT)
            for layer, (wH, wL, sH, sL, done, read) in enumerate(((h1H, h1L, hAH, hAL, g1_done, g1_act), (h2H, h2L, hBH, hBL, g2_done, g2_act))):
                for ch in range(4):
                    cols = slice(ch * BANK, (ch + 1) * BANK)
                    if layer:
                        pe.wait_ge(low_ready, 4 * ch + 4)
                    for m in range(HT4):
                        u = 4 * ch + m
                        if u >= 8:
                            pe.wait_ge(read, u - 7)
                        elif layer:
                            pe.wait_ge(g1_act, 8 + u + 1)
                        elif u == 6:
                            pe.wait_ge(fits_set, 1)
                        for k in range(HT4):
                            mm(bank(u % 8), wH[:, k, m * P:(m + 1) * P], sH[:, k, cols], start=(k == 0), stop=False)
                            i = mm(bank(u % 8), wL[:, k, m * P:(m + 1) * P], sL[:, k, cols], start=False, stop=(k == HT4 - 1))
                        i.then_inc(done, 1)
            for n in range(NT):
                if n % 4 == 0:
                    pe.wait_ge(low_ready, 16 + n + 4)
                    if n == 0:
                        pe.wait_ge(g2_act, 12)
                y = PS[:, n // 4, (n % 4) * P:(n % 4 + 1) * P]
                for k in range(HT4):
                    mm(y, hAH[:, k, n * P:(n + 1) * P], w3H[:, k, :], start=(k == 0), stop=False)
                    i = mm(y, hAL[:, k, n * P:(n + 1) * P], w3L[:, k, :], start=False, stop=(k == HT4 - 1))
                if n % 4 == 3:
                    i.then_inc(y_done, 1)

            def network():
                pe.wait_ge(gw_in, 32)
                with pe.Fori(0, 4) as c:
                    xc = xT[:, bass.ds(c * BANK, BANK)]
                    for m in range(HT4):
                        mm(bank(m), w1T[:, m * P:(m + 1) * P], xc, start=True, stop=True)
                        mm(bank(4 + m), w2T[:, m * P:(m + 1) * P], xc, start=True, stop=True).then_inc(gz_done, 1)
                    for b0, w, src in ((0, h1G, gA), (4, h2G, gB)):
                        (pe.wait_ge(ga_ready, c * HT4 + HT4) if b0 == 0 else pe.wait_ge(gb_ready, c * 2 * HT4 + HT4))
                        for m in range(HT4):
                            for k in range(HT4):
                                i = mm(bank(b0 + m), w[:, k, m * P:(m + 1) * P], src[:, k, :], start=(k == 0), stop=(k == HT4 - 1))
                            i.then_inc(gh_done, 1)
                    pe.wait_ge(gb_ready, c * 2 * HT4 + 2 * HT4)
                    for n in range(4):
                        for k in range(HT4):
                            i = mm(PS[:, 0, n * P:(n + 1) * P], gC[:, k, n * P:(n + 1) * P], w3T[:, k, :], start=(k == 0), stop=(k == HT4 - 1))
                    i.then_inc(gy_done, 1)
                    pe.wait_ge(gy_read, c + 1)

            network_general_path(pe, network)

        @block.scalar
        def _(act):
            f = nc.scalar.activation
            o = Order(act, act_order)
            act.dma_start(con[:], a["shape_constants"]).then_inc(early_in, 16)
            act.dma_start(wkT[:], a["WkT"]).then_inc(early_in, 16)
            act.dma_start(wvT[:], a["WvT"]).then_inc(early_in, 16)
            for h in range(2):
                act.wait_ge(var_ready, h + 1)
                f(lnt[:, 0:2, 8 * h:8 * h + 8], lnt[:, 0:2, 8 * h:8 * h + 8], ACT.Sqrt).then_inc(sd_ready, 1)
            act.wait_ge(early_in, 16 * 4)
            for b in range(2):
                act.wait_ge(xrt_done, b + 1)
                f(xrT[:, b * BANK:(b + 1) * BANK], bank(b), ACT.Copy, scale=normw[:, 0:1]).then_inc(xrt_act, 1)

            for h, (c0, c1) in enumerate(((0, BANK), (BANK, SH * HALF))):
                act.wait_ge(k_done, h + 1)
                n = o.did(f(KE[:, c0:c1], PS[:, 4:7, :].rearrange("p b c -> p (b c)")[:, c0:c1], ACT.Relu, scale=-1.0))
                o.need(n)
                f(KE[:, c0:c1], KE[:, c0:c1], ACT.Exp, scale=-1.0).then_inc(kphi_act, 1)
            zq = PS[:, 0:2, :].rearrange("p b c -> p (b c)")
            act.wait_ge(q_done, 1)
            f(QT, zq, ACT.Relu).then_inc(qphi_act, 1)
            n = o.did(f(QE, zq, ACT.Relu, scale=-1.0))
            o.need(n)
            for h, (c0, c1, d0) in enumerate(((0, K2, 0), (K2, SH, K2 - 1))):
                act.wait_ge(k_ready, h + 1)
                if h == 0:
                    act.wait_ge(eta_set, 1)
                f(KU[:, c0:c1, 1, 0:HALF], KU[:, c0:c1, 0, 0:HALF], ACT.Copy, scale=etac[:, 0:1]).then_inc(ku_act, 1)
                f(KU[:, d0:c1 - 1, 1, HALF:L], KU[:, d0 + 1:c1, 0, 0:HALF], ACT.Copy, scale=etac[:, 0:1]).then_inc(ku_act, 1)
            f(QE, QE, ACT.Exp, scale=-1.0).then_inc(qphi_act, 1)

            def values_gram(r):
                b, s0, cnt = V_RUNS[r]
                act.wait_ge(vgram_done, r + 1)
                f(G[2 * L:3 * L, :, s0:s0 + cnt].rearrange("p j s -> p s j"), PS[0:L, b, 0:cnt * (HALF + 1)].rearrange("p (s j) -> p s j", s=cnt),
                  ACT.Copy).then_inc(vgram_act, 1)

            def keys_gram(r):
                b, c0, cnt = KU_RUNS[r]
                act.wait_ge(gram_done, r + 1)
                for h in range(2):
                    first, end = max(c0, h), min(c0 + cnt, SH - 1 + h)
                    i = f(G[0:2 * L, :, first + h * (S - SH):end + h * (S - SH)].rearrange("p j s -> p s j"),
                          PS[0:2 * L, b, 0:cnt * 2 * (HALF + 1)].rearrange("p (c h j) -> p c h j", c=cnt, h=2)[:, first - c0:end - c0, h, :], ACT.Copy)
                i.then_inc(gram_act, 1)

            act.wait_ge(xrt_done, 4)
            values_gram(0)
            values_gram(1)
            values_gram(2)
            keys_gram(0)
            values_gram(3)
            values_gram(4)
            keys_gram(2)
            keys_gram(4)
            for b, (r0, cnt, behind) in enumerate(LANE_RUNS):
                act.wait_ge(lanes_done, b + 1)
                src = PS[0:W, b, 0:cnt * 3 * L].rearrange("p (j q t) -> p q j t", q=3, t=L)
                if behind:
                    i = f(CC[:, 0:3, r0:r0 + cnt, HALF:L], src[:, :, :, 0:HALF], ACT.Copy)
                else:
                    i = f(CC[:, 0:3, r0:r0 + cnt, :], src, ACT.Copy)
                i.then_inc(lanes_act, 1)
            act.wait_ge(q_ready, 1)
            for ch in range(4):
                act.wait_ge(xnt_done, ch + 1)
                f(xT[:, ch * BANK:(ch + 1) * BANK], bank(ch), ACT.Copy).then_inc(xnt_act, 1)
            act.wait_ge(last_done, 1)
            f(U32, PS[0:L, 7, 0:F], ACT.Copy).then_inc(last_act, 1)
            f(VW, PS[0:L, 7, F:F + D], ACT.Copy).then_inc(last_act, 1)
            f(WSUM, PS[0:L, 7, F + D:F + 2 * D], ACT.Copy).then_inc(last_act, 1)
            act.wait_ge(neg_done, 1)
            f(negm, PS[0:L, 6, 0:1], ACT.Copy, scale=-1.0).then_inc(neg_act, 1)
            act.wait_ge(moe_in, 64)
            for h in range(2):
                for ch in range(4):
                    act.wait_ge(eh_done, 4 * h + ch + 1)
                    f(HT[:, h, ch * BANK:(ch + 1) * BANK], bank((4, 0)[h] + ch), ACT.Relu, bias=b1e[:, h:h + 1]).then_inc(eh_act, 1)
            act.wait_ge(b_ready, 1)
            f(lane[:, SB, :], lane[:, T0, :], ACT.Sqrt).then_inc(sb_ready, 1)
            act.wait_ge(set_once, 17)
            for j in range(L):
                if 20 <= j < 24:
                    ch = j - 20
                    act.wait_ge(eo_done, ch + 1)
                    f(MOE[:, ch * BANK:(ch + 1) * BANK], bank(ch), ACT.Copy).then_inc(eo_act, 1)
                act.wait_ge(ssq_ready, j + 1)
                f(SG[:, j, 2:11].rearrange("p (g k) -> p g k", k=3)[:, :, 0:2], SQ[:, j:j + 1].unsqueeze(2).broadcast_to([W, 3, 2]),
                  ACT.Sqrt).then_inc(sigma_ready, 1)
                act.wait_ge(w_ready, j + 1)
                f(HG[:, j + 1, 1:3], WS[:, j, SCAN - 1:SCAN].broadcast_to([W, 2]), ACT.Sqrt).then_inc(h_ready, 1)
            act.wait_ge(wvo_done, 1)
            f(WVO, PS[:, 7, 0:D], ACT.Copy).then_inc(wvo_act, 1)
            act.wait_ge(mw_done, 1)
            for h0 in (0, F):
                f(MW[h0:h0 + F, :], PS[0:F, 7, 0:D], ACT.Copy).then_inc(mw_act, 1)

            def general():
                with act.Fori(0, T) as t:
                    act.wait_ge(ss_done, t + 1)
                    f(sp_, PS[:, 2, 0:1], ACT.Sqrt).then_inc(s_ready, 1)
                    act.wait_ge(var_s_ready, t + 1)
                    f(sd, var, ACT.Sqrt).then_inc(sd_s_ready, 1)
                act.wait_ge(gmt_done, 1)
                f(MT, PS[:, 0, 0:F], ACT.Copy).then_inc(gmt_act, 1)
                act.wait_ge(gmw_done, 1)
                for h0 in (0, F):
                    f(MW[h0:h0 + F, :], PS[0:F, 7, 0:D], ACT.Copy).then_inc(gmw_act, 1)

            general_path(act, general)

            act.wait_ge(var2_ready, 1)
            f(lnt[:, 1, :], lnt[:, 0, :], ACT.Sqrt).then_inc(sd2_ready, 1)

            def normed(c):
                for n in range(4 * c, 4 * c + 2):
                    f(xn[:, n, :], x[:, n, :], ACT.Identity, scale=lnt[:, 1, n:n + 1], bias=lnt[:, 6, n:n + 1]).then_inc(xn2_act, 1)

            act.wait_ge(shift_ready, 1)
            def transposed(c):
                act.wait_ge(xt2_done, c + 1)
                f(xT[:, c * BANK:(c + 1) * BANK], bank(4 * (c % 2)), ACT.Copy).then_inc(xt2_act, 1)

            def high(c):
                f(xH[:, c * BANK:(c + 1) * BANK], xT[:, c * BANK:(c + 1) * BANK], ACT.Copy).then_inc(xh_act, 1)

            normed(0)
            normed(1)
            transposed(0)
            for c in range(4):
                if c < 2:
                    normed(c + 2)
                if c < 3:
                    transposed(c + 1)
                b = 4 * (c % 2)
                cols = slice(c * BANK, (c + 1) * BANK)
                act.wait_ge(skip_done, c + 1)
                f(qT1[0:ROT, cols], PS[0:ROT, b + 1, :], ACT.Copy).then_inc(skip_act, 1)
                f(kT1[0:ROT, cols], PS[ROT:P, b + 1, :], ACT.Copy).then_inc(skip_act, 1)
                act.wait_ge(xt2_act, c + 1)
                high(c)
            for c in range(4):
                act.wait_ge(v1_done, c + 1)
                f(V1[:, 4 * c:4 * c + 4, :].rearrange("p n d -> p (n d)"), bank((0, 4, 1, 5)[c]), ACT.Copy).then_inc(v1_act, 1)

            def tanh(u):
                act.wait_ge(z_done, u + 1)
                if u == 0:
                    act.wait_ge(scales_ready, 2)
                if u >= 3:
                    act.wait_ge(hA_ready, u - 2)
                f(TH[u % 3], PS[:, GATE_BANK[u], 0:ZC], ACT.Tanh, scale=s1h[:, u % HT4:u % HT4 + 1]).then_inc(tanh_ready, 1)

            def halves(i):
                if i in (1, 5):
                    act.wait_ge(h_in[(i - 1) // 4], 16)
                k = (i - 1) % 4
                wH, wL, w = (q.rearrange("p m e -> p (m e)") for q in (w3H, w3L, w3T)) if i == 0 else (
                    q[:, k, :] for q in ((h1H, h1L, h1S), (h2H, h2L, h2S))[(i - 1) // 4])
                f(wH, w, ACT.Copy).then_inc(w16_ready, 1)
                f(wL, w, ACT.Copy, scale=1.0 / LOW).then_inc(w16_ready, 1)

            def turned_back(t):
                for gi, c, cnt in groups_of(t):
                    if gi % 2 == 0:
                        act.wait_ge(pt_done, gi + 1)
                        f(PT[t % 2][:, c * P:(c + cnt) * P], PS[:, 4, 0:cnt * P], ACT.Copy).then_inc(pt_act, 1)
                        yield

            for t in range(NT + 1):
                copies = turned_back(t - 1) if t else iter(())
                next(copies, None)
                if t < NT:
                    if t >= 2:
                        act.wait_ge(pv_done, t - 1)
                    act.wait_ge(bias_ready, t + 1)
                    for k, (gi, c, cnt) in enumerate(groups_of(t)):
                        if k == 2:
                            next(copies, None)
                        f(Pr[t % 2][:, c * P:(c + cnt) * P], PS[:, k, 0:cnt * P], ACT.Exp,
                          scale=1.0 / D, bias=nbs[:, t:t + 1], accum_out=rsums[:, gi:gi + 1]).then_inc(p_ready, 1)
                for _ in copies:
                    pass
                for u in GATE_TILE[t]:
                    tanh(u)
                if 0 <= t - 4 < 9:
                    halves(t - 4)
            for layer, (s_, done, read) in enumerate(((sh1, g1_done, g1_act), (sh2, g2_done, g2_act))):
                for u in range(4 * HT4):
                    piece = 4 * HT4 * layer + u
                    act.wait_ge(done, u + 1)
                    high = (hBH, hAH)[layer][:, u % HT4, u // HT4 * BANK:(u // HT4 + 1) * BANK]
                    if piece >= 4:
                        act.wait_ge(rest_ready, piece - 3)
                    f(FP[u % 4], bank(u % 8), ACT.Gelu, scale=s_[:, u % HT4:u % HT4 + 1])
                    f(high, bank(u % 8), ACT.Gelu, scale=s_[:, u % HT4:u % HT4 + 1]).then_inc(read, 1)

            def network():
                with act.Fori(0, 4) as c:
                    for m in range(HT4):
                        act.wait_ge(gz_done, c * HT4 + m + 1)
                        f(gT[:, m, :], bank(m), ACT.Tanh, scale=s1h[:, m:m + 1]).then_inc(gt_ready, 1)
                    for i, (b0, dst, s_) in enumerate(((0, gB, sh1), (4, gC, sh2))):
                        for m in range(HT4):
                            act.wait_ge(gh_done, c * 2 * HT4 + i * HT4 + m + 1)
                            f(dst[:, m, :], bank(b0 + m), ACT.Gelu, scale=s_[:, m:m + 1]).then_inc(gb_ready, 1)

            network_general_path(act, network)

        @block.gpsimd
        def _(pool):
            tt = nc.gpsimd.tensor_tensor
            o = Order(pool, pool_order)
            nc.gpsimd.memset(VX[:, :, HALF:HALF + 1], 1.0).then_inc(set_once, 1)
            nc.gpsimd.memset(VT[:, T:T + HALF], 0.0).then_inc(set_once, 1)
            nc.gpsimd.memset(KU[:, SH - 1, :, HALF:L], 0.0).then_inc(set_once, 1)
            nc.gpsimd.memset(SG, 0.0).then_inc(set_once, 1)
            nc.gpsimd.memset(HG, 0.0).then_inc(set_once, 1)
            nc.gpsimd.memset(CC[:, 3, :, L - 1:L], 0.0).then_inc(set_once, 1)
            nc.gpsimd.memset(GG[:, HALF - 1:L, 0:HALF], 0.0).then_inc(set_once, 1)
            nc.gpsimd.memset(STf, 0.0).then_inc(set_once, 1)
            nc.gpsimd.memset(EC[:, 0:1], 1.0 + EPS_LN).then_inc(set_once, 1)
            nc.gpsimd.memset(EC[:, 1:2], -EPS_LN).then_inc(set_once, 1)
            pool.wait_ge(set_once, 14)
            nc.gpsimd.memset(SG[:, :, SCAN - 1:SCAN], 1.0).then_inc(set_once, 1)
            nc.gpsimd.memset(ST[:, R_E, 0:1], EPS_LN).then_inc(set_once, 1)
            nc.gpsimd.memset(ST[:, R_X, 1:2], -EPS_LN).then_inc(set_once, 1)
            for ch in range(4):
                pool.wait_ge(vt_ready, ch + 1)
                nc.gpsimd.tensor_copy(VX[:, 32 * ch:32 * ch + 32, 0:HALF], VT[:, ch * BANK:(ch + 1) * BANK].rearrange("p (s i) -> p s i", i=HALF)).then_inc(vx_ready, 1)
            pool.wait_ge(qphi_act, 2)
            tt(QT, QT, QE, ALU.add).then_inc(q_ready, 1)
            pool.wait_ge(rows_set, 3)
            for dst, a_, b_ in ((tmpC, M2, KD), (tmpD, MR, FD)):
                for js, ts in BLOCKS:
                    x_, y_ = lane[:, a_, js], lane[:, b_, ts]
                    sh = [W, js.stop - js.start, ts.stop - ts.start]
                    tt(dst[:, js, ts], x_.unsqueeze(2).broadcast_to(sh), y_.unsqueeze(1).broadcast_to(sh), ALU.mult).then_inc(outer_ready, 1)
            pool.wait_ge(vc_ready, 2)
            for j in range(L - 2):
                n = L - 2 - j
                tt(OJ[j], CC[:, 0, j + 1, j + 2:L].unsqueeze(1).broadcast_to([W, n, n]), VC[:, j, j + 1:L - 1].unsqueeze(2).broadcast_to([W, n, n]),
                   ALU.mult).then_inc(oj_ready, 1)
            xf, xnf = x[:, :, :].rearrange("p n d -> p (n d)"), xn[:, :, :].rearrange("p n d -> p (n d)")
            pool.wait_ge(xn_ready, NT)
            n = o.did(tt(xf, xf, xnf, ALU.add))
            pool.wait_ge(eo_act, 4)
            o.need(n)
            n = o.did(tt(xf, xf, MOE, ALU.add))
            o.need(n)
            tt(x[:, :, :], x[:, :, :], b2e[:, :].unsqueeze(1).broadcast_to([P, NT, D]), ALU.add).then_inc(xres_ready, 1)

            o2 = Order(pool, pool2_order)

            def low_part(low, value, high, rest, cols):
                o2.need(o2.did(tt(rest, value, high, ALU.subtract)))
                return tt(low, rest, low_scale.broadcast_to([P, cols]), ALU.mult)

            o2.need(o2.did(nc.gpsimd.memset(low_scale, LOW)))
            pool.wait_ge(small_in, 16 * 13)
            pool.wait_ge(x1_ready, 4)
            for wH, wL, w in ((w1H, w1L, w1T), (w2H, w2L, w2T)):
                nc.gpsimd.tensor_copy(wH, w).then_inc(w16_ready, 1)
                nc.gpsimd.tensor_scalar(wL, w, 1.0 / LOW, None, ALU.mult).then_inc(w16_ready, 1)
            for c in range(4):
                cols = slice(c * BANK, (c + 1) * BANK)
                pool.wait_ge(rope_dve, 2 * c + 2)
                (pool.wait_ge(xl_ready, c) if c else pool.wait_ge(w16_ready, 4))
                tt(kT1[ROT:P, cols], TURN[c % 2][ROT:P, 0, :], TURN[c % 2][ROT:P, 1, :], ALU.add).then_inc(turned_pool, 1)
                pool.wait_ge(xh_act, c + 1)
                pool.wait_ge(turned_pool, c + 1)
                low_part(xL[:, cols], xT[:, cols], xH[:, cols], xd, BANK).then_inc(xl_ready, 1)

            def gate_parts(u):
                m, c = u % HT4, u // HT4
                cols = slice(c * ZC, (c + 1) * ZC)
                pool.wait_ge(gate_high, u + 1)
                if u:
                    pool.wait_ge(gate_low, u)
                low_part(hAL[:, m, cols], ZA[u % 3], hAH[:, m, cols], zd, ZC).then_inc(gate_low, 1)

            def weights(i):
                if i in (3, 7):
                    pool.wait_ge(h_in[(i - 3) // 4], 16)
                k = (i - 3) % 4
                w = (w1T, w2T, w3T.rearrange("p m e -> p (m e)"))[i] if i < 3 else (h1S, h2S)[(i - 3) // 4][:, k, :]
                if i == 0:
                    pool.wait_ge(turned_dve, 4)
                    pool.wait_ge(turned_pool, 4)
                    pool.wait_ge(xl_ready, 4)
                if i >= 2:
                    pool.wait_ge(tern_ready, i - 1)
                wc = WC[i % 2]
                o2.need(o2.did(tt(wc, w, w, ALU.mult)))
                o2.need(o2.did(tt(wc, wc, w, ALU.mult)))
                tt(wc, wc, w, ALU.subtract).then_inc(wc_ready, 1)

            for u in range(NU):
                gate_parts(u)
                if u % 2 == 1 and u // 2 < 11:
                    weights(u // 2)

            def network():
                pool.wait_ge(y_done, 4)
                pool.dma_start(h1G, a["h1_T"]).then_inc(gw_in, 16)
                pool.dma_start(h2G, a["h2_T"]).then_inc(gw_in, 16)
                pool.wait_ge(gy_read, 4)
                pool.wait_ge(out_sem, 64)
                pool.dma_start(out_dram, fin).then_inc(out_sem, 16)
                pool.wait_ge(out_sem, 80)

            network_general_path(pool, network)

        @block.vector
        def _(dve):
            v = nc.vector
            o = Order(dve, dve_order)
            did, need = o.did, o.need
            R = [lane[:, i, :] for i in range(12)]

            def last():
                need(o.n)

            def statistics(h):
                for n in range(8 * h, 8 * h + 8):
                    if n % 4 == 0:
                        dve.wait_ge(x_in[n // 4], 16)
                    did(v.bn_stats(st[:, n, :], x[:, n, :]))
                last()
                for n in range(8 * h, 8 * h + 8):
                    did(v.bn_aggr(mv[:, n, :], st[:, n, :]))
                last()
                did(v.tensor_scalar(lnt[:, 0, 8 * h:8 * h + 8], mv[:, 8 * h:8 * h + 8, 1], EPS_LN, None, ALU.add))
                v.tensor_scalar(lnt[:, 1, 8 * h:8 * h + 8], mv[:, 8 * h:8 * h + 8, 1], 1.0 + EPS_RMS, EPS_RMS * EPS_LN, ALU.mult, ALU.add).then_inc(var_ready, 1)

            def rms_normed(h):
                dve.wait_ge(sd_ready, h + 1)
                did(v.reciprocal(lnt[:, 0:2, 8 * h:8 * h + 8], lnt[:, 0:2, 8 * h:8 * h + 8]))
                last()
                for n in range(8 * h, 8 * h + 8):
                    v.tensor_scalar(XR[:, n, :], x[:, n, :], mv[:, n, 0:1], lnt[:, 1, n:n + 1], ALU.subtract, ALU.mult).then_inc(xr_ready, 1)

            v.memset(UX[0:F, :, 1, :], 0.0).then_inc(set_once, 1)
            v.memset(UX[F:P, :, 0, :], 0.0).then_inc(set_once, 1)
            v.memset(UX[0:F, :, 0, HALF:HALF + 1], 1.0).then_inc(set_once, 1)
            v.memset(UX[F:P, :, 1, HALF:HALF + 1], 1.0).then_inc(set_once, 1)
            statistics(0)
            statistics(1)
            rms_normed(0)
            rms_normed(1)
            dve.wait_ge(early_in, 16 * 4)
            for b in range(2, 4):
                dve.wait_ge(xrt_done, b + 1)
                v.tensor_scalar(xrT[:, b * BANK:(b + 1) * BANK], bank(b), normw[:, 0:1], None, ALU.mult).then_inc(xrt_dve, 1)
            dve.wait_ge(eta_in, 32)
            did(v.scalar_tensor_tensor(out=etac[:, :], in0=etac[:, :], scalar=-1.0, in1=etac[:, :], op0=ALU.mult, op1=ALU.max))
            last()
            v.tensor_scalar(etac[:, :], etac[:, :], ETA_MIN, None, ALU.max).then_inc(eta_set, 1)
            dve.wait_ge(eta_set, 1)
            dve.wait_ge(set_once, 17)

            def values(ch):
                dve.wait_ge(v_done, ch + 1)
                v.tensor_copy(VT[:, ch * BANK:(ch + 1) * BANK], bank(ch)).then_inc(vt_ready, 1)

            def keys(h):
                c0, c1, d0 = ((0, K2, 0), (K2, SH, K2 - 1))[h]
                z = PS[:, 4:7, :].rearrange("p b c -> p (b c)")[:, c0 * HALF:c1 * HALF].rearrange("p (c i) -> p c i", i=HALF)
                dve.wait_ge(kphi_act, h + 1)
                v.scalar_tensor_tensor(out=KU[:, c0:c1, 0, 0:HALF], in0=z, scalar=0.0, in1=KE[:, c0 * HALF:c1 * HALF].rearrange("p (c i) -> p c i", i=HALF),
                                       op0=ALU.max, op1=ALU.add).then_inc(k_ready, 1)
                dve.wait_ge(k_ready, h + 1)
                v.tensor_copy(KU[:, d0:c1 - 1, 0, HALF:L], KU[:, d0 + 1:c1, 0, 0:HALF]).then_inc(ku_ready, 1)
                for hf in range(2):
                    h0 = slice(F * hf, F * hf + F)
                    v.tensor_scalar(UX[h0, c0:c1, hf, 0:HALF], KU[h0, c0:c1, 0, 0:HALF], etac[h0, 0:1], None, ALU.mult).then_inc(ku_ready, 1)

            values(0)
            values(1)
            keys(0)
            values(2)
            values(3)
            keys(1)
            for n in range(NT):
                v.tensor_scalar(xn[:, n, :], x[:, n, :], mv[:, n, 0:1], lnt[:, 0, n:n + 1], ALU.subtract, ALU.mult).then_inc(xn_ready, 1)
            dve.wait_ge(xrt_done, 4)
            for r in (1, 3):
                b, c0_, cnt = KU_RUNS[r]
                dve.wait_ge(gram_done, r + 1)
                for h in range(2):
                    s0 = c0_ + h * (S - SH)
                    i = v.tensor_copy(G[0:2 * L, :, s0:s0 + cnt].rearrange("p j s -> p s j"),
                                      PS[0:2 * L, b, 0:cnt * 2 * (HALF + 1)].rearrange("p (c h j) -> p c h j", c=cnt, h=2)[:, :, h, :])
                i.then_inc(gram_dve, 1)

            aT, bT, V = (CC[:, q, 1:L + 1, :] for q in range(3))
            KAP, FUS, Dv = (CC[:, q, 0, :] for q in range(3))

            def diagonal(m, first=0, right=0):
                return m.rearrange("p j t -> p (j t)")[:, first * (L + 1) + right:L * L - right * L:L + 1]

            def rows_of(r, js, ts):
                return R[r][:, js].unsqueeze(2).broadcast_to([W, js.stop - js.start, ts.stop - ts.start])

            def columns_of(r, js, ts):
                return r[:, ts].unsqueeze(1).broadcast_to([W, js.stop - js.start, ts.stop - ts.start])

            dve.wait_ge(set_once, 17)
            dve.wait_ge(lanes_act, 8)
            did(v.tensor_scalar(R[VB], Dv, 2.0 / D, None, ALU.mult))
            did(v.tensor_tensor(R[KD], KAP, Dv, ALU.mult))
            did(v.tensor_tensor(R[FD], FUS, Dv, ALU.mult))
            did(v.tensor_copy(R[DVS], Dv))
            did(v.tensor_copy(ST[:, R_N, 0:L - 1], diagonal(V, 1)))
            last()
            v.tensor_scalar(R[M2], R[FD], 2.0 / N, None, ALU.mult).then_inc(rows_set, 1)
            v.tensor_scalar(R[MR], R[FD], -2.0 / N / N, None, ALU.mult).then_inc(rows_set, 1)
            v.tensor_scalar(R[MM], R[FD], 1.0 / N, None, ALU.mult).then_inc(mrow_ready, 1)
            did(v.tensor_scalar(R[MZ], R[FD], float(np.sqrt(2.0 * D)) / N, None, ALU.mult))
            for js, ts in BLOCKS:
                did(v.tensor_tensor(tmpA[:, js, ts], rows_of(DVS, js, ts), columns_of(R[VB], js, ts), ALU.mult))
            last()
            for js, ts in BLOCKS:
                v.scalar_tensor_tensor(out=VC[:, js, ts], in0=V[:, js, ts], scalar=2.0, in1=tmpA[:, js, ts], op0=ALU.mult, op1=ALU.subtract).then_inc(vc_ready, 1)
            v.tensor_scalar(R[DVS], R[DVS], float(np.sqrt(2.0 / D)), None, ALU.mult).then_inc(rows_set, 1)
            did(v.tensor_tensor(R[T0], diagonal(bT), diagonal(V), ALU.mult))
            did(v.tensor_tensor(R[T1], R[FD], R[FD], ALU.mult))
            last()
            did(v.scalar_tensor_tensor(out=R[T0], in0=R[T1], scalar=-1.0 / N, in1=R[T0], op0=ALU.mult, op1=ALU.add))
            dve.wait_ge(vc_ready, 2)
            did(v.tensor_scalar(R[VJJ], diagonal(VC), 0.5, None, ALU.mult))
            last()
            did(v.tensor_scalar(ST[:, R_B, 0:L], R[T0], 1.0 / N, None, ALU.mult))
            last()
            v.tensor_scalar(R[T0], R[T0], 1.0 / N, 0.0, ALU.mult, ALU.max).then_inc(b_ready, 1)
            dve.wait_ge(rows_set, 3)
            for js, ts in BLOCKS:
                did(v.tensor_tensor(tmpA[:, js, ts], aT[:, js, ts], rows_of(DVS, js, ts), ALU.mult))
                did(v.tensor_tensor(tmpB[:, js, ts], rows_of(MZ, js, ts), columns_of(KAP, js, ts), ALU.mult))
            last()
            C0, C1, C2 = (CC[:, q, 1:L + 1, :] for q in range(3, 6))
            for js, ts in BLOCKS:
                did(v.tensor_tensor(C2[:, js, ts], tmpA[:, js, ts], tmpB[:, js, ts], ALU.subtract))
            last()
            for js, ts in BLOCKS:
                did(v.tensor_tensor(tmpA[:, js, ts], aT[:, js, ts], rows_of(VJJ, js, ts), ALU.mult))
                did(v.scalar_tensor_tensor(out=tmpB[:, js, ts], in0=C2[:, js, ts], scalar=0.5, in1=C2[:, js, ts], op0=ALU.mult, op1=ALU.mult))
            last()
            for js, ts in BLOCKS:
                did(v.tensor_tensor(tmpA[:, js, ts], tmpA[:, js, ts], aT[:, js, ts], ALU.mult))
            last()
            for js, ts in BLOCKS:
                did(v.tensor_tensor(GG[:, js, ts], tmpA[:, js, ts], tmpB[:, js, ts], ALU.add))
            last()
            for js, ts in BLOCKS:
                did(v.tensor_tensor(tmpA[:, js, ts], aT[:, js, ts], V[:, js, ts], ALU.mult))
                did(v.tensor_tensor(tmpB[:, js, ts], bT[:, js, ts], V[:, js, ts], ALU.mult))
            did(v.tensor_copy(ST[:, R_G, 0:L - 1], diagonal(GG, 0, 1)))
            last()
            dve.wait_ge(outer_ready, 4)
            for js, ts in BLOCKS:
                t1 = slice(max(ts.start, 1), L)
                did(v.scalar_tensor_tensor(out=C0[:, js, t1.start - 1:L - 1], in0=tmpA[:, js, t1], scalar=-2.0, in1=tmpC[:, js, t1], op0=ALU.mult, op1=ALU.add))
            for js, ts in BLOCKS:
                did(v.scalar_tensor_tensor(out=C1[:, js, ts], in0=tmpB[:, js, ts], scalar=2.0 / N, in1=tmpD[:, js, ts], op0=ALU.mult, op1=ALU.add))
            last()
            did(v.tensor_copy(ST[:, R_CD, 0:L - 1], diagonal(C0)[:, 0:L - 1]))
            v.tensor_copy(SQ[:, 0:1], V[:, 0, 0:1]).then_inc(ssq_ready, 1)
            last()

            added = formed = o.n
            for j in range(L):
                sg = SG[:, j, 2:3]
                n = L - 2 - j
                need(max(added, formed))
                dve.wait_ge(sigma_ready, j + 1)
                v.tensor_tensor_scan(WS[:, j, :], SG[:, j, :], ST[:, R_N:R_X + 1, j], 0.0, ALU.mult, ALU.add).then_inc(w_ready, 1)
                if j == L - 1:
                    break
                if n > 0:
                    dve.wait_ge(oj_ready, j + 1)
                    nxt = ST[:, j + 1:j + 2, j + 2:L]
                    did(v.scalar_tensor_tensor(out=nxt, in0=OJ[j][:, 0:1, :], scalar=sg, in1=nxt, op0=ALU.mult, op1=ALU.add))
                rows = ST[:, R_D:R_Z + 1:R_R - R_D, j + 1:L]
                added = did(v.scalar_tensor_tensor(out=rows, in0=CC[:, 3:6, j + 1, j + 1:L], scalar=sg, in1=rows, op0=ALU.mult, op1=ALU.add))
                if n > 0:
                    u = did(v.scalar_tensor_tensor(out=U[:, 0:n], in0=GG[:, j, j + 2:L], scalar=sg, in1=ST[:, R_T, j + 1:L - 1], op0=ALU.mult, op1=ALU.add))
                dve.wait_ge(w_ready, j + 1)
                e0 = R_E * RW + j + 1
                did(v.tensor_tensor(STf[:, e0:e0 + RW + 2:RW + 1], WS[:, j, SCAN - 1:SCAN].broadcast_to([W, 2]), EC, ALU.mult))
                if n > 0:
                    need(added)
                    t1 = did(v.tensor_tensor(P2[:, :, 0:n], ST[:, j + 1:R_Z + 1:R_Z - j - 1, j + 2:L], CC[:, 0:6:5, j + 2, j + 2:L], ALU.mult))
                dve.wait_ge(h_ready, j + 1)
                s3_ = did(v.tensor_tensor_scan(S3[:, j, :], HG[:, j + 1, :], WS[:, j, 0:7:3], 0.0, ALU.mult, ALU.add))
                if n > 0:
                    need(u)
                    formed = did(v.scalar_tensor_tensor(out=ST[:, R_Q, j + 1:L - 1], in0=U[:, 0:n], scalar=sg, in1=ST[:, R_Q, j + 1:L - 1],
                                                        op0=ALU.mult, op1=ALU.add))
                need(s3_)
                v.tensor_scalar(SQ[:, j + 1:j + 2], S3[:, j, 2:3], 0.0, None, ALU.max).then_inc(ssq_ready, 1)
                if n > 0:
                    need(t1)
                    formed = did(v.tensor_tensor(ST[:, R_T, j + 1:L - 1], P2[:, 0, 0:n], P2[:, 1, 0:n], ALU.add))
                if n > 1:
                    later = ST[:, j + 2:L - 1, j + 2:L]
                    added = did(v.scalar_tensor_tensor(out=later, in0=OJ[j][:, 1:, :], scalar=sg, in1=later, op0=ALU.mult, op1=ALU.add))

            dve.wait_ge(h_ready, L)
            did(v.reciprocal(rh, HG[:, HALF:L + 1:HALF, 1]))
            last()
            v.tensor_scalar(wts, SG[:, :, 2], rh[:, 1:2], None, ALU.mult).then_inc(wts_ready, 1)
            dve.wait_ge(sb_ready, 1)
            v.scalar_tensor_tensor(out=c0, in0=SG[:, 0:HALF, 2], scalar=rh[:, 0:1], in1=R[SB][:, 0:HALF], op0=ALU.mult, op1=ALU.mult).then_inc(c0_ready, 1)
            dve.wait_ge(wts_ready, 1)
            cc = did(v.tensor_tensor(c1, wts, R[SB], ALU.mult))
            dve.wait_ge(wcol_done, 1)
            dve.wait_ge(neg_act, 1)
            dve.wait_ge(last_act, 3)
            did(v.tensor_copy(wcol, PS[0:L, 5, 0:1]))
            last()
            v.tensor_scalar(UW, U32, wcol, None, ALU.mult).then_inc(uw_ready, 1)
            v.tensor_scalar(WM, con[0:L, C_ONES:C_ONES + F], wcol, negm, ALU.mult, ALU.mult).then_inc(uw_ready, 1)
            need(cc)
            dve.wait_ge(shift_done, 1)
            did(v.tensor_tensor(c1[0:W - 1, HALF:L], c1[0:W - 1, HALF:L], PS[0:W - 1, 6, 0:HALF], ALU.subtract))
            last()
            did(v.tensor_reduce(bound, c1, AX.X, ALU.add, apply_absolute_value=True))
            last()
            v.tensor_scalar(agree, bound, TOLERANCE, None, ALU.is_le).then_inc(agree_ready, 1)
            dve.wait_ge(count_done, 1)
            v.tensor_scalar(flag[:, :], PS[0:1, 4, 1:2], W - 1.5, None, ALU.is_ge).then_inc(flag_set, 1)

            def general():
                lo = Order(dve, loop_order)
                lo.did(v.tensor_copy(KF[:, 0:T // 2].rearrange("p (c i) -> p c i", i=HALF), KU[0:F, 0:S // 2, 0, 0:HALF]))
                lo.did(v.tensor_copy(KF[:, T // 2:T].rearrange("p (c i) -> p c i", i=HALF), KU[F:P, 1:SH, 0, 0:HALF]))
                v.memset(MS, 0.0).then_inc(state_ready, 1)
                lo.need(lo.n)
                n0 = lo.n
                per = 8
                with dve.Fori(0, T) as t:
                    lo.offset = t * per
                    dve.wait_ge(state_ready, t + 1)
                    lo.did(v.tensor_copy(vt, VT[:, bass.ds(t, 1)]))
                    n = lo.did(v.tensor_copy(kt, KF[:, bass.ds(t, 1)]))
                    lo.need(n)
                    v.tensor_scalar(DIAG, ident, vt, None, ALU.mult).then_inc(token_ready, 1)
                    dve.wait_ge(pred_done, t + 1)
                    n = lo.did(v.tensor_tensor(dv_, vt, PS[:, 0, 0:1], ALU.subtract))
                    lo.need(n)
                    v.tensor_tensor(d2, dv_, dv_, ALU.mult).then_inc(d2_ready, 1)
                    dve.wait_ge(s_ready, t + 1)
                    n = lo.did(v.scalar_tensor_tensor(out=su, in0=kt, scalar=sp_[0:F, :], in1=etac[0:F, :], op0=ALU.mult, op1=ALU.mult))
                    lo.need(n)
                    n = lo.did(v.scalar_tensor_tensor(out=MS, in0=PS[0:F, 1, 0:D], scalar=su, in1=MS, op0=ALU.mult, op1=ALU.add))
                    lo.need(n)
                    v.tensor_reduce(rs, MS, AX.X, ALU.add).then_inc(rows_ready, 1)
                    dve.wait_ge(sum_done, t + 1)
                    n = lo.did(v.tensor_scalar(mean, PS[0:F, 3, 0:1], 1.0 / N, None, ALU.mult))
                    lo.need(n)
                    n = lo.did(v.tensor_scalar(MS, MS, mean, None, ALU.subtract))
                    lo.need(n)
                    v.tensor_tensor_reduce(out=MQ, in0=MS, in1=MS, scale=1.0, scalar=0.0, op0=ALU.mult, op1=ALU.add, accum_out=r2).then_inc(sq_rows_ready, 1)
                    dve.wait_ge(sq_done, t + 1)
                    v.tensor_scalar(var, PS[0:F, 3, 1:2], 1.0 / N, EPS_LN, ALU.mult, ALU.add).then_inc(var_s_ready, 1)
                    dve.wait_ge(sd_s_ready, t + 1)
                    n = lo.did(v.reciprocal(rinv_, sd))
                    lo.need(n)
                    v.tensor_scalar(MS, MS, rinv_, None, ALU.mult).then_inc(state_ready, 1)
                    assert lo.n == n0 + per
                dve.wait_ge(state_ready, T + 1)

            general_path(dve, general)
            o2 = Order(dve, dve_order2)

            did, need = o2.did, o2.need
            dve.wait_ge(xres_ready, 1)
            for b in range(4):
                xb = x[:, 4 * b:4 * b + 4, :].rearrange("p n d -> p (n d)")
                dve.wait_ge(ao_done, b + 1)
                v.tensor_tensor(xb, xb, bank(4 + b), ALU.add).then_inc(x1_ready, 1)
                if b:
                    for n in range(4 * b - 4, 4 * b):
                        i = did(v.bn_aggr(mv[:, n, :], st[:, n, :]))
                dve.wait_ge(x1_ready, b + 1)
                for n in range(4 * b, 4 * b + 4):
                    i = did(v.bn_stats(st[:, n, :], x[:, n, :]))
                need(i)
            for n in range(12, NT):
                i = did(v.bn_aggr(mv[:, n, :], st[:, n, :]))
            need(i)
            v.tensor_scalar(lnt[:, 0, :], mv[:, :, 1], EPS_LN, None, ALU.add).then_inc(var2_ready, 1)
            dve.wait_ge(small_in, 16 * 13)
            v.tensor_scalar(s1h, s1, 0.5, None, ALU.mult).then_inc(scales_ready, 1)
            v.scalar_tensor_tensor(out=s12, in0=s1, scalar=0.5, in1=s2, op0=ALU.mult, op1=ALU.mult).then_inc(scales_ready, 1)
            dve.wait_ge(sd2_ready, 1)
            need(did(v.reciprocal(lnt[:, 1, :], lnt[:, 1, :])))
            v.scalar_tensor_tensor(out=lnt[:, 6, :], in0=mv[:, :, 0], scalar=-1.0, in1=lnt[:, 1, :], op0=ALU.mult, op1=ALU.mult).then_inc(shift_ready, 1)

            def normed(c):
                for n in range(4 * c + 2, 4 * c + 4):
                    v.tensor_scalar(xn[:, n, :], x[:, n, :], mv[:, n, 0:1], lnt[:, 1, n:n + 1], ALU.subtract, ALU.mult).then_inc(xn2_dve, 1)

            normed(0)
            normed(1)
            dve.wait_ge(tab_in, 32)
            for c in range(4):
                b = 4 * (c % 2)
                cols = slice(c * BANK, (c + 1) * BANK)
                if c >= 2:
                    dve.wait_ge(turned_pool, c - 1)
                    dve.wait_ge(turned_dve, c - 1)
                dve.wait_ge(turn_done, 2 * c + 1)
                v.tensor_tensor(TURN[c % 2][:, 0, :], bank(b + 2), cosT[:, cols], ALU.mult).then_inc(rope_dve, 1)
                dve.wait_ge(turn_done, 2 * c + 2)
                v.tensor_tensor(TURN[c % 2][:, 1, :], bank(b + 3), sinT[:, cols], ALU.mult).then_inc(rope_dve, 1)
                if c < 2:
                    normed(c + 2)
                dve.wait_ge(rope_dve, 2 * c + 2)
                v.tensor_tensor(qT1[ROT:P, cols], TURN[c % 2][0:ROT, 0, :], TURN[c % 2][0:ROT, 1, :], ALU.add).then_inc(turned_dve, 1)

            def gate(u):
                m, c = u % HT4, u // HT4
                dve.wait_ge(tanh_ready, u + 1)
                if u:
                    dve.wait_ge(hA_ready, u)
                if u >= 3:
                    dve.wait_ge(gate_low, u - 2)
                need(did(v.scalar_tensor_tensor(out=ZG, in0=TH[u % 3], scalar=1.0, in1=PS[:, GATE_BANK[u], 0:ZC], op0=ALU.add, op1=ALU.mult)))
                v.scalar_tensor_tensor(out=ZA[u % 3], in0=PS[:, GATE_BANK[u], ZC:2 * ZC], scalar=s12[:, m:m + 1], in1=ZG,
                                       op0=ALU.mult, op1=ALU.mult).then_inc(hA_ready, 1)
                dve.wait_ge(hA_ready, u + 1)
                v.tensor_copy(hAH[:, m, c * ZC:(c + 1) * ZC], ZA[u % 3]).then_inc(gate_high, 1)
                i = (u - 5) // 2
                if u % 2 == 1 and 0 <= i < 11:
                    dve.wait_ge(wc_ready, i + 1)
                    v.tensor_reduce(tern[:, i:i + 1], WC[i % 2], AX.X, ALU.max, apply_absolute_value=True).then_inc(tern_ready, 1)

            def turned_back(t):
                for gi, c, cnt in groups_of(t):
                    if gi % 2 == 1:
                        dve.wait_ge(pt_done, gi + 1)
                        v.tensor_copy(PT[t % 2][:, c * P:(c + cnt) * P], PS[:, 5, 0:cnt * P]).then_inc(pt_dve, 1)
                        yield

            for t in range(NT + 1):
                if t < NT:
                    groups = groups_of(t)
                    for k, (gi, c, cnt) in enumerate(groups):
                        dve.wait_ge(s_done, gi + 1)
                        i = did(v.tensor_reduce(mxb[:, gi:gi + 1], PS[:, k, 0:cnt * P], AX.X, ALU.max))
                    need(i)
                    g0, g1 = groups[0][0], groups[-1][0]
                    top = mxb[:, g0:g1 + 1]
                    if g1 > g0:
                        need(did(v.tensor_reduce(mxs[:, t:t + 1], top, AX.X, ALU.max)))
                        top = mxs[:, t:t + 1]
                    v.tensor_scalar(nbs[:, t:t + 1], top, -1.0 / D, None, ALU.mult).then_inc(bias_ready, 1)
                copies = turned_back(t - 1) if t else iter(())
                for _ in copies:
                    pass
                for u in GATE_TILE[t][0:1]:
                    gate(u)
                if t == NT - 3:
                    need(did(v.tensor_tensor(s12a, s1, s2, ALU.mult)))
                    v.tensor_reduce(sums[:, 0:1], s12a, AX.X, ALU.add, apply_absolute_value=True).then_inc(sums_ready, 1)
                    v.tensor_reduce(sums[:, 1:2], sh1, AX.X, ALU.add, apply_absolute_value=True).then_inc(sums_ready, 1)
                if t == NT - 1:
                    dve.wait_ge(sums_done, 1)
                    need(did(v.tensor_scalar(reach[:, 0:1], PS[:, 6, 0:1], float(D * D), None, ALU.mult)))
                    i = did(v.tensor_tensor(reach[:, 1:2], reach[:, 0:1], PS[:, 6, 1:2], ALU.mult))
                    did(v.tensor_scalar(ends[:, 0:HT4], s12a, float(D * D), None, ALU.mult))
                    did(v.tensor_scalar(ends[:, HT4:2 * HT4], sh1, reach[:, 0:1], None, ALU.mult))
                    need(i)
                    did(v.tensor_scalar(ends[:, 2 * HT4:3 * HT4], sh2, reach[:, 1:2], None, ALU.mult))
                    dve.wait_ge(tern_ready, 11)
                    i = did(v.tensor_reduce(tmax, tern, AX.X, ALU.max))
                    need(i)
                    need(did(v.tensor_reduce(top_, ends, AX.X, ALU.max, apply_absolute_value=True)))
                    need(did(v.tensor_scalar(ends_ok, top_, LIMIT, None, ALU.is_le)))
                    v.scalar_tensor_tensor(out=fits, in0=tmax, scalar=0.0, in1=ends_ok, op0=ALU.is_le, op1=ALU.mult).then_inc(fits_ready, 1)
                if t:
                    g0, g1 = groups_of(t - 1)[0][0], groups_of(t - 1)[-1][0]
                    dve.wait_ge(p_ready, g1 + 1)
                    total = rsums[:, g0:g0 + 1]
                    if g1 > g0:
                        total = rsum[:, t - 1:t]
                        need(did(v.tensor_reduce(total, rsums[:, g0:g1 + 1], AX.X, ALU.add)))
                    need(did(v.reciprocal(rinv[:, t - 1:t], total)))
                    dve.wait_ge(pv_done, t)
                    v.scalar_tensor_tensor(out=x[:, t - 1, :], in0=PS[:, 7, ((t - 1) % 4) * D:((t - 1) % 4 + 1) * D], scalar=rinv[:, t - 1:t],
                                           in1=x[:, t - 1, :], op0=ALU.mult, op1=ALU.add).then_inc(pv_read, 1)
                for u in GATE_TILE[t][1:]:
                    gate(u)
            dve.wait_ge(fits_done, 1)
            v.tensor_scalar(fits_flag[:, :], PS[0:1, 6, 2:3], P - 0.5, None, ALU.is_ge).then_inc(fits_set, 1)
            for piece in range(2 * 4 * HT4):
                ch, m = piece // HT4 % 4, piece % HT4
                high = (hBH, hAH)[piece // (4 * HT4)][:, m, ch * BANK:(ch + 1) * BANK]
                dve.wait_ge((g1_act, g2_act)[piece // (4 * HT4)], piece % (4 * HT4) + 1)
                if piece >= 4:
                    dve.wait_ge(low_ready, piece - 3)
                v.tensor_tensor(RP[m], FP[m], high, ALU.subtract).then_inc(rest_ready, 1)
                dve.wait_ge(rest_ready, piece + 1)
                v.tensor_scalar((hBL, hAL)[piece // (4 * HT4)][:, m, ch * BANK:(ch + 1) * BANK], RP[m], LOW, None, ALU.mult).then_inc(low_ready, 1)
            for b in range(4):
                dve.wait_ge(y_done, b + 1)
                w = ysc[:, b * BANK:(b + 1) * BANK]
                need(did(v.tensor_tensor(w.rearrange("p (n e) -> p n e", n=4), bank(b).rearrange("p (n e) -> p n e", n=4),
                                         s3.unsqueeze(1).broadcast_to([P, 4, D]), ALU.mult)))
                xb = x[:, 4 * b:4 * b + 4, :].rearrange("p n d -> p (n d)")
                v.tensor_tensor(fin[:, 4 * b:4 * b + 4, :].rearrange("p n d -> p (n d)"), xb, w, ALU.add).then_inc(out_ready, 1)

            def network():
                xf, ff = x[:, :, :].rearrange("p n d -> p (n d)"), fin[:, :, :].rearrange("p n d -> p (n d)")
                dve.wait_ge(out_sem, 64)
                with dve.Fori(0, 4) as c:
                    for m in range(HT4):
                        dve.wait_ge(gt_ready, c * HT4 + m + 1)
                        v.scalar_tensor_tensor(out=gz[:, m, :], in0=gT[:, m, :], scalar=1.0, in1=bank(m), op0=ALU.add, op1=ALU.mult).then_inc(net_order, 1)
                        dve.wait_ge(net_order, c * (HT4 + 1) + m + 1)
                        v.scalar_tensor_tensor(out=gA[:, m, :], in0=bank(4 + m), scalar=s12[:, m:m + 1], in1=gz[:, m, :],
                                               op0=ALU.mult, op1=ALU.mult).then_inc(ga_ready, 1)
                    dve.wait_ge(gy_done, c + 1)
                    v.tensor_tensor(ysc[:, 0:BANK].rearrange("p (n e) -> p n e", n=4), bank(0).rearrange("p (n e) -> p n e", n=4),
                                    s3.unsqueeze(1).broadcast_to([P, 4, D]), ALU.mult).then_inc(net_order, 1)
                    dve.wait_ge(net_order, c * (HT4 + 1) + HT4 + 1)
                    v.tensor_tensor(ff[:, bass.ds(c * BANK, BANK)], xf[:, bass.ds(c * BANK, BANK)], ysc[:, 0:BANK], ALU.add).then_inc(gy_read, 1)

            network_general_path(dve, network)


INPUTS = ["L0_attn_x", "L0_attn_norm_weight", "L0_attn_eta", "L0_ffn_W1", "L0_ffn_W2", "L0_ffn_b2", "L1_attn_wo", "L1_ffn_w3_s"]
TRANSPOSED = {"WkT": "L0_attn_Wk", "WvT": "L0_attn_Wv", "WqT": "L0_attn_Wq", "WoutT": "L0_attn_Wout", "w1_T": "L1_ffn_w1_w", "w2_T": "L1_ffn_w2_w"}
BY_PARTITION = {"s1": "L1_ffn_w1_s", "s2": "L1_ffn_w2_s", "sh1": "L1_ffn_h1_s", "sh2": "L1_ffn_h2_s"}


def rotary_tables():
    freqs = np.power(np.float32(10000.0), -np.arange(ROT // 2, dtype=np.float32) / np.float32(ROT // 2))
    angle = (np.arange(T, dtype=np.float32)[None, :] * freqs[:, None]).astype(np.float32)
    cos, sin = np.cos(angle).astype(np.float32), np.sin(angle).astype(np.float32)
    return np.concatenate([cos] * 4), np.concatenate([-sin, sin] * 2)


def kernel(**inputs):
    import concourse.bacc as bacc
    from concourse.bass_utils import run_bass_kernel_spmd

    nc = bacc.Bacc("TRN2", target_bir_lowering=False, num_devices=1)
    given = {n: np.asarray(v) for n, v in inputs.items()}
    arrays = {n: given[n] for n in INPUTS}
    arrays.update({n: given[m].T for n, m in TRANSPOSED.items()})
    arrays.update({n: given[m].reshape(-1, P).T for n, m in BY_PARTITION.items()})
    arrays["b1_by_partition"] = given["L0_ffn_b1"].reshape(-1, 2, P).transpose(0, 2, 1)
    for n, m in (("h1_T", "L1_ffn_h1_w"), ("h2_T", "L1_ffn_h2_w"), ("w3_T", "L1_ffn_w3_w")):
        arrays[n] = given[m].T.reshape(HT4, P, -1).transpose(1, 0, 2)
    dims = np.arange(P)
    for n, cols in (("w_turn", dims[:ROT]), ("w_swap", np.roll(dims[:ROT], ROT // 2)), ("w_skip", dims[ROT:])):
        arrays[n] = np.concatenate([given["L1_attn_wq"][0][:, cols], given["L1_attn_wk"][0][:, cols]], axis=1)
    arrays["wv_T"] = given["L1_attn_wv"][0].T
    arrays["shape_constants"] = shape_constants()
    arrays["cos"], arrays["sin"] = rotary_tables()
    arrays = {n: np.ascontiguousarray(v) for n, v in arrays.items()}
    aps = {n: nc.dram_tensor(n, v.shape, mybir.dt.from_np(v.dtype), kind="ExternalInput").ap() for n, v in arrays.items()}
    out = nc.dram_tensor("out", (1, T, D), F32, kind="ExternalOutput").ap()
    program(nc, aps, out)
    return run_bass_kernel_spmd(nc, [arrays], core_ids=[0]).results[0]["out"]
```

```python
from contextlib import ExitStack

import numpy as np
import concourse.bass as bass
from concourse import mybir

ALU = mybir.AluOpType
ACT = mybir.ActivationFunctionType
AX = mybir.AxisListType
F32 = mybir.dt.float32
I32 = mybir.dt.int32
F16, BF16 = mybir.dt.float16, mybir.dt.bfloat16

P = 128
T, D = 2048, 128
NT = T // P
F = 64
HALF = 16
S = T // HALF
L = 2 * HALF
W = S - 1
SH = S // 2 + 1
N = float(F * D)
BANK = 512
EPS_LN, EPS_RMS, ETA_MIN = 1e-5, 1e-6, 1e-6
EXPERT = 1
EH = 256
HID = 512
TOLERANCE = 2.0 ** -12
HT4 = HID // P
ROT = 64
ZC = 256
LOW = 2.0 ** 11
LIMIT = 2.0 ** 15

C_ID, C_CAUSAL, C_ONES, C_END = 0, 128, 256, 384

RW = L + 2
R_N, R_0, R_CD, R_D, R_G, R_T, R_Q, R_B, R_R, R_E, R_X = range(L, L + 11)
R_Z = R_R + (R_R - R_D)
R_END = R_Z + 1
SCAN = R_X - R_N + 1
EO_STEP = 20
EH_LATE = 3
ACT_HIGH = 12
WT_TILE = 9
POOL_STEP = 8


def shape_constants():
    c = np.zeros((P, C_END), np.float32)
    i = np.arange(P)
    c[:, C_ID:C_ID + P] = np.eye(P)
    c[:, C_CAUSAL:C_CAUSAL + P] = np.where(i[None, :] > i[:, None], -1e30, 0.0)
    c[:, C_ONES:C_ONES + P] = 1.0
    return c


class Order:

    def __init__(self, engine, semaphore):
        self.engine, self.semaphore, self.n, self.offset = engine, semaphore, 0, 0

    def did(self, instruction):
        instruction.then_inc(self.semaphore, 1)
        self.n += 1
        return self.n

    def need(self, n):
        self.engine.wait_ge(self.semaphore, n + self.offset)


def program(nc, a, out):
    with ExitStack() as ctx:
        def sb(name, shape, dt=F32):
            return ctx.enter_context(nc.sbuf_tensor(name, shape, dt))

        def sem(name):
            return ctx.enter_context(nc.semaphore(name))

        x = sb("x", [P, NT, D])
        xn = sb("xn", [P, NT, D])
        xT = sb("xT", [P, T])
        con = sb("con", [P, C_END])
        ident = con[:, C_ID:C_ID + P]
        ones = con[:, C_ONES:C_ONES + P]
        wkT = sb("wkT", [P, F])
        wvT = sb("wvT", [P, D])
        wqT = sb("wqT", [P, F])
        woutT = sb("woutT", [P, D])
        normw = sb("normw", [P, 1])
        etac = sb("etac", [P, 1])
        w1e = sb("w1e", [P, EH])
        w2e = sb("w2e", [P, 2, D])
        b1e = sb("b1e", [P, 2])
        b2e = sb("b2e", [1, D])
        st = sb("st", [P, NT, 6])
        mv = sb("mv", [P, NT, 2])
        lnt = sb("lnt", [P, 7, NT])
        mxb = sb("mxb", [P, 40])
        rsums = sb("rsums", [P, 40])
        small = sb("small", [P, 40])

        arena = sb("arena", [P, 45000])
        at = [0]

        def take(n):
            at[0] += n
            return arena[:, at[0] - n:at[0]]

        wturn, wswap, wskip, wvT2, wo, WVO, s3 = (take(P) for _ in range(7))
        w1T, w2T, w3T = (take(HID) for _ in range(3))
        w3T = w3T.rearrange("p (m e) -> p m e", m=HT4)
        s1, s2, sh1, sh2, s1h, s12 = (take(HT4) for _ in range(6))
        a_tab = at[0]
        HT = take(2 * T).rearrange("p (h t) -> p h t", h=2)
        cosT, sinT = arena[:, a_tab:a_tab + T], arena[:, a_tab + T:a_tab + 2 * T]
        a_blocks = at[0]

        KU = take(SH * 2 * L).rearrange("p (c t i) -> p c t i", c=SH, t=2)
        UXf = take(SH * 2 * (HALF + 1))
        UX = UXf.rearrange("p (c h j) -> p c h j", c=SH, h=2)
        VT = take(T + HALF)
        VXf = take(S * (HALF + 1))
        VX = VXf.rearrange("p (s j) -> p s j", s=S)
        xrT = take(T)
        KE = take(SH * HALF)
        QT, QE = take(T // 2), xT[:, 0:T // 2]
        XR = arena[:, at[0]:at[0] + T].rearrange("p (n d) -> p n d", n=NT)
        Gf = take((HALF + 1) * S)
        G = Gf.rearrange("p (j s) -> p j s", j=HALF + 1)
        CC = take(6 * (L + 1) * L)[0:W].rearrange("p (q j t) -> p q j t", q=6, j=L + 1)
        GG = take(L * L)[0:W].rearrange("p (j t) -> p j t", j=L)
        VC = take(L * L)[0:W].rearrange("p (j l) -> p j l", j=L)
        tmpA, tmpB = (Gf[0:W, L * L * i:L * L * (i + 1)].rearrange("p (j t) -> p j t", j=L) for i in range(2))
        tmpC, tmpD = (xrT[0:W, L * L * i:L * L * (i + 1)].rearrange("p (j t) -> p j t", j=L) for i in range(2))
        tmpE, tmpF = (VXf[0:W, L * L * i:L * L * (i + 1)].rearrange("p (j t) -> p j t", j=L) for i in range(2))
        tmpK, tmpS = (q[0:W, 0:L * L].rearrange("p (j t) -> p j t", j=L) for q in (KE, UXf))
        STf = take(R_END * RW)[0:W]
        ST = STf.rearrange("p (r t) -> p r t", t=RW)
        lane = take(12 * L)[0:W].rearrange("p (r t) -> p r t", t=L)
        VB, MM, KD, FD, M2, MR, MZ, DVS, VJJ, SB, T0, T1 = range(12)
        SG = take(L * SCAN)[0:W].rearrange("p (j k) -> p j k", k=SCAN)
        WS = take(L * SCAN)[0:W].rearrange("p (j k) -> p j k", k=SCAN)
        HG = take((L + 1) * 3)[0:W].rearrange("p (j k) -> p j k", k=3)
        S3 = take(L * 3)[0:W].rearrange("p (j k) -> p j k", k=3)
        SQ = take(L)[0:W]
        U, P2 = take(L)[0:W], take(2 * L)[0:W].rearrange("p (r t) -> p r t", r=2)
        sc = take(6)
        rh, bound, agree = sc[0:W, 0:2], sc[0:W, 2:3], sc[0:W, 3:4]
        wcol, negm = sc[0:L, 4:5], sc[0:L, 5:6]
        wts, c0, c1 = take(L)[0:W], take(HALF)[0:W], take(L)[0:W]
        U_LAST, UW, WM = (take(F)[0:L] for _ in range(3))
        VW, WSUM = (take(D)[0:L] for _ in range(2))
        MW = take(D)
        OJf = take(sum(n * n for n in range(L - 1)))
        OJ, o_ = [], 0
        for j in range(L - 2):
            n_ = L - 2 - j
            OJ.append(OJf[0:W, o_:o_ + n_ * n_].rearrange("p (l t) -> p l t", l=n_))
            o_ += n_ * n_
        KF = OJf[0:F, 0:T]
        MS, MQ, DIAG = OJf[0:F, 2 * T:2 * T + D], OJf[0:F, 2 * T + D:2 * T + 2 * D], OJf[:, 2 * T + 2 * D:2 * T + 3 * D]
        MT = OJf[:, 2 * T + 3 * D:2 * T + 3 * D + F]
        g_ = OJf[:, 2 * T + 4 * D:2 * T + 4 * D + 16]
        vt, dv_, d2, sp_ = (g_[:, i:i + 1] for i in range(4))
        kt, su, rs, r2, mean, var, sd, rinv_ = (g_[0:F, i:i + 1] for i in range(4, 12))

        b_at = [a_blocks]

        def second(n):
            b_at[0] += n
            return arena[:, b_at[0] - n:b_at[0]]

        w1H, w1L, w2H, w2L = (second(HID // 2).bitcast(F16) for _ in range(4))
        w3H, w3L = (second(HID // 2).bitcast(F16).rearrange("p (m e) -> p m e", m=HT4) for _ in range(2))
        h1H, h1L, h2H, h2L = (second(HT4 * HID // 2).bitcast(F16).rearrange("p (k o) -> p k o", k=HT4) for _ in range(4))
        xH, xL = (second(T // 2).bitcast(F16) for _ in range(2))
        ident_b, causal_b = (second(P // 2).bitcast(BF16) for _ in range(2))
        qT1, kT1 = second(T), second(T)
        V1 = second(T).rearrange("p (n e) -> p n e", n=NT)
        hAf, hBf = second(HT4 * T), second(HT4 * T)
        hAH, hAL, hBH, hBL = (h[:, i * HT4 * T // 2:(i + 1) * HT4 * T // 2].bitcast(F16).rearrange("p (m t) -> p m t", m=HT4)
                              for h in (hAf, hBf) for i in range(2))
        Pr = [second(T) for _ in range(2)]
        PT = [second(T), xn[:, :, :].rearrange("p n d -> p (n d)")]
        assert max(b_at[0], at[0]) <= 45000, (b_at, at)
        TURN = [hBf[:, T * c:T * c + 2 * BANK].rearrange("p (k t) -> p k t", k=2) for c in range(2)]
        xd = hBf[:, T + 2 * BANK:T + 3 * BANK]
        h1S, h2S = (hBf[:, c:c + HT4 * HID].rearrange("p (k o) -> p k o", k=HT4) for c in (2 * T, 0))
        WC = [hBf[:, T + HID * i:T + HID * (i + 1)] for i in range(4)] + [second(HID) for _ in range(2)]
        NWC = len(WC)
        gate_ = [hBf[:, 3 * T + ZC * i:3 * T + ZC * (i + 1)] for i in range(8)]
        TH, ZA, ZG, zd = gate_[0:3], gate_[3:6] + [second(ZC) for _ in range(3)], gate_[6], gate_[7]
        NZ = len(ZA)
        FP, RP = ([q[:, BANK * i:BANK * (i + 1)] for i in range(4)] for q in (qT1, kT1))
        fin, ysc = V1, Pr[0]

        def weights_of(i):
            return (w1T, w2T, w3T.rearrange("p m e -> p (m e)"))[i] if i < 3 else (h1S, h2S)[(i - 3) // 4][:, (i - 3) % 4, :]

        NWT = 11

        def weights_with(t):
            return [i for i in range(NWT) if i // 2 + WT_TILE == t]

        h1G, h2G = (q.rearrange("p (k o) -> p k o", k=HT4) for q in (qT1, kT1))
        gA, gB, gC, gz = (hAf[:, T * i:T * (i + 1)].rearrange("p (m t) -> p m t", m=HT4) for i in range(4))
        gT = hBf[:, 0:T].rearrange("p (m t) -> p m t", m=HT4)
        s12a, tern, ends = small[:, 0:HT4], small[:, HT4:HT4 + NWT], small[:, 16:16 + 3 * HT4]
        sums, reach, tmax, top_, ends_ok, fits = small[:, 28:30], small[:, 30:32], small[:, 32:33], small[:, 33:34], small[:, 34:35], small[:, 35:36]
        low_scale = small[:, 36:37]
        mxs, nbs, rsum, rinv = (lnt[:, i, :] for i in range(2, 6))

        PS = ctx.enter_context(nc.psum_tensor("PS", [P, 8, BANK], F32))
        flag = sb("flag", [1, 1], I32)
        fits_flag = sb("fits_flag", [1, 1], I32)

        x_in = [sem(f"x_in{c}") for c in range(4)]
        early_in, eta_in, moe_in, late_in = sem("early_in"), sem("eta_in"), sem("moe_in"), sem("late_in")
        dve_order, act_order, pool_order, loop_order = (
            sem(n) for n in ("dve_order", "act_order", "pool_order", "loop_order"))
        var_ready, sd_ready = sem("var_ready"), sem("sd_ready")
        xr_ready, xn_ready, set_once = sem("xr_ready"), sem("xn_ready"), sem("set_once")
        xrt_done, xrt_act, xrt_dve = sem("xrt_done"), sem("xrt_act"), sem("xrt_dve")
        k_done, v_done, kphi_act, vt_ready, vx_ready = sem("k_done"), sem("v_done"), sem("kphi_act"), sem("vt_ready"), sem("vx_ready")
        eta_set, k_ready, ku_ready, ku_act = sem("eta_set"), sem("k_ready"), sem("ku_ready"), sem("ku_act")
        vgram_done, vgram_act, gram_done, gram_act, gram_dve, lanes_done, lanes_act = (
            sem(n) for n in ("vgram_done", "vgram_act", "gram_done", "gram_act", "gram_dve", "lanes_done", "lanes_act"))
        xnt_done, xnt_act, eh_done, eh_act = (sem(n) for n in ("xnt_done", "xnt_act", "eh_done", "eh_act"))
        q_done, qphi_act, q_ready = sem("q_done"), sem("qphi_act"), sem("q_ready")
        last_done, last_act, mrow_ready, neg_done, neg_act = (sem(n) for n in ("last_done", "last_act", "mrow_ready", "neg_done", "neg_act"))
        vc_ready, oj_ready, b_ready, sb_ready, rows_set, outer_ready = (
            sem(n) for n in ("vc_ready", "oj_ready", "b_ready", "sb_ready", "rows_set", "outer_ready"))
        ssq_ready, sigma_ready, w_ready, h_ready = sem("ssq_ready"), sem("sigma_ready"), sem("w_ready"), sem("h_ready")
        wts_ready, wcol_done, uw_ready, mw_done, mw_act = (sem(n) for n in ("wts_ready", "wcol_done", "uw_ready", "mw_done", "mw_act"))
        c0_ready, shift_done, agree_ready, count_done, flag_set = (sem(n) for n in ("c0_ready", "shift_done", "agree_ready", "count_done", "flag_set"))
        c2_ready, sq_act, step_ready, t_ready = (sem(n) for n in ("c2_ready", "sq_act", "step_ready", "t_ready"))
        ao_done, x1_ready = sem("ao_done"), sem("x1_ready")
        token_ready, state_ready, pred_done, d2_ready, ss_done, s_ready = (
            sem(n) for n in ("token_ready", "state_ready", "pred_done", "d2_ready", "ss_done", "s_ready"))
        rows_ready, sum_done, sq_rows_ready, sq_done, var_s_ready, sd_s_ready = (
            sem(n) for n in ("rows_ready", "sum_done", "sq_rows_ready", "sq_done", "var_s_ready", "sd_s_ready"))
        gmt_done, gmt_act, gmw_done, gmw_act = (sem(n) for n in ("gmt_done", "gmt_act", "gmw_done", "gmw_act"))
        tab_in, small_in, h_in = sem("tab_in"), sem("small_in"), [sem(f"h_in{i}") for i in range(2)]
        var2_ready, sd2_ready, shift_ready, xn2_act, xn2_dve, xt2_done, xt2_act = (
            sem(n) for n in ("var2_ready", "sd2_ready", "shift_ready", "xn2_act", "xn2_dve", "xt2_done", "xt2_act"))
        wvo_done, wvo_act, turn_done, skip_done, skip_act, rope_dve, turned_dve, turned_pool = (
            sem(n) for n in ("wvo_done", "wvo_act", "turn_done", "skip_done", "skip_act", "rope_dve", "turned_dve", "turned_pool"))
        v1_done, v1_act = sem("v1_done"), sem("v1_act")
        s_done, bias_ready, p_ready, pt_done, pt_act, pv_done, pv_read = (
            sem(n) for n in ("s_done", "bias_ready", "p_ready", "pt_done", "pt_act", "pv_done", "pv_read"))
        z_done, tanh_ready, hA_ready = sem("z_done"), sem("tanh_ready"), sem("hA_ready")
        g1_done, g1_act, g2_done, g2_act, y_done, out_ready = (
            sem(n) for n in ("g1_done", "g1_act", "g2_done", "g2_act", "y_done", "out_ready"))
        scales_ready, mask_act = sem("scales_ready"), sem("mask_act")
        w16_ready, xh_act, xl_ready, gate_high, gate_low, wsq_act, wc_ready, tern_ready, rest_ready, low_ready = (
            sem(n) for n in ("w16_ready", "xh_act", "xl_ready", "gate_high", "gate_low", "wsq_act", "wc_ready", "tern_ready", "rest_ready", "low_ready"))
        sums_ready, sums_done, reach_ready, fits_ready, fits_done, fits_set = (sem(n) for n in ("sums_ready", "sums_done", "reach_ready", "fits_ready", "fits_done", "fits_set"))
        gw_in, gz_done, gt_ready, ga_ready, gh_done, gb_ready, gy_done, gy_read, net_order = (
            sem(n) for n in ("gw_in", "gz_done", "gt_ready", "ga_ready", "gh_done", "gb_ready", "gy_done", "gy_read", "net_order"))
        out_sem, out_again = sem("out_sem"), sem("out_again")

        def bank(b, rows=P, cols=BANK):
            return PS[0:rows, b, 0:cols]

        def groups_of(t):
            before = sum((u + 4) // 4 for u in range(t))
            return [(before + k, c, min(4, t + 1 - c)) for k, c in enumerate(range(0, t + 1, 4))]

        FULL = 3 * NT // 4
        SCORE_BANK = [gi % (3 if t < FULL else 4) for t in range(NT) for gi, _, _ in groups_of(t)]
        SCORE_AFTER = [max([w for w in range(gi) if SCORE_BANK[w] == SCORE_BANK[gi]], default=None) for gi in range(len(SCORE_BANK))]
        NU = HT4 * T // ZC
        PER = NU // NT
        assert PER == 2
        GATE_EARLY = [range(PER * t, PER * t + (2 if t < FULL else 1)) if t < NT else () for t in range(NT + 1)]
        GATE_LATE = [range(GATE_EARLY[t].stop, PER * t + PER) if t < NT else () for t in range(NT + 1)]
        GATE_BANK = [3 if u % PER and u // PER < FULL else 6 for u in range(NU)]
        GATE_AFTER = [max([w for w in range(u) if GATE_BANK[w] == GATE_BANK[u]], default=None) for u in range(NU)]

        V_RUNS = [(b, s0, min(26, S - s0)) for b, s0 in zip((7, 2, 3, 5, 6), range(0, S, 26))]
        KU_RUNS = [(b, c0, min(15, SH - c0)) for b, c0 in zip((4, 7, 0, 1, 2), range(0, SH, 15))]
        K2 = BANK // HALF
        BLOCKS = [(slice(0, HALF), slice(0, L)), (slice(HALF, L), slice(HALF, L))]
        LANE_RUNS = [(0, 5, 0), (5, 5, 0), (10, 5, 0), (15, 2, 0), (17, 5, 1), (22, 5, 1), (27, 5, 1), (32, 1, 1)]

        block = ctx.enter_context(nc.Block())

        x_dram = a["L0_attn_x"].rearrange("b (n p) d -> p (b n) d", p=P)
        out_dram = out.rearrange("b (n p) d -> p (b n) d", p=P)

        @block.sync
        def _(sp):
            for c in range(4):
                sp.dma_start(x[:, 4 * c:4 * c + 4, :], x_dram[:, 4 * c:4 * c + 4, :]).then_inc(x_in[c], 16)
            sp.dma_start(normw[:], a["L0_attn_norm_weight"].rearrange("(d o) -> d o", o=1)).then_inc(early_in, 16)
            sp.dma_start(etac[0:F, :], a["L0_attn_eta"].rearrange("(d o) -> d o", o=1)).then_inc(eta_in, 16)
            sp.dma_start(etac[F:P, :], a["L0_attn_eta"].rearrange("(d o) -> d o", o=1)).then_inc(eta_in, 16)
            sp.dma_start(w1e[:], a["L0_ffn_W1"][EXPERT]).then_inc(moe_in, 16)
            sp.dma_start(w2e[:], a["L0_ffn_W2"][EXPERT].rearrange("(k p) o -> p k o", p=P)).then_inc(moe_in, 16)
            sp.dma_start(b1e[:], a["b1_by_partition"][EXPERT]).then_inc(moe_in, 16)
            sp.dma_start(b2e[:], a["L0_ffn_b2"][EXPERT:EXPERT + 1, :]).then_inc(moe_in, 16)
            sp.dma_start(wqT[:], a["WqT"]).then_inc(late_in, 16)
            sp.dma_start(woutT[:], a["WoutT"]).then_inc(late_in, 16)
            for dst, n in ((wturn, "w_turn"), (wswap, "w_swap"), (wskip, "w_skip"), (wvT2, "wv_T"), (wo, "L1_attn_wo"), (w1T, "w1_T"), (w2T, "w2_T"),
                           (w3T, "w3_T"), (s1, "s1"), (s2, "s2"), (sh1, "sh1"), (sh2, "sh2")):
                sp.dma_start(dst, a[n]).then_inc(small_in, 16)
            sp.dma_start(s3, a["L1_ffn_w3_s"].rearrange("(o d) -> o d", o=1).broadcast_to([P, D])).then_inc(small_in, 16)
            sp.wait_ge(x1_ready, 2)
            for i, n in enumerate(("cos", "sin")):
                sp.dma_start((cosT, sinT)[i], a[n]).then_inc(tab_in, 16)
            sp.wait_ge(x1_ready, 4)
            sp.dma_start(h1S, a["h1_T"]).then_inc(h_in[0], 16)
            sp.wait_ge(turned_dve, 4)
            sp.wait_ge(turned_pool, 4)
            sp.dma_start(h2S, a["h2_T"]).then_inc(h_in[1], 16)
            for c in range(4):
                sp.wait_ge(out_ready, c + 1)
                sp.dma_start(out_dram[:, 4 * c:4 * c + 4, :], fin[:, 4 * c:4 * c + 4, :]).then_inc(out_sem, 16)
            sp.wait_ge(out_sem, 64)

        def general_path(engine, run):
            engine.wait_ge(flag_set, 1)
            agreed = engine.value_load(flag[0:1, 0:1], min_val=0, max_val=1)
            with engine.If(agreed == 0):
                run()

        def network_general_path(engine, run):
            engine.wait_ge(fits_set, 1)
            fit = engine.value_load(fits_flag[0:1, 0:1], min_val=0, max_val=1)
            with engine.If(fit == 0):
                run()

        @block.tensor
        def _(pe):
            mm, tr = nc.tensor.matmul, nc.tensor.transpose

            pe.wait_ge(early_in, 16 * 4)
            for n in range(NT):
                pe.wait_ge(xr_ready, n + 1)
                i = tr(PS[:, n // 4, (n % 4) * P:(n % 4 + 1) * P], XR[:, n, :], ident)
                if n % 4 == 3:
                    i.then_inc(xrt_done, 1)
            pe.wait_ge(xrt_act, 2)
            pe.wait_ge(xrt_dve, 1)
            for b, c in enumerate(range(0, SH * HALF, BANK)):
                n = min(BANK, SH * HALF - c)
                for hf in range(2):
                    t0 = hf * (T - SH * HALF)
                    if b == 1 and hf == 1:
                        pe.wait_ge(xrt_dve, 2)
                    i = mm(PS[64 * hf:64 * hf + F, 4 + b, 0:n], wkT[:, :], xrT[:, t0 + c:t0 + c + n], start=True, stop=True)
                if b != 1:
                    i.then_inc(k_done, 1)
            for ch in range(4):
                mm(bank(ch), wvT[:, :], xrT[:, ch * BANK:(ch + 1) * BANK], start=True, stop=True).then_inc(v_done, 1)
            pe.wait_ge(late_in, 32)
            pe.wait_ge(vt_ready, 2)
            for hf in range(2):
                for b in range(2):
                    ch = 2 * hf + b
                    i = mm(PS[64 * hf:64 * hf + F, b, :], wqT[:, :], xrT[:, ch * BANK:(ch + 1) * BANK], start=True, stop=True)
            i.then_inc(q_done, 1)
            pe.wait_ge(set_once, 15)

            def values_gram(r):
                b, s0, cnt = V_RUNS[r]
                pe.wait_ge(vt_ready, min((s0 + cnt) * HALF // BANK, 3) + 1)
                pe.wait_ge(vx_ready, (s0 + cnt - 1) * HALF // BANK + 1)
                if r >= 1:
                    pe.wait_ge(vt_ready, 4)
                if r >= 3:
                    pe.wait_ge(k_ready, 2)
                for s in range(s0, s0 + cnt):
                    i = mm(PS[0:L, b, (s - s0) * (HALF + 1):(s - s0 + 1) * (HALF + 1)], VT[:, HALF * s:HALF * s + L], VX[:, s, :], start=True, stop=True)
                i.then_inc(vgram_done, 1)

            def keys_gram(r):
                b, c0, cnt = KU_RUNS[r]
                pe.wait_ge(ku_ready, 3 if r < 2 else 6)
                pe.wait_ge(ku_act, 2 if r < 2 else 4)
                if r == 1:
                    pe.wait_ge(vgram_act, 1)
                if r in (2, 3):
                    pe.wait_ge(qphi_act, 2)
                if r == 4:
                    pe.wait_ge(vgram_act, 2)
                for c in range(c0, c0 + cnt):
                    i = mm(PS[0:2 * L, b, (c - c0) * 2 * (HALF + 1):(c - c0 + 1) * 2 * (HALF + 1)], KU[:, c, :, :].rearrange("p t i -> p (t i)"),
                           UX[:, c, :, :].rearrange("p h j -> p (h j)"), start=True, stop=True)
                i.then_inc(gram_done, 1)

            values_gram(0)
            values_gram(1)
            values_gram(2)
            keys_gram(0)
            values_gram(3)
            values_gram(4)
            for r in range(1, 5):
                keys_gram(r)
            pe.wait_ge(vgram_act, 5)
            pe.wait_ge(gram_act, 3)
            pe.wait_ge(gram_dve, 2)
            for b, (r0, cnt, behind) in enumerate(LANE_RUNS):
                for r in range(r0, r0 + cnt):
                    j = (HALF if r == 0 else r - 1) if not behind else r - 1 - HALF
                    i = tr(PS[0:W, b, (r - r0) * 3 * L:(r - r0 + 1) * 3 * L], G[0:3 * L, j, behind:behind + W], ident[0:3 * L, 0:3 * L])
                i.then_inc(lanes_done, 1)
            pe.wait_ge(xn_ready, NT)
            for n in range(NT):
                if n % 4 == 0:
                    pe.wait_ge(lanes_act, n // 4 + 1)
                i = tr(PS[:, n // 4, (n % 4) * P:(n % 4 + 1) * P], xn[:, n, :], ident)
                if n % 4 == 3:
                    i.then_inc(xnt_done, 1)
            pe.wait_ge(lanes_act, 8)
            tr(PS[0:L, 7, 0:F], KU[F:P, SH - 2, 1, :], con[F:P, C_ID + F:C_ID + P])
            mm(PS[0:L, 7, F:F + D], VT[:, T - L:T], woutT[:, :], start=True, stop=True)
            mm(PS[0:L, 7, F + D:F + 2 * D], ones[:, 0:L], woutT[:, :], start=True, stop=True).then_inc(last_done, 1)
            pe.wait_ge(mrow_ready, 1)
            mm(PS[0:L, 6, 0:1], lane[:, MM, :], con[0:W, C_ID + W - 1:C_ID + W], start=True, stop=True).then_inc(neg_done, 1)
            pe.wait_ge(moe_in, 64)
            pe.wait_ge(xnt_act, 4)
            pe.wait_ge(last_act, 3)
            pe.wait_ge(neg_act, 1)
            for h in range(2):
                for ch in range(4):
                    mm(bank((4, 0)[h] + ch), w1e[:, h * P:(h + 1) * P], xT[:, ch * BANK:(ch + 1) * BANK], start=True, stop=True).then_inc(eh_done, 1)
            pe.wait_ge(small_in, 16 * 13)
            pe.wait_ge(eh_act, 8)
            mm(PS[:, 7, 0:D], wvT2, wo, start=True, stop=True).then_inc(wvo_done, 1)
            def expert_output(first, end):
                for n in range(first, end):
                    for h in range(2):
                        mm(PS[:, n // 4, (n % 4) * P:(n % 4 + 1) * P], HT[:, h, n * P:(n + 1) * P], w2e[:, h, :], start=(h == 0 and n % 4 == 0), stop=False)
                    mm(PS[:, n // 4, (n % 4) * P:(n % 4 + 1) * P], con[0:1, C_ONES:C_ONES + P], b2e[:, :], start=False, stop=False)
                    mm(PS[:, n // 4, (n % 4) * P:(n % 4 + 1) * P], xT[:, n * P:(n + 1) * P], ident, start=False, stop=False)

            def memory_output(first, end):
                for n in range(first, end):
                    h0 = F * (n // (NT // 2))
                    i = mm(PS[:, n // 4, (n % 4) * P:(n % 4 + 1) * P], QT[h0:h0 + F, n % (NT // 2) * P:(n % (NT // 2) + 1) * P], MW[h0:h0 + F, :], start=False, stop=(n % 4 == 3))
                    if n % 4 == 3:
                        i.then_inc(ao_done, 1)

            pe.wait_ge(w_ready, EO_STEP)
            expert_output(0, NT - 2)
            pe.wait_ge(wts_ready, 1)
            mm(PS[0:L, 5, 0:1], wts, con[0:W, C_ID + W - 1:C_ID + W], start=True, stop=True).then_inc(wcol_done, 1)
            pe.wait_ge(c0_ready, 1)
            mm(PS[0:W - 1, 6, 0:HALF], con[0:W, C_ID + 1:C_ID + W], c0, start=True, stop=True).then_inc(shift_done, 1)
            pe.wait_ge(uw_ready, 2)
            pe.wait_ge(wvo_act, 1)
            mm(PS[0:F, 7, 0:D], UW, VW, start=True, stop=False)
            mm(PS[0:F, 7, 0:D], WM, WSUM, start=False, stop=True).then_inc(mw_done, 1)
            pe.wait_ge(agree_ready, 1)
            mm(PS[0:1, 4, 1:2], agree[0:W - 1, :], con[0:W - 1, C_ONES:C_ONES + 1], start=True, stop=True).then_inc(count_done, 1)
            expert_output(NT - 2, NT - 1)

            def general():
                with pe.Fori(0, T) as t:
                    pe.wait_ge(state_ready, t + 1)
                    pe.wait_ge(token_ready, t + 1)
                    mm(PS[:, 4, 0:1], MS, kt, start=True, stop=True)
                    mm(PS[:, 5, 0:D], ones, DIAG, start=True, stop=True).then_inc(pred_done, 1)
                    pe.wait_ge(d2_ready, t + 1)
                    mm(PS[:, 6, 0:1], ones, d2, start=True, stop=True).then_inc(ss_done, 1)
                    pe.wait_ge(rows_ready, t + 1)
                    mm(PS[:, 7, 0:1], ones[0:F, :], rs, start=True, stop=True).then_inc(sum_done, 1)
                    pe.wait_ge(sq_rows_ready, t + 1)
                    mm(PS[:, 7, 1:2], ones[0:F, :], r2, start=True, stop=True).then_inc(sq_done, 1)
                pe.wait_ge(state_ready, T + 1)
                tr(PS[:, 4, 0:F], MS, con[0:F, C_ID:C_ID + F]).then_inc(gmt_done, 1)
                pe.wait_ge(gmt_act, 1)
                mm(PS[0:F, 7, 0:D], MT, woutT[:, :], start=True, stop=True).then_inc(gmw_done, 1)
                pe.wait_ge(gmw_act, 2)
                expert_output(0, NT)
                memory_output(0, NT)

            pe.wait_ge(mw_act, 2)
            pe.wait_ge(q_ready, 1)
            memory_output(0, 4)
            expert_output(NT - 1, NT)
            memory_output(4, NT)
            general_path(pe, general)

            def normed(c):
                b = 4 * ((c + 1) % 2)
                pe.wait_ge(xn2_act, 2 * c + 2)
                pe.wait_ge(xn2_dve, 2 * c + 2)
                if c >= 2:
                    pe.wait_ge(xt2_act, c - 1)
                for n in range(4 * c, 4 * c + 4):
                    i = tr(PS[:, b, (n % 4) * P:(n % 4 + 1) * P], xn[:, n, :], ident)
                i.then_inc(xt2_done, 1)

            def projected(c):
                b = 4 * ((c + 1) % 2)
                xc = xT[:, c * BANK:(c + 1) * BANK]
                pe.wait_ge(xt2_act, c + 1)
                if c >= 2:
                    pe.wait_ge(rope_dve, 2 * c - 2)
                mm(bank(b + 2), wturn, xc, start=True, stop=True).then_inc(turn_done, 1)
                mm(bank(b + 3), wswap, xc, start=True, stop=True).then_inc(turn_done, 1)
                if c == 0:
                    normed(1)
                if c >= 2:
                    pe.wait_ge(skip_act, 2 * c - 2)
                mm(bank(b + 1), wskip, xc, start=True, stop=True).then_inc(skip_done, 1)

            def values(c):
                b = (4, 0, 5, 1)[c]
                pe.wait_ge(*((xt2_act, c + 3) if c < 2 else (skip_act, 2 * c + 2)))
                for n in range(4 * c, 4 * c + 4):
                    i = mm(PS[:, b, (n % 4) * P:(n % 4 + 1) * P], xT[:, n * P:(n + 1) * P], WVO, start=True, stop=True)
                i.then_inc(v1_done, 1)

            normed(0)
            for c in range(4):
                if c == 1:
                    pe.wait_ge(x1_ready, 4)
                projected(c)
                for n in ((2,), (3,), (), ())[c]:
                    normed(n)
            for c in range(4):
                values(c)

            def gated(u):
                m, c = u % HT4, u // HT4
                if GATE_AFTER[u] is not None:
                    pe.wait_ge(hA_ready, GATE_AFTER[u] + 1)
                if u == 0:
                    pe.wait_ge(w16_ready, 4)
                if u % (2 * HT4) == 0:
                    pe.wait_ge(xl_ready, u // (2 * HT4) + 1)
                for k, (wH, wL) in enumerate(((w1H, w1L), (w2H, w2L))):
                    z = PS[:, GATE_BANK[u], k * ZC:(k + 1) * ZC]
                    mm(z, wH[:, m * P:(m + 1) * P], xH[:, c * ZC:(c + 1) * ZC], start=True, stop=False)
                    i = mm(z, wL[:, m * P:(m + 1) * P], xL[:, c * ZC:(c + 1) * ZC], start=False, stop=True)
                i.then_inc(z_done, 1)

            def scores(t):
                if t % 4 == 0:
                    pe.wait_ge(skip_act, t // 2 + 2)
                    pe.wait_ge(turned_dve, t // 4 + 1)
                    pe.wait_ge(turned_pool, t // 4 + 1)
                    pe.wait_ge(v1_act, max(t // 4 + 1, 2))
                if t == 0:
                    pe.wait_ge(mask_act, 2)
                if t == FULL:
                    pe.wait_ge(hA_ready, PER * FULL)
                for gi, c, cnt in groups_of(t):
                    k = SCORE_BANK[gi]
                    if SCORE_AFTER[gi] is not None:
                        pe.wait_ge(p_ready, SCORE_AFTER[gi] + 1)
                    last = c + 4 > t
                    i = mm(PS[:, k, 0:cnt * P], qT1[:, t * P:(t + 1) * P], kT1[:, c * P:(c + cnt) * P], start=True, stop=not last)
                    if last:
                        i = mm(PS[:, k, (cnt - 1) * P:cnt * P], ident_b, causal_b, start=False, stop=True)
                    i.then_inc(s_done, 1)

            def turn_round(t, gi, c, cnt):
                pe.wait_ge(p_ready, gi + 1)
                if gi >= 2:
                    pe.wait_ge(pt_act, gi - 1)
                for b in range(c, c + cnt):
                    i = tr(PS[:, 4 + gi % 2, (b - c) * P:(b - c + 1) * P], Pr[t % 2][:, b * P:(b + 1) * P], ident)
                i.then_inc(pt_done, 1)

            def weighted(t, gi, c, cnt):
                pe.wait_ge(pt_act, gi + 1)
                if c == 0:
                    (pe.wait_ge(pv_read, t) if t else pe.wait_ge(reach_ready, 2))
                for b in range(c, c + cnt):
                    i = mm(PS[:, 7, (t % 4) * D:(t % 4 + 1) * D], PT[t % 2][:, b * P:(b + 1) * P], V1[:, b, :], start=(b == 0), stop=(b == t))
                if c + cnt > t:
                    i.then_inc(pv_done, 1)

            for t in range(NT + 1):
                if t < NT:
                    scores(t)
                groups = groups_of(t - 1) if t else []
                for g in groups[0:2]:
                    turn_round(t - 1, *g)
                if t < NT:
                    if t == 0:
                        pe.wait_ge(skip_act, 8)
                        pe.wait_ge(rope_dve, 8)
                        pe.wait_ge(v1_act, 4)
                        pe.wait_ge(sums_ready, 2)
                        mm(PS[:, 7, 0:2], ones, sums, start=True, stop=True).then_inc(sums_done, 1)
                for u in GATE_EARLY[t]:
                    gated(u)
                for k, g in enumerate(groups):
                    if k + 1 == len(groups):
                        for u in GATE_LATE[t]:
                            gated(u)
                    weighted(t - 1, *g)
                    if k + 2 < len(groups):
                        turn_round(t - 1, *groups[k + 2])
            pe.wait_ge(w16_ready, 2 * NWT)
            pe.wait_ge(pv_read, NT)
            for layer, (wH, wL, sH, sL, done, read) in enumerate(((h1H, h1L, hAH, hAL, g1_done, g1_act), (h2H, h2L, hBH, hBL, g2_done, g2_act))):
                for ch in range(4):
                    cols = slice(ch * BANK, (ch + 1) * BANK)
                    (pe.wait_ge(low_ready, 4 * ch + 4) if layer else pe.wait_ge(gate_low, NU // 4 * (ch + 1)))
                    for m in range(HT4):
                        u = 4 * ch + m
                        if u >= 8:
                            pe.wait_ge(read, u - 7)
                        elif layer:
                            pe.wait_ge(g1_act, 8 + u + 1)
                        for k in range(HT4):
                            mm(bank(u % 8), wH[:, k, m * P:(m + 1) * P], sH[:, k, cols], start=(k == 0), stop=False)
                            i = mm(bank(u % 8), wL[:, k, m * P:(m + 1) * P], sL[:, k, cols], start=False, stop=(k == HT4 - 1))
                        i.then_inc(done, 1)
            for n in range(NT):
                if n % 4 == 0:
                    pe.wait_ge(low_ready, 16 + n + 4)
                    if n == 0:
                        pe.wait_ge(g2_act, 12)
                if n == 12:
                    pe.wait_ge(fits_ready, 1)
                    mm(PS[0:1, 7, 0:1], fits, con[:, C_ONES:C_ONES + 1], start=True, stop=True).then_inc(fits_done, 1)
                y = PS[:, n // 4, (n % 4) * P:(n % 4 + 1) * P]
                for k in range(HT4):
                    mm(y, hAH[:, k, n * P:(n + 1) * P], w3H[:, k, :], start=(k == 0), stop=False)
                    i = mm(y, hAL[:, k, n * P:(n + 1) * P], w3L[:, k, :], start=False, stop=(k == HT4 - 1))
                if n % 4 == 3:
                    i.then_inc(y_done, 1)

            def network():
                pe.wait_ge(gw_in, 32)
                pe.wait_ge(out_ready, 4)
                with pe.Fori(0, 4) as c:
                    xc = xT[:, bass.ds(c * BANK, BANK)]
                    for m in range(HT4):
                        mm(bank(m), w1T[:, m * P:(m + 1) * P], xc, start=True, stop=True)
                        mm(bank(4 + m), w2T[:, m * P:(m + 1) * P], xc, start=True, stop=True).then_inc(gz_done, 1)
                    for b0, w, src in ((0, h1G, gA), (4, h2G, gB)):
                        (pe.wait_ge(ga_ready, c * HT4 + HT4) if b0 == 0 else pe.wait_ge(gb_ready, c * 2 * HT4 + HT4))
                        for m in range(HT4):
                            for k in range(HT4):
                                i = mm(bank(b0 + m), w[:, k, m * P:(m + 1) * P], src[:, k, :], start=(k == 0), stop=(k == HT4 - 1))
                            i.then_inc(gh_done, 1)
                    pe.wait_ge(gb_ready, c * 2 * HT4 + 2 * HT4)
                    for n in range(4):
                        for k in range(HT4):
                            i = mm(PS[:, 0, n * P:(n + 1) * P], gC[:, k, n * P:(n + 1) * P], w3T[:, k, :], start=(k == 0), stop=(k == HT4 - 1))
                    i.then_inc(gy_done, 1)
                    pe.wait_ge(gy_read, c + 1)

            network_general_path(pe, network)

        @block.scalar
        def _(act):
            f = nc.scalar.activation
            o = Order(act, act_order)
            act.dma_start(con[:], a["shape_constants"]).then_inc(early_in, 16)
            act.dma_start(wkT[:], a["WkT"]).then_inc(early_in, 16)
            act.dma_start(wvT[:], a["WvT"]).then_inc(early_in, 16)
            for h in range(2):
                act.wait_ge(var_ready, h + 1)
                f(lnt[:, 0:2, 8 * h:8 * h + 8], lnt[:, 0:2, 8 * h:8 * h + 8], ACT.Sqrt).then_inc(sd_ready, 1)
            act.wait_ge(early_in, 16 * 4)
            for b in range(2):
                act.wait_ge(xrt_done, b + 1)
                f(xrT[:, b * BANK:(b + 1) * BANK], bank(b), ACT.Copy, scale=normw[:, 0:1]).then_inc(xrt_act, 1)

            for h, (c0, c1) in enumerate(((0, BANK), (BANK, SH * HALF))):
                act.wait_ge(k_done, h + 1)
                n = o.did(f(KE[:, c0:c1], PS[:, 4:7, :].rearrange("p b c -> p (b c)")[:, c0:c1], ACT.Relu, scale=-1.0))
                o.need(n)
                f(KE[:, c0:c1], KE[:, c0:c1], ACT.Exp, scale=-1.0).then_inc(kphi_act, 1)
            zq = PS[:, 0:2, :].rearrange("p b c -> p (b c)")
            act.wait_ge(q_done, 1)
            f(QT, zq, ACT.Relu).then_inc(qphi_act, 1)
            n = o.did(f(QE, zq, ACT.Relu, scale=-1.0))
            o.need(n)
            for h, (c0, c1, d0) in enumerate(((0, K2, 0), (K2, SH, K2 - 1))):
                act.wait_ge(k_ready, h + 1)
                if h == 0:
                    act.wait_ge(eta_set, 1)
                f(KU[:, c0:c1, 1, 0:HALF], KU[:, c0:c1, 0, 0:HALF], ACT.Copy, scale=etac[:, 0:1]).then_inc(ku_act, 1)
                f(KU[:, d0:c1 - 1, 1, HALF:L], KU[:, d0 + 1:c1, 0, 0:HALF], ACT.Copy, scale=etac[:, 0:1]).then_inc(ku_act, 1)
            f(QE, QE, ACT.Exp, scale=-1.0).then_inc(qphi_act, 1)

            def values_gram(r):
                b, s0, cnt = V_RUNS[r]
                act.wait_ge(vgram_done, r + 1)
                f(G[2 * L:3 * L, :, s0:s0 + cnt].rearrange("p j s -> p s j"), PS[0:L, b, 0:cnt * (HALF + 1)].rearrange("p (s j) -> p s j", s=cnt),
                  ACT.Copy).then_inc(vgram_act, 1)

            def keys_gram(r):
                b, c0, cnt = KU_RUNS[r]
                act.wait_ge(gram_done, r + 1)
                for h in range(2):
                    first, end = max(c0, h), min(c0 + cnt, SH - 1 + h)
                    i = f(G[0:2 * L, :, first + h * (S - SH):end + h * (S - SH)].rearrange("p j s -> p s j"),
                          PS[0:2 * L, b, 0:cnt * 2 * (HALF + 1)].rearrange("p (c h j) -> p c h j", c=cnt, h=2)[:, first - c0:end - c0, h, :], ACT.Copy)
                i.then_inc(gram_act, 1)

            act.wait_ge(xrt_done, 4)
            values_gram(0)
            values_gram(1)
            values_gram(2)
            keys_gram(0)
            values_gram(3)
            values_gram(4)
            keys_gram(2)
            keys_gram(4)
            for b, (r0, cnt, behind) in enumerate(LANE_RUNS):
                act.wait_ge(lanes_done, b + 1)
                src = PS[0:W, b, 0:cnt * 3 * L].rearrange("p (j q t) -> p q j t", q=3, t=L)
                if behind:
                    i = f(CC[:, 0:3, r0:r0 + cnt, HALF:L], src[:, :, :, 0:HALF], ACT.Copy)
                else:
                    i = f(CC[:, 0:3, r0:r0 + cnt, :], src, ACT.Copy)
                i.then_inc(lanes_act, 1)
            act.wait_ge(q_ready, 1)
            act.wait_ge(lanes_act, 8)
            for ch in range(4):
                act.wait_ge(xnt_done, ch + 1)
                f(xT[:, ch * BANK:(ch + 1) * BANK], bank(ch), ACT.Copy).then_inc(xnt_act, 1)
            act.wait_ge(last_done, 1)
            f(U_LAST, PS[0:L, 7, 0:F], ACT.Copy).then_inc(last_act, 1)
            f(VW, PS[0:L, 7, F:F + D], ACT.Copy).then_inc(last_act, 1)
            f(WSUM, PS[0:L, 7, F + D:F + 2 * D], ACT.Copy).then_inc(last_act, 1)
            act.wait_ge(neg_done, 1)
            f(negm, PS[0:L, 6, 0:1], ACT.Copy, scale=-1.0).then_inc(neg_act, 1)
            for js, ts in BLOCKS:
                f(tmpS[:, js, ts], CC[:, 0, 1:L + 1, :][:, js, ts], ACT.Square).then_inc(sq_act, 1)
            act.wait_ge(b_ready, 1)
            f(lane[:, SB, :], lane[:, T0, :], ACT.Sqrt).then_inc(sb_ready, 1)
            def hidden(h, ch):
                act.wait_ge(eh_done, 4 * h + ch + 1)
                f(HT[:, h, ch * BANK:(ch + 1) * BANK], bank((4, 0)[h] + ch), ACT.Relu, bias=b1e[:, h:h + 1]).then_inc(eh_act, 1)

            act.wait_ge(moe_in, 64)
            for h in range(2):
                for ch in range(4):
                    if (h, ch) == (0, 0):
                        act.wait_ge(c2_ready, 2)
                        for js, ts in BLOCKS:
                            f(tmpB[:, js, ts], CC[:, 5, 1:L + 1, :][:, js, ts], ACT.Square).then_inc(sq_act, 1)
                    if 4 * h + ch < 8 - EH_LATE:
                        hidden(h, ch)
            act.wait_ge(set_once, 15)
            for j in range(L):
                act.wait_ge(ssq_ready, j + 1)
                f(SG[:, j, 2:11].rearrange("p (g k) -> p g k", k=3)[:, :, 0:2], SQ[:, j:j + 1].unsqueeze(2).broadcast_to([W, 3, 2]),
                  ACT.Sqrt).then_inc(sigma_ready, 1)
                act.wait_ge(w_ready, j + 1)
                f(HG[:, j + 1, 1:3], WS[:, j, SCAN - 1:SCAN].broadcast_to([W, 2]), ACT.Sqrt).then_inc(h_ready, 1)
                if j < L - 1:
                    w = WS[:, j, SCAN - 1:SCAN]
                    f(ST[:, R_E, j + 1:j + 2], w, ACT.Copy, scale=1.0 + EPS_LN)
                    f(ST[:, R_X, j + 2:j + 3], w, ACT.Copy, scale=-EPS_LN)
                if j < EH_LATE:
                    hidden(1, 4 - EH_LATE + j)
            act.wait_ge(wvo_done, 1)
            f(WVO, PS[:, 7, 0:D], ACT.Copy).then_inc(wvo_act, 1)
            act.wait_ge(mw_done, 1)
            for h0 in (0, F):
                f(MW[h0:h0 + F, :], PS[0:F, 7, 0:D], ACT.Copy).then_inc(mw_act, 1)

            def general():
                with act.Fori(0, T) as t:
                    act.wait_ge(ss_done, t + 1)
                    f(sp_, PS[:, 6, 0:1], ACT.Sqrt).then_inc(s_ready, 1)
                    act.wait_ge(var_s_ready, t + 1)
                    f(sd, var, ACT.Sqrt).then_inc(sd_s_ready, 1)
                act.wait_ge(gmt_done, 1)
                f(MT, PS[:, 4, 0:F], ACT.Copy).then_inc(gmt_act, 1)
                act.wait_ge(gmw_done, 1)
                for h0 in (0, F):
                    f(MW[h0:h0 + F, :], PS[0:F, 7, 0:D], ACT.Copy).then_inc(gmw_act, 1)

            general_path(act, general)

            def deviations(c):
                piece = slice(4 * c, 4 * c + 4)
                act.wait_ge(var2_ready, c + 1)
                f(lnt[:, 1, piece], lnt[:, 0, piece], ACT.Sqrt).then_inc(sd2_ready, 1)

            def normed(c):
                act.wait_ge(shift_ready, c + 1)
                for n in range(4 * c, 4 * c + 2):
                    f(xn[:, n, :], x[:, n, :], ACT.Identity, scale=lnt[:, 1, n:n + 1], bias=lnt[:, 6, n:n + 1]).then_inc(xn2_act, 1)

            def transposed(c):
                act.wait_ge(xt2_done, c + 1)
                f(xT[:, c * BANK:(c + 1) * BANK], bank(4 * ((c + 1) % 2)), ACT.Copy).then_inc(xt2_act, 1)

            def high(c):
                f(xH[:, c * BANK:(c + 1) * BANK], xT[:, c * BANK:(c + 1) * BANK], ACT.Copy).then_inc(xh_act, 1)

            deviations(0)
            normed(0)
            transposed(0)
            deviations(1)
            normed(1)
            deviations(2)
            normed(2)
            transposed(1)
            deviations(3)
            normed(3)
            transposed(2)
            f(small[:, 38:39], lnt[:, 0, 12:13], ACT.Tanh)
            for c in range(4):
                b = 4 * ((c + 1) % 2)
                cols = slice(c * BANK, (c + 1) * BANK)
                act.wait_ge(skip_done, c + 1)
                f(qT1[0:ROT, cols], PS[0:ROT, b + 1, :], ACT.Copy).then_inc(skip_act, 1)
                f(kT1[0:ROT, cols], PS[ROT:P, b + 1, :], ACT.Copy).then_inc(skip_act, 1)
                act.wait_ge(xt2_act, c + 1)
                high(c)
                if c == 0:
                    transposed(3)
            f(ident_b, ident, ACT.Copy).then_inc(mask_act, 1)
            f(causal_b, con[:, C_CAUSAL:C_CAUSAL + P], ACT.Copy).then_inc(mask_act, 1)
            for c in range(4):
                act.wait_ge(v1_done, c + 1)
                f(V1[:, 4 * c:4 * c + 4, :].rearrange("p n d -> p (n d)"), bank((4, 0, 5, 1)[c]), ACT.Copy).then_inc(v1_act, 1)

            def tanh(u):
                act.wait_ge(z_done, u + 1)
                if u == 0:
                    act.wait_ge(scales_ready, 2)
                if u >= 3:
                    act.wait_ge(hA_ready, u - 2)
                f(TH[u % 3], PS[:, GATE_BANK[u], 0:ZC], ACT.Tanh, scale=s1h[:, u % HT4:u % HT4 + 1]).then_inc(tanh_ready, 1)

            def weights(i):
                if i in (3, 7):
                    act.wait_ge(h_in[(i - 3) // 4], 16)
                if i == 0:
                    act.wait_ge(turned_dve, 4)
                    act.wait_ge(turned_pool, 4)
                    act.wait_ge(xl_ready, 4)
                if i >= NWC:
                    act.wait_ge(tern_ready, i - NWC + 1)
                w = weights_of(i)
                f(WC[i % NWC], w, ACT.Square).then_inc(wsq_act, 1)
                if i >= 2:
                    k = (i - 3) % 4
                    wH, wL = (q.rearrange("p m e -> p (m e)") for q in (w3H, w3L)) if i == 2 else (
                        q[:, k, :] for q in ((h1H, h1L), (h2H, h2L))[(i - 3) // 4])
                    f(wH, w, ACT.Copy).then_inc(w16_ready, 1)
                    f(wL, w, ACT.Copy, scale=1.0 / LOW).then_inc(w16_ready, 1)

            def turned_back(t):
                for gi, c, cnt in groups_of(t):
                    act.wait_ge(pt_done, gi + 1)
                    f(PT[t % 2][:, c * P:(c + cnt) * P], PS[:, 4 + gi % 2, 0:cnt * P], ACT.Copy).then_inc(pt_act, 1)
                    yield

            for t in range(NT + 1):
                copies = turned_back(t - 1) if t else iter(())
                next(copies, None)
                next(copies, None)
                for u in GATE_EARLY[t]:
                    tanh(u)
                if t < NT:
                    if t >= 2:
                        act.wait_ge(pv_done, t - 1)
                    act.wait_ge(bias_ready, t + 1)
                    for k, (gi, c, cnt) in enumerate(groups_of(t)):
                        if k >= 1:
                            next(copies, None)
                        f(Pr[t % 2][:, c * P:(c + cnt) * P], PS[:, SCORE_BANK[gi], 0:cnt * P], ACT.Exp,
                          scale=1.0 / D, bias=nbs[:, t:t + 1], accum_out=rsums[:, gi:gi + 1]).then_inc(p_ready, 1)
                for _ in copies:
                    pass
                for u in GATE_EARLY[t]:
                    if u < ACT_HIGH:
                        act.wait_ge(hA_ready, u + 1)
                        f(hAH[:, u % HT4, u // HT4 * ZC:(u // HT4 + 1) * ZC], ZA[u % NZ], ACT.Copy).then_inc(gate_high, 1)
                for u in GATE_LATE[t]:
                    tanh(u)
                for i in weights_with(t):
                    weights(i)
            for layer, (s_, done, read) in enumerate(((sh1, g1_done, g1_act), (sh2, g2_done, g2_act))):
                if layer == 0:
                    act.wait_ge(gate_low, NU)
                    act.wait_ge(tern_ready, NWT)
                for u in range(4 * HT4):
                    piece = 4 * HT4 * layer + u
                    act.wait_ge(done, u + 1)
                    high = (hBH, hAH)[layer][:, u % HT4, u // HT4 * BANK:(u // HT4 + 1) * BANK]
                    if piece >= 4:
                        act.wait_ge(rest_ready, piece - 3)
                    f(FP[u % 4], bank(u % 8), ACT.Gelu, scale=s_[:, u % HT4:u % HT4 + 1])
                    f(high, bank(u % 8), ACT.Gelu, scale=s_[:, u % HT4:u % HT4 + 1]).then_inc(read, 1)

            def network():
                with act.Fori(0, 4) as c:
                    for m in range(HT4):
                        act.wait_ge(gz_done, c * HT4 + m + 1)
                        f(gT[:, m, :], bank(m), ACT.Tanh, scale=s1h[:, m:m + 1]).then_inc(gt_ready, 1)
                    for i, (b0, dst, s_) in enumerate(((0, gB, sh1), (4, gC, sh2))):
                        for m in range(HT4):
                            act.wait_ge(gh_done, c * 2 * HT4 + i * HT4 + m + 1)
                            f(dst[:, m, :], bank(b0 + m), ACT.Gelu, scale=s_[:, m:m + 1]).then_inc(gb_ready, 1)

            network_general_path(act, network)

        @block.gpsimd
        def _(pool):
            tt = nc.gpsimd.tensor_tensor
            o = Order(pool, pool_order)
            nc.gpsimd.memset(VX[:, :, HALF:HALF + 1], 1.0).then_inc(set_once, 1)
            nc.gpsimd.memset(VT[:, T:T + HALF], 0.0).then_inc(set_once, 1)
            nc.gpsimd.memset(KU[:, SH - 1, :, HALF:L], 0.0).then_inc(set_once, 1)
            nc.gpsimd.memset(SG, 0.0).then_inc(set_once, 1)
            nc.gpsimd.memset(HG, 0.0).then_inc(set_once, 1)
            nc.gpsimd.memset(CC[:, 3, :, L - 1:L], 0.0).then_inc(set_once, 1)
            nc.gpsimd.memset(GG[:, HALF - 1:L, 0:HALF], 0.0).then_inc(set_once, 1)
            nc.gpsimd.memset(STf, 0.0).then_inc(set_once, 1)
            pool.wait_ge(set_once, 12)
            nc.gpsimd.memset(SG[:, :, SCAN - 1:SCAN], 1.0).then_inc(set_once, 1)
            nc.gpsimd.memset(ST[:, R_E, 0:1], EPS_LN).then_inc(set_once, 1)
            nc.gpsimd.memset(ST[:, R_X, 1:2], -EPS_LN).then_inc(set_once, 1)
            for ch in range(4):
                pool.wait_ge(vt_ready, ch + 1)
                nc.gpsimd.tensor_copy(VX[:, 32 * ch:32 * ch + 32, 0:HALF], VT[:, ch * BANK:(ch + 1) * BANK].rearrange("p (s i) -> p s i", i=HALF)).then_inc(vx_ready, 1)
            pool.wait_ge(qphi_act, 2)
            tt(QT, QT, QE, ALU.add).then_inc(q_ready, 1)
            aT, bT, V = (CC[:, q, 1:L + 1, :] for q in range(3))

            def outer(dst, a_, b_):
                for js, ts in BLOCKS:
                    sh = [W, js.stop - js.start, ts.stop - ts.start]
                    tt(dst[:, js, ts], a_[:, js].unsqueeze(2).broadcast_to(sh), b_[:, ts].unsqueeze(1).broadcast_to(sh), ALU.mult).then_inc(outer_ready, 1)

            def product(dst, a_, b_):
                for js, ts in BLOCKS:
                    tt(dst[:, js, ts], a_[:, js, ts], b_[:, js, ts], ALU.mult).then_inc(outer_ready, 1)

            pool.wait_ge(rows_set, 1)
            outer(tmpK, lane[:, MZ, :], CC[:, 0, 0, :])
            pool.wait_ge(rows_set, 3)
            outer(tmpC, lane[:, M2, :], lane[:, KD, :])
            pool.wait_ge(lanes_act, 8)
            product(tmpE, aT, V)
            product(tmpF, bT, V)
            outer(tmpD, lane[:, MR, :], lane[:, FD, :])
            pool.wait_ge(vc_ready, 2)
            for j in range(L - 2):
                n = L - 2 - j
                tt(OJ[j], CC[:, 0, j + 1, j + 2:L].unsqueeze(1).broadcast_to([W, n, n]), VC[:, j, j + 1:L - 1].unsqueeze(2).broadcast_to([W, n, n]),
                   ALU.mult).then_inc(oj_ready, 1)
            for j in range(POOL_STEP, L - 2):
                n = L - 2 - j
                k = j - POOL_STEP
                pool.wait_ge(step_ready, 2 * k + 1)
                p2 = o.did(tt(P2[:, :, 0:n], ST[:, j + 1:R_Z + 1:R_Z - j - 1, j + 2:L], CC[:, 0:6:5, j + 2, j + 2:L], ALU.mult))
                pool.wait_ge(step_ready, 2 * k + 2)
                o.need(p2)
                tt(ST[:, R_T, j + 1:L - 1], P2[:, 0, 0:n], P2[:, 1, 0:n], ALU.add).then_inc(t_ready, 1)


            def low_part(low, value, high, rest, cols):
                o.need(o.did(tt(rest, value, high, ALU.subtract)))
                return tt(low, rest, low_scale.broadcast_to([P, cols]), ALU.mult)

            o.need(o.did(nc.gpsimd.memset(low_scale, LOW)))
            pool.wait_ge(small_in, 16 * 13)
            pool.wait_ge(x1_ready, 4)
            for wH, wL, w in ((w1H, w1L, w1T), (w2H, w2L, w2T)):
                nc.gpsimd.tensor_copy(wH, w).then_inc(w16_ready, 1)
                nc.gpsimd.tensor_scalar(wL, w, 1.0 / LOW, None, ALU.mult).then_inc(w16_ready, 1)
            for c in range(4):
                cols = slice(c * BANK, (c + 1) * BANK)
                pool.wait_ge(rope_dve, 2 * c + 2)
                (pool.wait_ge(xl_ready, c) if c else pool.wait_ge(w16_ready, 4))
                tt(kT1[ROT:P, cols], TURN[c % 2][ROT:P, 0, :], TURN[c % 2][ROT:P, 1, :], ALU.add).then_inc(turned_pool, 1)
                pool.wait_ge(xh_act, c + 1)
                pool.wait_ge(turned_pool, c + 1)
                low_part(xL[:, cols], xT[:, cols], xH[:, cols], xd, BANK).then_inc(xl_ready, 1)

            def gate_parts(u):
                m, c = u % HT4, u // HT4
                cols = slice(c * ZC, (c + 1) * ZC)
                pool.wait_ge(gate_high, u + 1)
                if u:
                    pool.wait_ge(gate_low, u)
                low_part(hAL[:, m, cols], ZA[u % NZ], hAH[:, m, cols], zd, ZC).then_inc(gate_low, 1)

            def weights(i):
                pool.wait_ge(wsq_act, i + 1)
                o.need(o.did(tt(WC[i % NWC], WC[i % NWC], weights_of(i), ALU.mult)))
                tt(WC[i % NWC], WC[i % NWC], weights_of(i), ALU.subtract).then_inc(wc_ready, 1)

            for t in range(NT):
                for u in (*GATE_EARLY[t], *GATE_LATE[t]):
                    gate_parts(u)
                for i in weights_with(t - 1):
                    weights(i)

            def network():
                pool.wait_ge(y_done, 4)
                pool.dma_start(h1G, a["h1_T"]).then_inc(gw_in, 16)
                pool.dma_start(h2G, a["h2_T"]).then_inc(gw_in, 16)
                pool.wait_ge(gy_read, 4)
                pool.wait_ge(out_sem, 64)
                pool.dma_start(out_dram, fin).then_inc(out_again, 16)
                pool.wait_ge(out_again, 16)

            network_general_path(pool, network)

        @block.vector
        def _(dve):
            v = nc.vector
            o = Order(dve, dve_order)
            did, need = o.did, o.need
            R = [lane[:, i, :] for i in range(12)]

            def last():
                need(o.n)

            def statistics(h):
                for n in range(8 * h, 8 * h + 8):
                    if n % 4 == 0:
                        dve.wait_ge(x_in[n // 4], 16)
                    did(v.bn_stats(st[:, n, :], x[:, n, :]))
                last()
                for n in range(8 * h, 8 * h + 8):
                    did(v.bn_aggr(mv[:, n, :], st[:, n, :]))
                last()
                did(v.tensor_scalar(lnt[:, 0, 8 * h:8 * h + 8], mv[:, 8 * h:8 * h + 8, 1], EPS_LN, None, ALU.add))
                v.tensor_scalar(lnt[:, 1, 8 * h:8 * h + 8], mv[:, 8 * h:8 * h + 8, 1], 1.0 + EPS_RMS, EPS_RMS * EPS_LN, ALU.mult, ALU.add).then_inc(var_ready, 1)

            def rms_normed(h):
                dve.wait_ge(sd_ready, h + 1)
                did(v.reciprocal(lnt[:, 0:2, 8 * h:8 * h + 8], lnt[:, 0:2, 8 * h:8 * h + 8]))
                last()
                for n in range(8 * h, 8 * h + 8):
                    v.tensor_scalar(XR[:, n, :], x[:, n, :], mv[:, n, 0:1], lnt[:, 1, n:n + 1], ALU.subtract, ALU.mult).then_inc(xr_ready, 1)

            v.memset(UX[0:F, :, 1, :], 0.0).then_inc(set_once, 1)
            v.memset(UX[F:P, :, 0, :], 0.0).then_inc(set_once, 1)
            v.memset(UX[0:F, :, 0, HALF:HALF + 1], 1.0).then_inc(set_once, 1)
            v.memset(UX[F:P, :, 1, HALF:HALF + 1], 1.0).then_inc(set_once, 1)
            statistics(0)
            statistics(1)
            rms_normed(0)
            rms_normed(1)
            dve.wait_ge(early_in, 16 * 4)
            for b in range(2, 4):
                dve.wait_ge(xrt_done, b + 1)
                v.tensor_scalar(xrT[:, b * BANK:(b + 1) * BANK], bank(b), normw[:, 0:1], None, ALU.mult).then_inc(xrt_dve, 1)
            dve.wait_ge(eta_in, 32)
            did(v.scalar_tensor_tensor(out=etac[:, :], in0=etac[:, :], scalar=-1.0, in1=etac[:, :], op0=ALU.mult, op1=ALU.max))
            last()
            v.tensor_scalar(etac[:, :], etac[:, :], ETA_MIN, None, ALU.max).then_inc(eta_set, 1)
            dve.wait_ge(eta_set, 1)
            dve.wait_ge(set_once, 15)

            def values(ch):
                dve.wait_ge(v_done, ch + 1)
                v.tensor_copy(VT[:, ch * BANK:(ch + 1) * BANK], bank(ch)).then_inc(vt_ready, 1)

            def keys(h):
                c0, c1, d0 = ((0, K2, 0), (K2, SH, K2 - 1))[h]
                z = PS[:, 4:7, :].rearrange("p b c -> p (b c)")[:, c0 * HALF:c1 * HALF].rearrange("p (c i) -> p c i", i=HALF)
                dve.wait_ge(kphi_act, h + 1)
                v.scalar_tensor_tensor(out=KU[:, c0:c1, 0, 0:HALF], in0=z, scalar=0.0, in1=KE[:, c0 * HALF:c1 * HALF].rearrange("p (c i) -> p c i", i=HALF),
                                       op0=ALU.max, op1=ALU.add).then_inc(k_ready, 1)
                dve.wait_ge(k_ready, h + 1)
                v.tensor_copy(KU[:, d0:c1 - 1, 0, HALF:L], KU[:, d0 + 1:c1, 0, 0:HALF]).then_inc(ku_ready, 1)
                for hf in range(2):
                    h0 = slice(F * hf, F * hf + F)
                    v.tensor_scalar(UX[h0, c0:c1, hf, 0:HALF], KU[h0, c0:c1, 0, 0:HALF], etac[h0, 0:1], None, ALU.mult).then_inc(ku_ready, 1)

            values(0)
            values(1)
            keys(0)
            values(2)
            values(3)
            keys(1)
            for n in range(NT):
                v.tensor_scalar(xn[:, n, :], x[:, n, :], mv[:, n, 0:1], lnt[:, 0, n:n + 1], ALU.subtract, ALU.mult).then_inc(xn_ready, 1)
            dve.wait_ge(xrt_done, 4)
            for r in (1, 3):
                b, c0_, cnt = KU_RUNS[r]
                dve.wait_ge(gram_done, r + 1)
                for h in range(2):
                    s0 = c0_ + h * (S - SH)
                    i = v.tensor_copy(G[0:2 * L, :, s0:s0 + cnt].rearrange("p j s -> p s j"),
                                      PS[0:2 * L, b, 0:cnt * 2 * (HALF + 1)].rearrange("p (c h j) -> p c h j", c=cnt, h=2)[:, :, h, :])
                i.then_inc(gram_dve, 1)

            aT, bT, V = (CC[:, q, 1:L + 1, :] for q in range(3))
            KAP, FUS, Dv = (CC[:, q, 0, :] for q in range(3))

            def diagonal(m, first=0, right=0):
                return m.rearrange("p j t -> p (j t)")[:, first * (L + 1) + right:L * L - right * L:L + 1]

            def rows_of(r, js, ts):
                return R[r][:, js].unsqueeze(2).broadcast_to([W, js.stop - js.start, ts.stop - ts.start])

            def columns_of(r, js, ts):
                return r[:, ts].unsqueeze(1).broadcast_to([W, js.stop - js.start, ts.stop - ts.start])

            dve.wait_ge(set_once, 15)
            dve.wait_ge(lanes_act, 1)
            did(v.tensor_scalar(R[VB], Dv, 2.0 / D, None, ALU.mult))
            did(v.tensor_tensor(R[KD], KAP, Dv, ALU.mult))
            did(v.tensor_tensor(R[FD], FUS, Dv, ALU.mult))
            did(v.tensor_copy(R[DVS], Dv))
            last()
            v.tensor_scalar(R[MZ], R[FD], float(np.sqrt(2.0 * D)) / N, None, ALU.mult).then_inc(rows_set, 1)
            v.tensor_scalar(R[M2], R[FD], 2.0 / N, None, ALU.mult).then_inc(rows_set, 1)
            v.tensor_scalar(R[MR], R[FD], -2.0 / N / N, None, ALU.mult).then_inc(rows_set, 1)
            v.tensor_scalar(R[MM], R[FD], 1.0 / N, None, ALU.mult).then_inc(mrow_ready, 1)
            for js, ts in BLOCKS:
                did(v.tensor_tensor(GG[:, js, ts], rows_of(DVS, js, ts), columns_of(R[VB], js, ts), ALU.mult))
            last()
            dve.wait_ge(lanes_act, 8)
            for js, ts in BLOCKS:
                v.scalar_tensor_tensor(out=VC[:, js, ts], in0=V[:, js, ts], scalar=2.0, in1=GG[:, js, ts], op0=ALU.mult, op1=ALU.subtract).then_inc(vc_ready, 1)
            v.tensor_scalar(R[DVS], R[DVS], float(np.sqrt(2.0 / D)), None, ALU.mult).then_inc(rows_set, 1)
            did(v.tensor_copy(ST[:, R_N, 0:L - 1], diagonal(V, 1)))
            did(v.tensor_tensor(R[T0], diagonal(bT), diagonal(V), ALU.mult))
            did(v.tensor_tensor(R[T1], R[FD], R[FD], ALU.mult))
            last()
            did(v.scalar_tensor_tensor(out=R[T0], in0=R[T1], scalar=-1.0 / N, in1=R[T0], op0=ALU.mult, op1=ALU.add))
            dve.wait_ge(vc_ready, 2)
            did(v.tensor_scalar(R[VJJ], diagonal(VC), 0.5, None, ALU.mult))
            last()
            did(v.tensor_scalar(ST[:, R_B, 0:L], R[T0], 1.0 / N, None, ALU.mult))
            last()
            v.tensor_scalar(R[T0], R[T0], 1.0 / N, 0.0, ALU.mult, ALU.max).then_inc(b_ready, 1)
            dve.wait_ge(rows_set, 4)
            for js, ts in BLOCKS:
                did(v.tensor_tensor(tmpA[:, js, ts], aT[:, js, ts], rows_of(DVS, js, ts), ALU.mult))
            last()
            C0, C1, C2 = (CC[:, q, 1:L + 1, :] for q in range(3, 6))
            dve.wait_ge(outer_ready, 2)
            for js, ts in BLOCKS:
                v.tensor_tensor(C2[:, js, ts], tmpA[:, js, ts], tmpK[:, js, ts], ALU.subtract).then_inc(c2_ready, 1)
            dve.wait_ge(outer_ready, 6)
            for js, ts in BLOCKS:
                t1 = slice(max(ts.start, 1), L)
                did(v.scalar_tensor_tensor(out=C0[:, js, t1.start - 1:L - 1], in0=tmpE[:, js, t1], scalar=-2.0, in1=tmpC[:, js, t1], op0=ALU.mult, op1=ALU.add))
            dve.wait_ge(sq_act, 2)
            dve.wait_ge(c2_ready, 2)
            for js, ts in BLOCKS:
                did(v.tensor_tensor(tmpA[:, js, ts], tmpS[:, js, ts], rows_of(VJJ, js, ts), ALU.mult))
            dve.wait_ge(sq_act, 4)
            last()
            for js, ts in BLOCKS:
                did(v.scalar_tensor_tensor(out=GG[:, js, ts], in0=tmpB[:, js, ts], scalar=0.5, in1=tmpA[:, js, ts], op0=ALU.mult, op1=ALU.add))
            dve.wait_ge(outer_ready, 10)
            for js, ts in BLOCKS:
                did(v.scalar_tensor_tensor(out=C1[:, js, ts], in0=tmpF[:, js, ts], scalar=2.0 / N, in1=tmpD[:, js, ts], op0=ALU.mult, op1=ALU.add))
            last()
            did(v.tensor_copy(ST[:, R_CD, 0:L - 1], diagonal(C0)[:, 0:L - 1]))
            did(v.tensor_copy(ST[:, R_G, 0:L - 1], diagonal(GG, 0, 1)))
            v.tensor_copy(SQ[:, 0:1], V[:, 0, 0:1]).then_inc(ssq_ready, 1)
            last()

            added = formed = o.n
            for j in range(L):
                sg = SG[:, j, 2:3]
                n = L - 2 - j
                by_pool = POOL_STEP <= j < L - 2
                k = j - POOL_STEP
                need(max(added, formed))
                if k > 0:
                    dve.wait_ge(t_ready, min(k, L - 2 - POOL_STEP))
                dve.wait_ge(sigma_ready, j + 1)
                v.tensor_tensor_scan(WS[:, j, :], SG[:, j, :], ST[:, R_N:R_X + 1, j], 0.0, ALU.mult, ALU.add).then_inc(w_ready, 1)
                if j == L - 1:
                    break
                if n > 0:
                    dve.wait_ge(oj_ready, j + 1)
                    nxt = ST[:, j + 1:j + 2, j + 2:L]
                    did(v.scalar_tensor_tensor(out=nxt, in0=OJ[j][:, 0:1, :], scalar=sg, in1=nxt, op0=ALU.mult, op1=ALU.add))
                rows = ST[:, R_D:R_Z + 1:R_R - R_D, j + 1:L]
                i = v.scalar_tensor_tensor(out=rows, in0=CC[:, 3:6, j + 1, j + 1:L], scalar=sg, in1=rows, op0=ALU.mult, op1=ALU.add)
                if by_pool:
                    i.then_inc(step_ready, 1)
                else:
                    added = did(i)
                if n > 0:
                    i = v.scalar_tensor_tensor(out=U[:, 0:n], in0=GG[:, j, j + 2:L], scalar=sg, in1=ST[:, R_T, j + 1:L - 1], op0=ALU.mult, op1=ALU.add)
                    if by_pool:
                        i.then_inc(step_ready, 1)
                    else:
                        u = did(i)
                if n > 0 and not by_pool:
                    need(added)
                    t1 = did(v.tensor_tensor(P2[:, :, 0:n], ST[:, j + 1:R_Z + 1:R_Z - j - 1, j + 2:L], CC[:, 0:6:5, j + 2, j + 2:L], ALU.mult))
                dve.wait_ge(w_ready, j + 1)
                dve.wait_ge(h_ready, j + 1)
                s3_ = did(v.tensor_tensor_scan(S3[:, j, :], HG[:, j + 1, :], WS[:, j, 0:7:3], 0.0, ALU.mult, ALU.add))
                if n > 0:
                    (dve.wait_ge(step_ready, 2 * k + 2) if by_pool else need(u))
                    formed = did(v.scalar_tensor_tensor(out=ST[:, R_Q, j + 1:L - 1], in0=U[:, 0:n], scalar=sg, in1=ST[:, R_Q, j + 1:L - 1],
                                                        op0=ALU.mult, op1=ALU.add))
                need(s3_)
                v.tensor_scalar(SQ[:, j + 1:j + 2], S3[:, j, 2:3], 0.0, None, ALU.max).then_inc(ssq_ready, 1)
                if n > 0 and not by_pool:
                    need(t1)
                    formed = did(v.tensor_tensor(ST[:, R_T, j + 1:L - 1], P2[:, 0, 0:n], P2[:, 1, 0:n], ALU.add))
                if n > 1:
                    later = ST[:, j + 2:L - 1, j + 2:L]
                    added = did(v.scalar_tensor_tensor(out=later, in0=OJ[j][:, 1:, :], scalar=sg, in1=later, op0=ALU.mult, op1=ALU.add))

            dve.wait_ge(h_ready, L)
            did(v.reciprocal(rh, HG[:, HALF:L + 1:HALF, 1]))
            last()
            v.tensor_scalar(wts, SG[:, :, 2], rh[:, 1:2], None, ALU.mult).then_inc(wts_ready, 1)
            dve.wait_ge(sb_ready, 1)
            v.scalar_tensor_tensor(out=c0, in0=SG[:, 0:HALF, 2], scalar=rh[:, 0:1], in1=R[SB][:, 0:HALF], op0=ALU.mult, op1=ALU.mult).then_inc(c0_ready, 1)
            dve.wait_ge(wts_ready, 1)
            cc = did(v.tensor_tensor(c1, wts, R[SB], ALU.mult))
            dve.wait_ge(wcol_done, 1)
            dve.wait_ge(neg_act, 1)
            dve.wait_ge(last_act, 3)
            did(v.tensor_copy(wcol, PS[0:L, 5, 0:1]))
            last()
            v.tensor_scalar(UW, U_LAST, wcol, None, ALU.mult).then_inc(uw_ready, 1)
            v.tensor_scalar(WM, con[0:L, C_ONES:C_ONES + F], wcol, negm, ALU.mult, ALU.mult).then_inc(uw_ready, 1)
            need(cc)
            dve.wait_ge(shift_done, 1)
            did(v.tensor_tensor(c1[0:W - 1, HALF:L], c1[0:W - 1, HALF:L], PS[0:W - 1, 6, 0:HALF], ALU.subtract))
            last()
            did(v.tensor_reduce(bound, c1, AX.X, ALU.add, apply_absolute_value=True))
            last()
            v.tensor_scalar(agree, bound, TOLERANCE, None, ALU.is_le).then_inc(agree_ready, 1)
            dve.wait_ge(count_done, 1)
            v.tensor_scalar(flag[:, :], PS[0:1, 4, 1:2], W - 1.5, None, ALU.is_ge).then_inc(flag_set, 1)

            def general():
                lo = Order(dve, loop_order)
                lo.did(v.tensor_copy(KF[:, 0:T // 2].rearrange("p (c i) -> p c i", i=HALF), KU[0:F, 0:S // 2, 0, 0:HALF]))
                lo.did(v.tensor_copy(KF[:, T // 2:T].rearrange("p (c i) -> p c i", i=HALF), KU[F:P, 1:SH, 0, 0:HALF]))
                v.memset(MS, 0.0).then_inc(state_ready, 1)
                lo.need(lo.n)
                n0 = lo.n
                per = 8
                with dve.Fori(0, T) as t:
                    lo.offset = t * per
                    dve.wait_ge(state_ready, t + 1)
                    lo.did(v.tensor_copy(vt, VT[:, bass.ds(t, 1)]))
                    n = lo.did(v.tensor_copy(kt, KF[:, bass.ds(t, 1)]))
                    lo.need(n)
                    v.tensor_scalar(DIAG, ident, vt, None, ALU.mult).then_inc(token_ready, 1)
                    dve.wait_ge(pred_done, t + 1)
                    n = lo.did(v.tensor_tensor(dv_, vt, PS[:, 4, 0:1], ALU.subtract))
                    lo.need(n)
                    v.tensor_tensor(d2, dv_, dv_, ALU.mult).then_inc(d2_ready, 1)
                    dve.wait_ge(s_ready, t + 1)
                    n = lo.did(v.scalar_tensor_tensor(out=su, in0=kt, scalar=sp_[0:F, :], in1=etac[0:F, :], op0=ALU.mult, op1=ALU.mult))
                    lo.need(n)
                    n = lo.did(v.scalar_tensor_tensor(out=MS, in0=PS[0:F, 5, 0:D], scalar=su, in1=MS, op0=ALU.mult, op1=ALU.add))
                    lo.need(n)
                    v.tensor_reduce(rs, MS, AX.X, ALU.add).then_inc(rows_ready, 1)
                    dve.wait_ge(sum_done, t + 1)
                    n = lo.did(v.tensor_scalar(mean, PS[0:F, 7, 0:1], 1.0 / N, None, ALU.mult))
                    lo.need(n)
                    n = lo.did(v.tensor_scalar(MS, MS, mean, None, ALU.subtract))
                    lo.need(n)
                    v.tensor_tensor_reduce(out=MQ, in0=MS, in1=MS, scale=1.0, scalar=0.0, op0=ALU.mult, op1=ALU.add, accum_out=r2).then_inc(sq_rows_ready, 1)
                    dve.wait_ge(sq_done, t + 1)
                    v.tensor_scalar(var, PS[0:F, 7, 1:2], 1.0 / N, EPS_LN, ALU.mult, ALU.add).then_inc(var_s_ready, 1)
                    dve.wait_ge(sd_s_ready, t + 1)
                    n = lo.did(v.reciprocal(rinv_, sd))
                    lo.need(n)
                    v.tensor_scalar(MS, MS, rinv_, None, ALU.mult).then_inc(state_ready, 1)
                    assert lo.n == n0 + per
                dve.wait_ge(state_ready, T + 1)
                dve.wait_ge(ao_done, 8)

            general_path(dve, general)

            def first_block(b):
                xb = x[:, 4 * b:4 * b + 4, :].rearrange("p n d -> p (n d)")
                dve.wait_ge(ao_done, b + 1)
                v.tensor_tensor(xb, xb, bank(b), ALU.add).then_inc(x1_ready, 1)

            def statistics(b):
                dve.wait_ge(x1_ready, b + 1)
                for n in range(4 * b, 4 * b + 4):
                    did(v.bn_stats(st[:, n, :], x[:, n, :]))

            def variances(c):
                need(o.n)
                for n in range(4 * c, 4 * c + 4):
                    did(v.bn_aggr(mv[:, n, :], st[:, n, :]))
                need(o.n)
                v.tensor_scalar(lnt[:, 0, 4 * c:4 * c + 4], mv[:, 4 * c:4 * c + 4, 1], EPS_LN, None, ALU.add).then_inc(var2_ready, 1)

            def shifts(c):
                piece = slice(4 * c, 4 * c + 4)
                dve.wait_ge(sd2_ready, c + 1)
                need(did(v.reciprocal(lnt[:, 1, piece], lnt[:, 1, piece])))
                v.scalar_tensor_tensor(out=lnt[:, 6, piece], in0=mv[:, piece, 0], scalar=-1.0, in1=lnt[:, 1, piece], op0=ALU.mult, op1=ALU.mult).then_inc(shift_ready, 1)

            def normed(c):
                for n in range(4 * c + 2, 4 * c + 4):
                    v.tensor_scalar(xn[:, n, :], x[:, n, :], mv[:, n, 0:1], lnt[:, 1, n:n + 1], ALU.subtract, ALU.mult).then_inc(xn2_dve, 1)

            first_block(0)
            for c in range(4):
                statistics(c)
                variances(c)
                if c < 3:
                    first_block(c + 1)
                shifts(c)
                normed(c)
            dve.wait_ge(small_in, 16 * 13)
            v.tensor_scalar(s1h, s1, 0.5, None, ALU.mult).then_inc(scales_ready, 1)
            v.scalar_tensor_tensor(out=s12, in0=s1, scalar=0.5, in1=s2, op0=ALU.mult, op1=ALU.mult).then_inc(scales_ready, 1)
            need(did(v.tensor_tensor(s12a, s1, s2, ALU.mult)))
            v.tensor_reduce(sums[:, 0:1], s12a, AX.X, ALU.add, apply_absolute_value=True).then_inc(sums_ready, 1)
            v.tensor_reduce(sums[:, 1:2], sh1, AX.X, ALU.add, apply_absolute_value=True).then_inc(sums_ready, 1)
            dve.wait_ge(tab_in, 32)
            for c in range(4):
                b = 4 * ((c + 1) % 2)
                cols = slice(c * BANK, (c + 1) * BANK)
                if c >= 2:
                    dve.wait_ge(turned_pool, c - 1)
                    dve.wait_ge(turned_dve, c - 1)
                dve.wait_ge(turn_done, 2 * c + 1)
                v.tensor_tensor(TURN[c % 2][:, 0, :], bank(b + 2), cosT[:, cols], ALU.mult).then_inc(rope_dve, 1)
                dve.wait_ge(turn_done, 2 * c + 2)
                v.tensor_tensor(TURN[c % 2][:, 1, :], bank(b + 3), sinT[:, cols], ALU.mult).then_inc(rope_dve, 1)
                dve.wait_ge(rope_dve, 2 * c + 2)
                v.tensor_tensor(qT1[ROT:P, cols], TURN[c % 2][0:ROT, 0, :], TURN[c % 2][0:ROT, 1, :], ALU.add).then_inc(turned_dve, 1)

            def gate(u):
                m, c = u % HT4, u // HT4
                dve.wait_ge(tanh_ready, u + 1)
                if u:
                    dve.wait_ge(hA_ready, u)
                if u >= NZ:
                    dve.wait_ge(gate_low, u - NZ + 1)
                need(did(v.scalar_tensor_tensor(out=ZG, in0=TH[u % 3], scalar=1.0, in1=PS[:, GATE_BANK[u], 0:ZC], op0=ALU.add, op1=ALU.mult)))
                v.scalar_tensor_tensor(out=ZA[u % NZ], in0=PS[:, GATE_BANK[u], ZC:2 * ZC], scalar=s12[:, m:m + 1], in1=ZG,
                                       op0=ALU.mult, op1=ALU.mult).then_inc(hA_ready, 1)
                if u >= ACT_HIGH:
                    if u == ACT_HIGH:
                        dve.wait_ge(gate_high, ACT_HIGH)
                    dve.wait_ge(hA_ready, u + 1)
                    v.tensor_copy(hAH[:, m, c * ZC:(c + 1) * ZC], ZA[u % NZ]).then_inc(gate_high, 1)

            for t in range(NT + 1):
                if t < NT:
                    groups = groups_of(t)
                    for gi, c, cnt in groups:
                        dve.wait_ge(s_done, gi + 1)
                        i = did(v.tensor_reduce(mxb[:, gi:gi + 1], PS[:, SCORE_BANK[gi], 0:cnt * P], AX.X, ALU.max))
                    need(i)
                    g0, g1 = groups[0][0], groups[-1][0]
                    top = mxb[:, g0:g1 + 1]
                    if g1 > g0:
                        need(did(v.tensor_reduce(mxs[:, t:t + 1], top, AX.X, ALU.max)))
                        top = mxs[:, t:t + 1]
                    v.tensor_scalar(nbs[:, t:t + 1], top, -1.0 / D, None, ALU.mult).then_inc(bias_ready, 1)
                if t == 0:
                    dve.wait_ge(sums_done, 1)
                    v.tensor_scalar(reach[:, 0:1], PS[:, 7, 0:1], float(D * D), None, ALU.mult).then_inc(reach_ready, 1)
                    dve.wait_ge(reach_ready, 1)
                    v.tensor_tensor(reach[:, 1:2], reach[:, 0:1], PS[:, 7, 1:2], ALU.mult).then_inc(reach_ready, 1)
                for u in GATE_EARLY[t]:
                    gate(u)
                if t:
                    g0, g1 = groups_of(t - 1)[0][0], groups_of(t - 1)[-1][0]
                    dve.wait_ge(p_ready, g1 + 1)
                    total = rsums[:, g0:g0 + 1]
                    if g1 > g0:
                        total = rsum[:, t - 1:t]
                        need(did(v.tensor_reduce(total, rsums[:, g0:g1 + 1], AX.X, ALU.add)))
                    need(did(v.reciprocal(rinv[:, t - 1:t], total)))
                    dve.wait_ge(pv_done, t)
                    v.scalar_tensor_tensor(out=x[:, t - 1, :], in0=PS[:, 7, ((t - 1) % 4) * D:((t - 1) % 4 + 1) * D], scalar=rinv[:, t - 1:t],
                                           in1=x[:, t - 1, :], op0=ALU.mult, op1=ALU.add).then_inc(pv_read, 1)
                for u in GATE_LATE[t]:
                    gate(u)
                for i in weights_with(t - 2):
                    dve.wait_ge(wc_ready, i + 1)
                    v.tensor_reduce(tern[:, i:i + 1], WC[i % NWC], AX.X, ALU.max, apply_absolute_value=True).then_inc(tern_ready, 1)
            dve.wait_ge(reach_ready, 2)
            did(v.tensor_scalar(ends[:, 0:HT4], s12a, float(D * D), None, ALU.mult))
            did(v.tensor_scalar(ends[:, HT4:2 * HT4], sh1, reach[:, 0:1], None, ALU.mult))
            i = did(v.tensor_scalar(ends[:, 2 * HT4:3 * HT4], sh2, reach[:, 1:2], None, ALU.mult))
            need(i)
            need(did(v.tensor_reduce(top_, ends, AX.X, ALU.max, apply_absolute_value=True)))
            did(v.tensor_scalar(ends_ok, top_, LIMIT, None, ALU.is_le))
            dve.wait_ge(tern_ready, NWT)
            need(did(v.tensor_reduce(tmax, tern, AX.X, ALU.max)))
            v.scalar_tensor_tensor(out=fits, in0=tmax, scalar=0.0, in1=ends_ok, op0=ALU.is_le, op1=ALU.mult).then_inc(fits_ready, 1)
            for piece in range(2 * 4 * HT4):
                ch, m = piece // HT4 % 4, piece % HT4
                high = (hBH, hAH)[piece // (4 * HT4)][:, m, ch * BANK:(ch + 1) * BANK]
                dve.wait_ge((g1_act, g2_act)[piece // (4 * HT4)], piece % (4 * HT4) + 1)
                if piece >= 4:
                    dve.wait_ge(low_ready, piece - 3)
                v.tensor_tensor(RP[m], FP[m], high, ALU.subtract).then_inc(rest_ready, 1)
                dve.wait_ge(rest_ready, piece + 1)
                v.tensor_scalar((hBL, hAL)[piece // (4 * HT4)][:, m, ch * BANK:(ch + 1) * BANK], RP[m], LOW, None, ALU.mult).then_inc(low_ready, 1)
            for b in range(4):
                if b == 3:
                    dve.wait_ge(fits_done, 1)
                    v.tensor_scalar(fits_flag[:, :], PS[0:1, 7, 0:1], P - 0.5, None, ALU.is_ge).then_inc(fits_set, 1)
                dve.wait_ge(y_done, b + 1)
                w = ysc[:, b * BANK:(b + 1) * BANK]
                need(did(v.tensor_tensor(w.rearrange("p (n e) -> p n e", n=4), bank(b).rearrange("p (n e) -> p n e", n=4),
                                         s3.unsqueeze(1).broadcast_to([P, 4, D]), ALU.mult)))
                xb = x[:, 4 * b:4 * b + 4, :].rearrange("p n d -> p (n d)")
                v.tensor_tensor(fin[:, 4 * b:4 * b + 4, :].rearrange("p n d -> p (n d)"), xb, w, ALU.add).then_inc(out_ready, 1)

            def network():
                xf, ff = x[:, :, :].rearrange("p n d -> p (n d)"), fin[:, :, :].rearrange("p n d -> p (n d)")
                dve.wait_ge(out_sem, 64)
                with dve.Fori(0, 4) as c:
                    for m in range(HT4):
                        dve.wait_ge(gt_ready, c * HT4 + m + 1)
                        v.scalar_tensor_tensor(out=gz[:, m, :], in0=gT[:, m, :], scalar=1.0, in1=bank(m), op0=ALU.add, op1=ALU.mult).then_inc(net_order, 1)
                        dve.wait_ge(net_order, c * (HT4 + 1) + m + 1)
                        v.scalar_tensor_tensor(out=gA[:, m, :], in0=bank(4 + m), scalar=s12[:, m:m + 1], in1=gz[:, m, :],
                                               op0=ALU.mult, op1=ALU.mult).then_inc(ga_ready, 1)
                    dve.wait_ge(gy_done, c + 1)
                    v.tensor_tensor(ysc[:, 0:BANK].rearrange("p (n e) -> p n e", n=4), bank(0).rearrange("p (n e) -> p n e", n=4),
                                    s3.unsqueeze(1).broadcast_to([P, 4, D]), ALU.mult).then_inc(net_order, 1)
                    dve.wait_ge(net_order, c * (HT4 + 1) + HT4 + 1)
                    v.tensor_tensor(ff[:, bass.ds(c * BANK, BANK)], xf[:, bass.ds(c * BANK, BANK)], ysc[:, 0:BANK], ALU.add).then_inc(gy_read, 1)

            network_general_path(dve, network)


INPUTS = ["L0_attn_x", "L0_attn_norm_weight", "L0_attn_eta", "L0_ffn_W1", "L0_ffn_W2", "L0_ffn_b2", "L1_attn_wo", "L1_ffn_w3_s"]
TRANSPOSED = {"WkT": "L0_attn_Wk", "WvT": "L0_attn_Wv", "WqT": "L0_attn_Wq", "WoutT": "L0_attn_Wout", "w1_T": "L1_ffn_w1_w", "w2_T": "L1_ffn_w2_w"}
BY_PARTITION = {"s1": "L1_ffn_w1_s", "s2": "L1_ffn_w2_s", "sh1": "L1_ffn_h1_s", "sh2": "L1_ffn_h2_s"}


def rotary_tables():
    freqs = np.power(np.float32(10000.0), -np.arange(ROT // 2, dtype=np.float32) / np.float32(ROT // 2))
    angle = (np.arange(T, dtype=np.float32)[None, :] * freqs[:, None]).astype(np.float32)
    cos, sin = np.cos(angle).astype(np.float32), np.sin(angle).astype(np.float32)
    return np.concatenate([cos] * 4), np.concatenate([-sin, sin] * 2)


def kernel(**inputs):
    import concourse.bacc as bacc
    from concourse.bass_utils import run_bass_kernel_spmd

    nc = bacc.Bacc("TRN2", target_bir_lowering=False, num_devices=1)
    given = {n: np.asarray(v) for n, v in inputs.items()}
    arrays = {n: given[n] for n in INPUTS}
    arrays.update({n: given[m].T for n, m in TRANSPOSED.items()})
    arrays.update({n: given[m].reshape(-1, P).T for n, m in BY_PARTITION.items()})
    arrays["b1_by_partition"] = given["L0_ffn_b1"].reshape(-1, 2, P).transpose(0, 2, 1)
    for n, m in (("h1_T", "L1_ffn_h1_w"), ("h2_T", "L1_ffn_h2_w"), ("w3_T", "L1_ffn_w3_w")):
        arrays[n] = given[m].T.reshape(HT4, P, -1).transpose(1, 0, 2)
    dims = np.arange(P)
    for n, cols in (("w_turn", dims[:ROT]), ("w_swap", np.roll(dims[:ROT], ROT // 2)), ("w_skip", dims[ROT:])):
        arrays[n] = np.concatenate([given["L1_attn_wq"][0][:, cols], given["L1_attn_wk"][0][:, cols]], axis=1)
    arrays["wv_T"] = given["L1_attn_wv"][0].T
    arrays["shape_constants"] = shape_constants()
    arrays["cos"], arrays["sin"] = rotary_tables()
    arrays = {n: np.ascontiguousarray(v) for n, v in arrays.items()}
    aps = {n: nc.dram_tensor(n, v.shape, mybir.dt.from_np(v.dtype), kind="ExternalInput").ap() for n, v in arrays.items()}
    out = nc.dram_tensor("out", (1, T, D), F32, kind="ExternalOutput").ap()
    program(nc, aps, out)
    return run_bass_kernel_spmd(nc, [arrays], core_ids=[0]).results[0]["out"]
```
